# Optimizing a Trainium2 kernel written in Bass

```python
import numpy as np
import jax
import jax.numpy as jnp

def _softmax(x, axis=-1):
    return jax.nn.softmax(x, axis=axis)

def _gelu(x):
    return jax.nn.gelu(x, approximate=True)

def _silu(x):
    return jax.nn.silu(x)

def _sigmoid(x):
    return jax.nn.sigmoid(x)

def _layernorm(x, axis=-1, eps=1e-05):
    m = jnp.mean(x, axis=axis, keepdims=True)
    v = jnp.var(x, axis=axis, keepdims=True)
    return (x - m) / jnp.sqrt(v + eps)

def _scatter_add(tgt, idx, src, axis=0):
    return tgt.at[idx].add(src)

def _segment_sum(src, seg, n):
    return jax.ops.segment_sum(src, seg, n)
kernel_name = 'mk_xattn_ffn_d2_seqx_r4_5bd88a'

def setup_inputs(seed: int=0):
    np.random.seed(seed)
    _w = jnp.asarray

    def _rec_inputs():
        import jax
        import jax.numpy as jnp
        _rk = jax.random.key(seed)
        x = 7.22e-05 + 1 * jax.random.normal(jax.random.fold_in(_rk, 1), (4, 1024, 256), jnp.float32)
        _lenS = 1024 - jax.random.randint(jax.random.fold_in(_rk, 7), (4,), 0, max(1, 1024 // 4) + 1, jnp.int32)
        _lenS2 = 64 - jax.random.randint(jax.random.fold_in(_rk, 8), (4,), 0, max(1, 64 // 4) + 1, jnp.int32)
        _ctx_768P = jax.random.normal(jax.random.fold_in(_rk, 11), (4, 16, 192), jnp.float32)
        _ctx_768c = jax.random.dirichlet(jax.random.fold_in(_rk, 511), 0.3 * jnp.ones((16,), jnp.float32), (4, 64))
        _ctx_768t = jnp.einsum('bsk,bkd->bsd', _ctx_768c, _ctx_768P)
        _ctx_768t = _ctx_768t * jax.lax.rsqrt(jnp.mean(jnp.square(_ctx_768t)) + 1e-12) * 0.953939
        ctx_768 = -7.36909e-05 + 0.999899 * (_ctx_768t + 0.3 * jax.random.normal(jax.random.fold_in(_rk, 611), (4, 64, 192), jnp.float32))
        return (x, ctx_768)
    x, ctx_768 = _rec_inputs()

    def _L0_xattn_setup():
        import jax, jax.numpy as jnp
        import numpy as np
        NUM_HEADS = 16
        HEAD_DIM = 64
        INNER = NUM_HEADS * HEAD_DIM
        QUERY_DIM = 256
        CONTEXT_DIM = 192
        SCALE = HEAD_DIM ** (-0.5)
        key = jax.random.key(seed)
        ks = jax.random.split(key, 6)
        B, NQ, NKV = (8, 256, 512)
        query = jax.random.normal(ks[0], (B, NQ, QUERY_DIM), dtype=jnp.float32)
        context = jax.random.normal(ks[1], (B, NKV, CONTEXT_DIM), dtype=jnp.float32)
        w_q = jax.random.normal(ks[2], (QUERY_DIM, INNER), dtype=jnp.float32) * QUERY_DIM ** (-0.5)
        w_kv = jax.random.normal(ks[3], (CONTEXT_DIM, 2 * INNER), dtype=jnp.float32) * CONTEXT_DIM ** (-0.5)
        w_out = jax.random.normal(ks[4], (INNER, QUERY_DIM), dtype=jnp.float32) * INNER ** (-0.5)
        b_out = jax.random.normal(ks[5], (QUERY_DIM,), dtype=jnp.float32) * 0.01
        return {'query': query, 'context': context, 'w_q': w_q, 'w_kv': w_kv, 'w_out': w_out, 'b_out': b_out}
    _L0_xattn_all = _L0_xattn_setup()
    _L0_xattn_in = {k: v for k, v in _L0_xattn_all.items() if k in ('w_q', 'w_kv', 'w_out', 'b_out')}
    del _L0_xattn_all

    def _L0_ffn_setup():
        import jax, jax.numpy as jnp
        import numpy as np
        BLOCK = 32
        W_BITS = 4
        ACT_BITS = 16

        def act_qdq(x):
            qmax = 2.0 ** (ACT_BITS - 1) - 1.0
            scale = jnp.maximum(jnp.max(jnp.abs(x)) / qmax, 1e-12)
            return jnp.clip(jnp.round(x / scale), -qmax - 1.0, qmax) * scale

        def fixed_qdq_u16(x):
            scale = 1.0 / 65536.0
            return jnp.clip(jnp.round(x / scale), 0.0, 65535.0) * scale

        def lpbq_dequant(w):
            O, I = w.shape
            qmax = 2.0 ** (W_BITS - 1) - 1.0
            wb = w.reshape(O, I // BLOCK, BLOCK)
            s = jnp.maximum(jnp.max(jnp.abs(wb), axis=-1, keepdims=True) / qmax, 1e-12)
            wq = jnp.clip(jnp.round(wb / s), -qmax - 1.0, qmax) * s
            return wq.reshape(O, I)
        key = jax.random.key(seed)
        k1, k2, k3, k4 = jax.random.split(key, 4)
        B, S, H, I = (2, 1024, 256, 768)
        x = jax.random.normal(k1, (B, S, H), jnp.float32)
        w_gate = jax.random.normal(k2, (I, H), jnp.float32) * 0.02
        w_up = jax.random.normal(k3, (I, H), jnp.float32) * 0.02
        w_down = jax.random.normal(k4, (H, I), jnp.float32) * 0.02
        return {'x': x, 'w_gate': w_gate, 'w_up': w_up, 'w_down': w_down}
    _L0_ffn_all = _L0_ffn_setup()
    _L0_ffn_in = {k: v for k, v in _L0_ffn_all.items() if k in ('w_gate', 'w_up', 'w_down')}
    del _L0_ffn_all

    def _L1_xattn_setup():
        import jax, jax.numpy as jnp
        import numpy as np
        HEADS = 16
        DIM_HEAD = 64
        RANK = 32
        LORA_W = 1.0
        IPA_SCALE = 1.0
        IPA_TOKENS = 4
        SCALE = DIM_HEAD ** (-0.5)

        def _split_heads(t):
            b, n, _ = t.shape
            return t.reshape(b, n, HEADS, DIM_HEAD).transpose(0, 2, 1, 3)

        def _merge_heads(t):
            b, h, n, d = t.shape
            return t.transpose(0, 2, 1, 3).reshape(b, n, h * d)

        def _attention(q_in, k_in, v_in):
            q = _split_heads(q_in)
            k = _split_heads(k_in)
            v = _split_heads(v_in)
            s = jnp.einsum('bhid,bhjd->bhij', q, k) * SCALE
            p = jax.nn.softmax(s, axis=-1)
            o = jnp.einsum('bhij,bhjd->bhid', p, v)
            return _merge_heads(o)

        def _lora(t, down, up, alpha):
            return t @ down @ up * (LORA_W * alpha[0] / RANK)
        key = jax.random.key(seed)
        ks = jax.random.split(key, 20)
        B, N, QD, CD, ID = (8, 1024, 256, 192, HEADS * DIM_HEAD)
        CTX = 77 + IPA_TOKENS
        s = 0.02
        return {'x': jax.random.normal(ks[0], (B, N, QD), jnp.float32), 'context': jax.random.normal(ks[1], (B, CTX, CD), jnp.float32), 'Wq': jax.random.normal(ks[2], (QD, ID), jnp.float32) * s, 'Wk': jax.random.normal(ks[3], (CD, ID), jnp.float32) * s, 'Wv': jax.random.normal(ks[4], (CD, ID), jnp.float32) * s, 'Wo': jax.random.normal(ks[5], (ID, QD), jnp.float32) * s, 'bo': jnp.zeros((QD,), jnp.float32), 'q_down': jax.random.normal(ks[6], (QD, RANK), jnp.float32) * s, 'q_up': jax.random.normal(ks[7], (RANK, ID), jnp.float32) * s, 'q_alpha': jnp.ones((1,), jnp.float32) * RANK, 'k_down': jax.random.normal(ks[8], (CD, RANK), jnp.float32) * s, 'k_up': jax.random.normal(ks[9], (RANK, ID), jnp.float32) * s, 'k_alpha': jnp.ones((1,), jnp.float32) * RANK, 'v_down': jax.random.normal(ks[10], (CD, RANK), jnp.float32) * s, 'v_up': jax.random.normal(ks[11], (RANK, ID), jnp.float32) * s, 'v_alpha': jnp.ones((1,), jnp.float32) * RANK, 'o_down': jax.random.normal(ks[12], (ID, RANK), jnp.float32) * s, 'o_up': jax.random.normal(ks[13], (RANK, QD), jnp.float32) * s, 'o_alpha': jnp.ones((1,), jnp.float32) * RANK, 'Wk_ipa': jax.random.normal(ks[14], (CD, ID), jnp.float32) * s, 'Wv_ipa': jax.random.normal(ks[15], (CD, ID), jnp.float32) * s}
    _L1_xattn_all = _L1_xattn_setup()
    _L1_xattn_in = {k: v for k, v in _L1_xattn_all.items() if k in ('Wq', 'Wk', 'Wv', 'Wo', 'bo', 'q_down', 'q_up', 'q_alpha', 'k_down', 'k_up', 'k_alpha', 'v_down', 'v_up', 'v_alpha', 'o_down', 'o_up', 'o_alpha', 'Wk_ipa', 'Wv_ipa')}
    del _L1_xattn_all

    def _L1_ffn_setup():
        import jax, jax.numpy as jnp
        import numpy as np
        K = 2
        key = jax.random.key(seed)
        ks = jax.random.split(key, 7)
        B, S, D, E = (2, 512, 256, 8)
        H = 4 * D
        sd = 1.0 / np.sqrt(D)
        sh = 1.0 / np.sqrt(H)
        return {'x': jax.random.normal(ks[0], (B, S, D), jnp.float32), 'Wr': jax.random.normal(ks[1], (D, E), jnp.float32) * sd, 'br': jax.random.normal(ks[2], (E,), jnp.float32) * sd, 'W1': jax.random.normal(ks[3], (E, D, H), jnp.float32) * sd, 'b1': jax.random.normal(ks[4], (E, H), jnp.float32) * sd, 'W2': jax.random.normal(ks[5], (E, H, D), jnp.float32) * sh, 'b2': jax.random.normal(ks[6], (E, D), jnp.float32) * sh}
    _L1_ffn_all = _L1_ffn_setup()
    _L1_ffn_in = {k: v for k, v in _L1_ffn_all.items() if k in ('Wr', 'br', 'W1', 'b1', 'W2', 'b2')}
    del _L1_ffn_all
    return {'x': x, 'ctx_768': ctx_768, 'L0_xattn_w_q': _L0_xattn_in['w_q'], 'L0_xattn_w_kv': _L0_xattn_in['w_kv'], 'L0_xattn_w_out': _L0_xattn_in['w_out'], 'L0_xattn_b_out': _L0_xattn_in['b_out'], 'L0_ffn_w_gate': _L0_ffn_in['w_gate'], 'L0_ffn_w_up': _L0_ffn_in['w_up'], 'L0_ffn_w_down': _L0_ffn_in['w_down'], 'L1_xattn_Wq': _L1_xattn_in['Wq'], 'L1_xattn_Wk': _L1_xattn_in['Wk'], 'L1_xattn_Wv': _L1_xattn_in['Wv'], 'L1_xattn_Wo': _L1_xattn_in['Wo'], 'L1_xattn_bo': _L1_xattn_in['bo'], 'L1_xattn_q_down': _L1_xattn_in['q_down'], 'L1_xattn_q_up': _L1_xattn_in['q_up'], 'L1_xattn_q_alpha': _L1_xattn_in['q_alpha'], 'L1_xattn_k_down': _L1_xattn_in['k_down'], 'L1_xattn_k_up': _L1_xattn_in['k_up'], 'L1_xattn_k_alpha': _L1_xattn_in['k_alpha'], 'L1_xattn_v_down': _L1_xattn_in['v_down'], 'L1_xattn_v_up': _L1_xattn_in['v_up'], 'L1_xattn_v_alpha': _L1_xattn_in['v_alpha'], 'L1_xattn_o_down': _L1_xattn_in['o_down'], 'L1_xattn_o_up': _L1_xattn_in['o_up'], 'L1_xattn_o_alpha': _L1_xattn_in['o_alpha'], 'L1_xattn_Wk_ipa': _L1_xattn_in['Wk_ipa'], 'L1_xattn_Wv_ipa': _L1_xattn_in['Wv_ipa'], 'L1_ffn_Wr': _L1_ffn_in['Wr'], 'L1_ffn_br': _L1_ffn_in['br'], 'L1_ffn_W1': _L1_ffn_in['W1'], 'L1_ffn_b1': _L1_ffn_in['b1'], 'L1_ffn_W2': _L1_ffn_in['W2'], 'L1_ffn_b2': _L1_ffn_in['b2']}

def reference(x, ctx_768, L0_xattn_w_q, L0_xattn_w_kv, L0_xattn_w_out, L0_xattn_b_out, L0_ffn_w_gate, L0_ffn_w_up, L0_ffn_w_down, L1_xattn_Wq, L1_xattn_Wk, L1_xattn_Wv, L1_xattn_Wo, L1_xattn_bo, L1_xattn_q_down, L1_xattn_q_up, L1_xattn_q_alpha, L1_xattn_k_down, L1_xattn_k_up, L1_xattn_k_alpha, L1_xattn_v_down, L1_xattn_v_up, L1_xattn_v_alpha, L1_xattn_o_down, L1_xattn_o_up, L1_xattn_o_alpha, L1_xattn_Wk_ipa, L1_xattn_Wv_ipa, L1_ffn_Wr, L1_ffn_br, L1_ffn_W1, L1_ffn_b1, L1_ffn_W2, L1_ffn_b2):
    import jax
    import jax.numpy as jnp

    def _L0_xattn_ref(query, context, w_q, w_kv, w_out, b_out):
        import jax, jax.numpy as jnp
        import numpy as np
        NUM_HEADS = 16
        HEAD_DIM = 64
        INNER = NUM_HEADS * HEAD_DIM
        QUERY_DIM = 256
        CONTEXT_DIM = 192
        SCALE = HEAD_DIM ** (-0.5)
        B, NQ, _ = query.shape
        NKV = context.shape[1]
        q = query @ w_q
        kv = context @ w_kv
        k, v = jnp.split(kv, 2, axis=-1)
        q = q.reshape(B, NQ, NUM_HEADS, HEAD_DIM).transpose(0, 2, 1, 3)
        k = k.reshape(B, NKV, NUM_HEADS, HEAD_DIM).transpose(0, 2, 1, 3)
        v = v.reshape(B, NKV, NUM_HEADS, HEAD_DIM).transpose(0, 2, 1, 3)
        scores = jnp.einsum('bhqd,bhkd->bhqk', q, k) * SCALE
        attn = jax.nn.softmax(scores, axis=-1)
        out = jnp.einsum('bhqk,bhkd->bhqd', attn, v)
        out = out.transpose(0, 2, 1, 3).reshape(B, NQ, INNER)
        return out @ w_out + b_out

    def _L0_ffn_ref(x, w_gate, w_up, w_down):
        import jax, jax.numpy as jnp
        import numpy as np
        BLOCK = 32
        W_BITS = 4
        ACT_BITS = 16

        def act_qdq(x):
            qmax = 2.0 ** (ACT_BITS - 1) - 1.0
            scale = jnp.maximum(jnp.max(jnp.abs(x)) / qmax, 1e-12)
            return jnp.clip(jnp.round(x / scale), -qmax - 1.0, qmax) * scale

        def fixed_qdq_u16(x):
            scale = 1.0 / 65536.0
            return jnp.clip(jnp.round(x / scale), 0.0, 65535.0) * scale

        def lpbq_dequant(w):
            O, I = w.shape
            qmax = 2.0 ** (W_BITS - 1) - 1.0
            wb = w.reshape(O, I // BLOCK, BLOCK)
            s = jnp.maximum(jnp.max(jnp.abs(wb), axis=-1, keepdims=True) / qmax, 1e-12)
            wq = jnp.clip(jnp.round(wb / s), -qmax - 1.0, qmax) * s
            return wq.reshape(O, I)
        x = act_qdq(x)
        up = act_qdq(x @ lpbq_dequant(w_up).T)
        gate = act_qdq(x @ lpbq_dequant(w_gate).T)
        sig = fixed_qdq_u16(jax.nn.sigmoid(gate))
        gate = act_qdq(gate * sig)
        o = act_qdq(gate * up)
        return o @ lpbq_dequant(w_down).T

    def _L1_xattn_ref(x, context, Wq, Wk, Wv, Wo, bo, q_down, q_up, q_alpha, k_down, k_up, k_alpha, v_down, v_up, v_alpha, o_down, o_up, o_alpha, Wk_ipa, Wv_ipa):
        import jax, jax.numpy as jnp
        import numpy as np
        HEADS = 16
        DIM_HEAD = 64
        RANK = 32
        LORA_W = 1.0
        IPA_SCALE = 1.0
        IPA_TOKENS = 4
        SCALE = DIM_HEAD ** (-0.5)

        def _split_heads(t):
            b, n, _ = t.shape
            return t.reshape(b, n, HEADS, DIM_HEAD).transpose(0, 2, 1, 3)

        def _merge_heads(t):
            b, h, n, d = t.shape
            return t.transpose(0, 2, 1, 3).reshape(b, n, h * d)

        def _attention(q_in, k_in, v_in):
            q = _split_heads(q_in)
            k = _split_heads(k_in)
            v = _split_heads(v_in)
            s = jnp.einsum('bhid,bhjd->bhij', q, k) * SCALE
            p = jax.nn.softmax(s, axis=-1)
            o = jnp.einsum('bhij,bhjd->bhid', p, v)
            return _merge_heads(o)

        def _lora(t, down, up, alpha):
            return t @ down @ up * (LORA_W * alpha[0] / RANK)
        q_in = x @ Wq + _lora(x, q_down, q_up, q_alpha)
        end = context.shape[1] - IPA_TOKENS
        org_ctx = context[:, :end, :]
        ipa_ctx = context[:, end:, :]
        k_in = org_ctx @ Wk + _lora(org_ctx, k_down, k_up, k_alpha)
        v_in = org_ctx @ Wv + _lora(org_ctx, v_down, v_up, v_alpha)
        out = _attention(q_in, k_in, v_in)
        ipa_k = ipa_ctx @ Wk_ipa
        ipa_v = ipa_ctx @ Wv_ipa
        out_ipa = _attention(q_in, ipa_k, ipa_v)
        out = out + IPA_SCALE * out_ipa
        return out @ Wo + bo + _lora(out, o_down, o_up, o_alpha)

    def _L1_ffn_ref(x, Wr, br, W1, b1, W2, b2):
        import jax, jax.numpy as jnp
        import numpy as np
        K = 2
        E = Wr.shape[-1]
        scores = jnp.einsum('bsd,de->bse', x, Wr) + br
        _, topk_idx = jax.lax.top_k(scores, K)
        indicator = jax.nn.one_hot(topk_idx, E, dtype=scores.dtype).sum(-2)
        neg_inf = jnp.asarray(-jnp.inf, scores.dtype)
        weights = jax.nn.softmax(jnp.where(indicator > 0, scores, neg_inf), axis=-1)
        out = jnp.zeros_like(x)
        for i in range(E):
            xi = x * indicator[..., i:i + 1]
            h = jax.nn.relu(jnp.einsum('bsd,dh->bsh', xi, W1[i]) + b1[i])
            yi = jnp.einsum('bsh,hd->bsd', h, W2[i]) + b2[i]
            out = out + yi * weights[..., i:i + 1]
        return out
    x = x + _L0_xattn_ref(_layernorm(x, axis=-1), ctx_768, L0_xattn_w_q, L0_xattn_w_kv, L0_xattn_w_out, L0_xattn_b_out)
    x = x + _L0_ffn_ref(_layernorm(x, axis=-1), L0_ffn_w_gate, L0_ffn_w_up, L0_ffn_w_down)
    x = x + _L1_xattn_ref(_layernorm(x, axis=-1), ctx_768, L1_xattn_Wq, L1_xattn_Wk, L1_xattn_Wv, L1_xattn_Wo, L1_xattn_bo, L1_xattn_q_down, L1_xattn_q_up, L1_xattn_q_alpha, L1_xattn_k_down, L1_xattn_k_up, L1_xattn_k_alpha, L1_xattn_v_down, L1_xattn_v_up, L1_xattn_v_alpha, L1_xattn_o_down, L1_xattn_o_up, L1_xattn_o_alpha, L1_xattn_Wk_ipa, L1_xattn_Wv_ipa)
    x = x + _L1_ffn_ref(_layernorm(x, axis=-1), L1_ffn_Wr, L1_ffn_br, L1_ffn_W1, L1_ffn_b1, L1_ffn_W2, L1_ffn_b2)
    return x

_drawn_inputs = setup_inputs


def setup_inputs(seed=0):
    import zlib

    import numpy as np

    out = dict(_drawn_inputs(seed))
    spreads = {'L1_xattn_bo': (0.0, 0.1)}
    factors = {'L1_xattn_Wq': 2.799,
     'L1_xattn_Wk': 3.954,
     'L1_xattn_q_down': 7.826,
     'L1_xattn_q_up': 8.0,
     'L1_xattn_k_down': 8.0,
     'L1_xattn_k_up': 8.0,
     'L1_ffn_b2': 3.023}
    for name, (base, spread) in spreads.items():
        noise = np.random.default_rng([zlib.crc32(name.encode()), seed]).standard_normal(out[name].shape)
        drawn = base * np.exp(spread * noise) if base else spread * noise
        out[name] = jnp.asarray(drawn.astype(out[name].dtype))
    for name, factor in factors.items():
        out[name] = (out[name] * factor).astype(out[name].dtype)
    return out
```

```python
from contextlib import ExitStack

import concourse.bass as bass
from concourse import mybir

F32 = mybir.dt.float32
I16 = mybir.dt.int16
U16 = mybir.dt.uint16
U32 = mybir.dt.uint32
ALU = mybir.AluOpType
ACT = mybir.ActivationFunctionType
AX = mybir.AxisListType
RMAX = bass.bass_isa.ReduceOp.max

P = 128
B, S, D = 4, 1024, 256
T = B * S
NT = T // P
DT = D // P
KV, C = 64, 192
C1 = C - P
H, HD = 16, 64
INNER = H * HD
NP = INNER // P
IPA = 4
RANK = 32
FF, QB = 768, 32
FT = FF // P
CH = 512
NC = T // CH
E, HID = 8, 1024
HT = HID // P
EPS = 1e-5
MAGIC = 12582912.0
QACT = 32767.0


class Scope:

    def __init__(self, nc, tag):
        self.nc, self.tag, self.ctx = nc, tag, ExitStack()

    def __enter__(self):
        self.ctx.__enter__()
        return self

    def __exit__(self, *a):
        return self.ctx.__exit__(*a)

    def sb(self, name, shape, dt=F32):
        return self.ctx.enter_context(self.nc.sbuf_tensor(f"{self.tag}_{name}", shape, dt))

    def ps(self, name, shape, dt=F32):
        return self.ctx.enter_context(self.nc.psum_tensor(f"{self.tag}_{name}", shape, dt))

    def sem(self, name):
        return self.ctx.enter_context(self.nc.semaphore(f"{self.tag}_{name}"))

    def block(self):
        return self.ctx.enter_context(self.nc.Block())


def load_and_stats(nc, x, ctx_in, x_res, stats, ident, ctxT):
    with Scope(nc, "ld") as s:
        crow = s.sb("crow", [P, 2, C])
        pT = s.ps("pT", [P, 4, P])
        xin, cin = s.sem("xin"), s.sem("cin")
        idz, idr, ctx_t = s.sem("idz"), s.sem("idr"), s.sem("ctx_t")
        xv = x.rearrange("b (t p) d -> p (b t) d", p=P)
        block = s.block()
        G = 4

        @block.sync
        def _(sp):
            sp.dma_start(crow[:, :, :], ctx_in.rearrange("(r b) k c -> (b k) r c", r=2)).then_inc(cin, 16)
            for g in range(NT // G):
                sp.dma_start(x_res[:, G * g:G * g + G, :], xv[:, G * g:G * g + G, :]).then_inc(xin, 16)
                sp.wait_ge(xin, 16 * (g + 1))

        @block.gpsimd
        def _(pool):
            nc.gpsimd.memset(ident[:, :], 0.0).then_inc(idz, 1)
            pool.wait_ge(idz, 1)
            nc.gpsimd.affine_select(out=ident[:, :], in_=ident[:, :], compare_op=ALU.not_equal, fill=1.0,
                                    base=0, pattern=[[-1, P]], channel_multiplier=1).then_inc(idr, 1)

        @block.tensor
        def _(pe):
            pe.wait_ge(idr, 1)
            pe.wait_ge(cin, 16)
            for r in range(2):
                nc.tensor.transpose(pT[:, 2 * r, :], crow[:, r, 0:P], ident[:, :])
                last = nc.tensor.transpose(pT[0:C1, 2 * r + 1, :], crow[:, r, P:C], ident[:, :])
            last.then_inc(ctx_t, 1)

        @block.vector
        def _(dve):
            dve.wait_ge(ctx_t, 1)
            for r in range(2):
                nc.vector.tensor_copy(ctxT[:, 0, r * P:(r + 1) * P], pT[:, 2 * r, :])
                nc.vector.tensor_copy(ctxT[0:C1, 1, r * P:(r + 1) * P], pT[0:C1, 2 * r + 1, :])
            for t in range(NT):
                if t % G == 0:
                    dve.wait_ge(xin, 16 * (t // G + 1))
                nc.vector.bn_stats(stats[:, t, :], x_res[:, t, :])


def prepare_attention(nc, tag, w, ctxT, ident, M, VW):
    lora = "q_down" in w
    RING = 6
    with Scope(nc, tag) as s:
        wq, wk, wv = (s.sb(n, [P, 2, INNER]) for n in ("wq", "wk", "wv"))
        wo = s.sb("wo", [P, NP, D])
        WqT = s.sb("WqT", [P, NP, D])
        Kd = s.sb("Kd", [P, NP, B, P])
        Vd = s.sb("Vd", [P, NP, B, P])
        if lora:
            wki, wvi = (s.sb(n, [P, 2, INNER]) for n in ("wki", "wvi"))
            down = s.sb("down", [P, 3, 2, RANK])
            odown = s.sb("odown", [P, NP, RANK])
            up = s.sb("up", [RANK, INNER])
            oup = s.sb("oup", [RANK, D])
            downT = s.sb("downT", [RANK, 4, P])
            odownT = s.sb("odownT", [RANK, NP, P])
            alpha = s.sb("alpha", [P, 4])
            alpha_r = s.sb("alpha_r", [P, 4])
            ups = {"q": up}
        ring = s.ps("ring", [P, RING, CH])
        loaded, up_in, made, moved, zero = (s.sem(n) for n in ("loaded", "up_in", "made", "moved", "zero"))
        used, alpha_s = s.sem("used"), s.sem("alpha_s")
        block = s.block()
        loads = [(wq[:, :, :], w["q"].rearrange("(t p) n -> p t n", p=P)),
                 (wo[:, :, :], w["o"].rearrange("(t p) n -> p t n", p=P))]
        for dst, key in ((wk, "k"), (wv, "v")) + (((wki, "k_ipa"), (wvi, "v_ipa")) if lora else ()):
            loads += [(dst[:, 0, :], w[key][0:P, :]), (dst[0:C1, 1, :], w[key][P:C, :])]
        if lora:
            loads += [(down[:, 0, :, :], w["q_down"].rearrange("(t p) r -> p t r", p=P))]
            for n, key in ((1, "k_down"), (2, "v_down")):
                loads += [(down[:, n, 0, :], w[key][0:P, :]), (down[0:C1, n, 1, :], w[key][P:C, :])]
            loads += [(odown[:, :, :], w["o_down"].rearrange("(t p) r -> p t r", p=P)), (oup[:, :], w["o_up"])]
            for n, key in enumerate(("q_alpha", "k_alpha", "v_alpha", "o_alpha")):
                loads += [(alpha[:, n:n + 1], w[key].unsqueeze(0).to_broadcast([P, 1]))]
        rows = {"q": (P, P), "k": (P, C1), "v": (P, C1)}

        @block.sync
        def _(sp):
            for dst, src in loads:
                sp.dma_start(dst, src).then_inc(loaded, 16)
            if lora:
                for n, key in enumerate(("q_up", "k_up", "v_up")):
                    if n:
                        sp.wait_ge(used, n)
                    sp.dma_start(up[:, :], w[key]).then_inc(up_in, 16)

        @block.gpsimd
        def _(pool):
            nc.gpsimd.memset(Kd[:, :, :, :], 0.0).then_inc(zero, 1)
            nc.gpsimd.memset(Vd[:, :, :, :], 0.0).then_inc(zero, 1)

        @block.tensor
        def _(pe):
            n = [0]

            def bank():
                if n[0] >= RING:
                    pe.wait_ge(moved, n[0] - RING + 1)
                n[0] += 1
                return (n[0] - 1) % RING

            pe.wait_ge(loaded, 16 * len(loads))
            if lora:
                for i in range(3):
                    b = bank()
                    for t in range(2):
                        m = rows["qkv"[i]][t]
                        last = nc.tensor.transpose(ring[0:RANK, b, t * P:t * P + m], down[0:m, i, t, :], ident[0:m, 0:m])
                    last.then_inc(made, 1)
                    pe.wait_ge(moved, n[0])
                    pe.wait_ge(up_in, 16 * (i + 1))
                    for t in range(2):
                        m = rows["qkv"[i]][t]
                        for c in range(2):
                            b = bank()
                            last = nc.tensor.matmul(ring[0:m, b, :], downT[:, t, 0:m], up[:, c * CH:(c + 1) * CH],
                                                    start=True, stop=True)
                            last.then_inc(made, 1)
                    pe.wait_ge(moved, n[0])
                    pe.sem_inc(used, 1)
                for g in range(2):
                    b = bank()
                    for t in range(4):
                        last = nc.tensor.transpose(ring[0:RANK, b, t * P:(t + 1) * P], odown[:, 4 * g + t, :], ident[:, :])
                    last.then_inc(made, 1)
                pe.wait_ge(moved, n[0])
                for g in range(4):
                    b = bank()
                    for t in range(2):
                        last = nc.tensor.matmul(ring[:, b, t * D:(t + 1) * D], odownT[:, 2 * g + t, :], oup[:, :],
                                                start=True, stop=True)
                    last.then_inc(made, 1)
                pe.wait_ge(moved, n[0])
            for g in range(NP // 2):
                b = bank()
                for i in range(2):
                    for t in range(2):
                        last = nc.tensor.transpose(ring[:, b, i * D + t * P:i * D + (t + 1) * P],
                                                   wq[:, t, (2 * g + i) * P:(2 * g + i + 1) * P], ident[:, :])
                last.then_inc(made, 1)
            for base, ipa in ((wk, wki if lora else None), (wv, wvi if lora else None)):
                for j in range(NP):
                    b = bank()
                    parts = [(base, 0, KV - IPA), (ipa, KV - IPA, KV)] if lora else [(base, 0, KV)]
                    for wt, lo, hi in parts:
                        for t in range(2):
                            m = (P, C1)[t]
                            last = nc.tensor.matmul(
                                ring[:, b, 0:B * KV].rearrange("p (b k) -> p b k", b=B)[:, :, lo:hi],
                                wt[0:m, t, j * P:(j + 1) * P],
                                ctxT[0:m, t, :].rearrange("p (b k) -> p b k", b=B)[:, :, lo:hi],
                                start=(t == 0), stop=(t == 1))
                    last.then_inc(made, 1)
            pe.wait_ge(moved, n[0])
            for j in range(NP):
                for t in range(DT):
                    b = bank()
                    nc.tensor.matmul(ring[:, b, :], WqT[:, j, t * P:(t + 1) * P], Kd[:, j, :, :],
                                     start=True, stop=True).then_inc(made, 1)
            for j in range(NP):
                for g in range(2):
                    b = bank()
                    for i in range(2):
                        last = nc.tensor.matmul(ring[:, b, i * D:(i + 1) * D], Vd[:, j, 2 * g + i, :], wo[:, j, :],
                                                start=True, stop=True)
                    last.then_inc(made, 1)

        @block.vector
        def _(dve):
            n = [0]

            def bank():
                n[0] += 1
                dve.wait_ge(made, n[0])
                return (n[0] - 1) % RING

            dve.wait_ge(loaded, 16 * len(loads))
            dve.wait_ge(zero, 2)
            if lora:
                nc.vector.tensor_scalar(alpha_r[:, :], alpha[:, :], 1.0 / RANK, None, ALU.mult).then_inc(alpha_s, 1)
                dve.wait_ge(alpha_s, 1)
                for i, wt in enumerate((wq, wk, wv)):
                    b = bank()
                    if i == 0:
                        nc.vector.tensor_copy(downT[:, 0:2, :], ring[0:RANK, b, 0:2 * P]).then_inc(moved, 1)
                    else:
                        nc.vector.tensor_copy(downT[:, 0:2, :].rearrange("r t p -> r (t p)")[:, 0:C],
                                              ring[0:RANK, b, 0:C]).then_inc(moved, 1)
                    for t in range(2):
                        m = rows["qkv"[i]][t]
                        for c in range(2):
                            b = bank()
                            part = wt[0:m, t, c * CH:(c + 1) * CH]
                            nc.vector.scalar_tensor_tensor(out=part, in0=ring[0:m, b, :], scalar=alpha_r[0:m, i:i + 1],
                                                           in1=part, op0=ALU.mult, op1=ALU.add).then_inc(moved, 1)
                for g in range(2):
                    b = bank()
                    nc.vector.tensor_copy(odownT[:, 4 * g:4 * g + 4, :], ring[0:RANK, b, :]).then_inc(moved, 1)
                for g in range(4):
                    b = bank()
                    part = wo[:, 2 * g:2 * g + 2, :]
                    nc.vector.scalar_tensor_tensor(out=part, in0=ring[:, b, :].rearrange("p (t n) -> p t n", t=2),
                                                   scalar=alpha_r[:, 3:4], in1=part,
                                                   op0=ALU.mult, op1=ALU.add).then_inc(moved, 1)
            for g in range(NP // 2):
                b = bank()
                nc.vector.tensor_copy(WqT[:, 2 * g:2 * g + 2, :], ring[:, b, :]).then_inc(moved, 1)
            for dst in (Kd, Vd):
                for j in range(NP):
                    b = bank()
                    for h in range(2):
                        last = nc.vector.tensor_copy(dst[h * HD:(h + 1) * HD, j, :, h * KV:(h + 1) * KV],
                                                     ring[h * HD:(h + 1) * HD, b, 0:B * KV].rearrange("p (b k) -> p b k", b=B))
                    last.then_inc(moved, 1)
            for j in range(NP):
                for t in range(DT):
                    b = bank()
                    nc.vector.tensor_scalar(M[:, t, :, j * P:(j + 1) * P],
                                            ring[:, b, :].rearrange("p (b k) -> p b k", b=B),
                                            HD ** -0.5, None, ALU.mult).then_inc(moved, 1)
            for j in range(NP):
                for g in range(2):
                    b = bank()
                    nc.vector.tensor_copy(VW[:, 2 * g:2 * g + 2, j, :],
                                          ring[:, b, :].rearrange("p (b n) -> p b n", b=2)).then_inc(moved, 1)


def rstd_of(nc, tag, stats, mv, rstd):
    with Scope(nc, tag) as s:
        ve, sd = s.sb("ve", [P, NT]), s.sb("sd", [P, NT])
        m, a, b = s.sem("m"), s.sem("a"), s.sem("b")
        block = s.block()

        @block.vector
        def _(dve):
            for t in range(NT):
                last = nc.vector.bn_aggr(mv[:, t, :], stats[:, t, :])
            last.then_inc(m, 1)
            dve.wait_ge(m, 1)
            nc.vector.tensor_scalar(ve[:, :], mv[:, :, 1], EPS, None, ALU.add).then_inc(a, 1)
            dve.wait_ge(b, 1)
            nc.vector.reciprocal(rstd[:, :], sd[:, :])

        @block.scalar
        def _(act):
            act.wait_ge(a, 1)
            nc.scalar.activation(sd[:, :], ve[:, :], ACT.Sqrt).then_inc(b, 1)


def attention(nc, tag, groups, bias_in, x_res, mv, rstd, stats, ident, M, VW):
    NG = len(groups)
    with Scope(nc, tag) as s:
        xn = s.sb("xn", [P, 2, D])
        xnT = [s.sb(f"xnT{j}", [P, DT, P]) for j in range(2)]
        sc = [s.sb(f"sc{j}", [P, H, KV]) for j in range(2)]
        mx = s.sb("mx", [P, 2, H, NG])
        sm = s.sb("sm", [P, 2, H, NG])
        ri = s.sb("ri", [P, 2, H, NG])
        pT = [s.sb(f"pT{j}", [P, NP, P]) for j in range(2)]
        bias = s.sb("bias", [P, D])
        new = [s.sb(f"new{j}", [P, D]) for j in range(2)]
        st = [s.sb(f"st{j}", [P, 6]) for j in range(2)]
        ps_xT = s.ps("ps_xT", [P, DT, P])
        ps_s = [s.ps(f"ps_s{j}", [P, INNER]) for j in range(2)]
        ps_p = s.ps("ps_p", [P, NP, P])
        ps_y = s.ps("ps_y", [P, D])
        names = ("bias_in", "xn_r", "xb_r", "xT_r", "xnT_r", "sc_r", "mx_r", "sub_r", "exp_r", "sum_r", "ri_r",
                 "prob_r", "pT_r", "pTs_r", "y_r", "res_r", "st_r", "new_c")
        (bias_s, xn_r, xb_r, xT_r, xnT_r, sc_r, mx_r, sub_r, exp_r, sum_r, ri_r,
         prob_r, pT_r, pTs_r, y_r, res_r, st_r, new_c) = (s.sem(n) for n in names)
        block = s.block()

        def steps(eng, step):
            step(0, 0, 2, True)
            step(1, 1, 2, True)
            with eng.Fori(1, NT // 2 - 1, 1) as i:
                for j in range(2):
                    step(2 * i + j, j, 2, False)
            step(NT - 2, 0, 1, False)
            step(NT - 1, 1, 0, False)

        def tile(buf, t):
            return buf[:, bass.ds(t, 1), :].rearrange("p o d -> p (o d)")

        @block.sync
        def _(sp):
            sp.dma_start(bias[:, :], bias_in.unsqueeze(0).to_broadcast([P, D])).then_inc(bias_s, 16)

        @block.tensor
        def _(pe):
            def turn_x(t, j, first):
                pe.wait_ge(xn_r, t + 1)
                if not first:
                    pe.wait_ge(xnT_r, t)
                for d in range(DT):
                    last = nc.tensor.transpose(ps_xT[:, d, :], xn[:, j, d * P:(d + 1) * P], ident[:, :])
                last.then_inc(xT_r, 1)

            def scores(t, j, first):
                pe.wait_ge(xnT_r, t + 1)
                if not first:
                    pe.wait_ge(sub_r, t - 1)
                off = t // (NT // B) * INNER
                for c in range(2):
                    for d in range(DT):
                        last = nc.tensor.matmul(ps_s[j][:, c * CH:(c + 1) * CH], xnT[j][:, d, :],
                                                M[:, d, :, :].rearrange("p b n -> p (b n)")[:, bass.ds(off + c * CH, CH)],
                                                start=(d == 0), stop=(d == DT - 1))
                last.then_inc(sc_r, 1)

            def turn_probs(t, j, first):
                pe.wait_ge(prob_r, t + 1)
                if not first:
                    pe.wait_ge(pTs_r, 2 * t)
                for g in range(2):
                    for i in range(4):
                        n = 4 * g + i
                        last = nc.tensor.transpose(ps_p[:, n, :], sc[j][:, 2 * n:2 * n + 2, :], ident[:, :])
                    last.then_inc(pT_r, 1)

            def output(t, j, first):
                if not first:
                    pe.wait_ge(res_r, t)
                off = t // (NT // B) * (NP * D)
                vw = VW[:, :, :, :].rearrange("p b j n -> p (b j n)")
                for n in range(NP):
                    if n % 4 == 0:
                        pe.wait_ge(pTs_r, 2 * t + n // 4 + 1)
                    last = nc.tensor.matmul(ps_y[:, :], pT[j][:, n, :], vw[:, bass.ds(off + n * D, D)],
                                            start=(n == 0), stop=(n == NP - 1))
                last.then_inc(y_r, 1)

            def step(k, j, more, head):
                if more >= 1:
                    scores(k + 1, 1 - j, head and k == 0)
                turn_probs(k, j, head and k == 0)
                if more >= 2:
                    turn_x(k + 2, j, False)
                output(k, j, head and k == 0)

            turn_x(0, 0, True)
            turn_x(1, 1, False)
            scores(0, 0, True)
            steps(nc.tensor, step)

        @block.scalar
        def _(act):
            def copy_xT(t, j, first):
                act.wait_ge(xT_r, t + 1)
                if not first:
                    act.wait_ge(sc_r, t - 1)
                nc.scalar.copy(xnT[j][:, :, :], ps_xT[:, :, :]).then_inc(xnT_r, 1)

            def copy_pT(t, j, first):
                if not first:
                    act.wait_ge(y_r, t - 1)
                for g in range(2):
                    act.wait_ge(pT_r, 2 * t + g + 1)
                    nc.scalar.copy(pT[j][:, 4 * g:4 * g + 4, :], ps_p[:, 4 * g:4 * g + 4, :]).then_inc(pTs_r, 1)

            def exps(t, j):
                act.wait_ge(sub_r, t + 1)
                nc.scalar.activation(sc[j][:, :, :], sc[j][:, :, :], ACT.Exp).then_inc(exp_r, 1)

            def keep(t, j):
                act.wait_ge(res_r, t + 1)
                nc.scalar.copy(tile(x_res, t), new[j][:, :]).then_inc(new_c, 1)

            def step(k, j, more, head):
                if not (head and k == 0):
                    keep(k - 1, 1 - j)
                copy_pT(k, j, head)
                if more >= 2:
                    copy_xT(k + 2, j, False)
                if more >= 1:
                    exps(k + 1, 1 - j)

            copy_xT(0, 0, True)
            copy_xT(1, 1, True)
            exps(0, 0)
            steps(nc.scalar, step)
            keep(NT - 1, 1)

        @block.vector
        def _(dve):
            def norm(t, j, first):
                if not first:
                    dve.wait_ge(xT_r, t - 1)
                tt = tile(x_res, t)
                nc.vector.tensor_scalar(xn[:, j, :], tt, mv[:, bass.ds(t, 1), 0:1].rearrange("p a b -> p (a b)"),
                                        rstd[:, bass.ds(t, 1)], ALU.subtract, ALU.mult).then_inc(xn_r, 1)
                nc.vector.tensor_tensor(tt, tt, bias[:, :], ALU.add).then_inc(xb_r, 1)

            def softmax_in(t, j, first):
                dve.wait_ge(sc_r, t + 1)
                scv = ps_s[j][:, :].rearrange("p (h k) -> p h k", h=H)
                for g, (lo, hi) in enumerate(groups):
                    last = nc.vector.tensor_reduce(mx[:, j, :, g], scv[:, :, lo:hi], AX.X, ALU.max)
                last.then_inc(mx_r, 1)
                dve.wait_ge(mx_r, t + 1)
                if not first:
                    dve.wait_ge(pT_r, 2 * (t - 1))
                for g, (lo, hi) in enumerate(groups):
                    last = nc.vector.tensor_tensor(sc[j][:, :, lo:hi], scv[:, :, lo:hi],
                                                   mx[:, j, :, g].unsqueeze(2).to_broadcast([P, H, hi - lo]),
                                                   ALU.subtract)
                last.then_inc(sub_r, 1)

            def sums(t, j, first):
                dve.wait_ge(exp_r, t + 1)
                for g, (lo, hi) in enumerate(groups):
                    last = nc.vector.tensor_reduce(sm[:, j, :, g], sc[j][:, :, lo:hi], AX.X, ALU.add)
                last.then_inc(sum_r, 1)
                dve.wait_ge(sum_r, t + 1)
                if not first:
                    dve.wait_ge(prob_r, t - 1)
                nc.vector.reciprocal(ri[:, j, :, :], sm[:, j, :, :]).then_inc(ri_r, 1)

            def residual(t, j, first):
                dve.wait_ge(y_r, t + 1)
                dve.wait_ge(xb_r, t + 1)
                if not first:
                    dve.wait_ge(new_c, t - 1)
                nc.vector.tensor_tensor(new[j][:, :], ps_y[:, :], tile(x_res, t), ALU.add).then_inc(res_r, 1)
                dve.wait_ge(res_r, t + 1)
                nc.vector.bn_stats(st[j][:, :], new[j][:, :]).then_inc(st_r, 1)
                dve.wait_ge(st_r, t + 1)
                nc.vector.tensor_copy(tile(stats, t), st[j][:, :])

            def step(k, j, more, head):
                if more >= 2:
                    norm(k + 2, j, False)
                if more >= 1:
                    softmax_in(k + 1, 1 - j, head and k == 0)
                    sums(k + 1, 1 - j, head and k == 0)
                residual(k, j, head)

            dve.wait_ge(bias_s, 16)
            norm(0, 0, True)
            norm(1, 1, True)
            softmax_in(0, 0, True)
            sums(0, 0, True)
            steps(nc.vector, step)

        @block.gpsimd
        def _(pool):
            def step(k, j, more, head):
                pool.wait_ge(ri_r, k + 1)
                for g, (lo, hi) in enumerate(groups):
                    part = sc[j][:, :, lo:hi]
                    last = nc.gpsimd.tensor_tensor(part, part, ri[:, j, :, g].unsqueeze(2).to_broadcast([P, H, hi - lo]),
                                                   ALU.mult)
                last.then_inc(prob_r, 1)

            steps(nc.gpsimd, step)


def quantise_weights(nc, w_gate, w_up, w_down, WgT, WuT, WdT, ident):
    NB = FF * D // (P * QB)
    with Scope(nc, "qw") as s:
        w = [s.sb(f"w{i}", [P, NB, QB]) for i in range(3)]
        am, sc, rs = s.sb("am", [P, NB]), s.sb("sc", [P, NB]), s.sb("rs", [P, NB])
        ring = s.ps("ring", [P, 4, CH])
        loaded = [s.sem(f"loaded{i}") for i in range(3)]
        c, ready, made, moved = s.sem("c"), s.sem("ready"), s.sem("made"), s.sem("moved")
        block = s.block()

        @block.sync
        def _(sp):
            for i, src in enumerate((w_gate, w_up, w_down)):
                sp.dma_start(w[i][:, :, :].rearrange("p (o b) q -> p o (b q)", o=src.shape[0] // P),
                             src.rearrange("(o p) i -> p o i", p=P)).then_inc(loaded[i], 16)

        @block.vector
        def _(dve):
            n = [0]

            def then(ins):
                n[0] += 1
                ins.then_inc(c, 1)
                dve.wait_ge(c, n[0])

            for i in range(3):
                dve.wait_ge(loaded[i], 16)
                wi, per = w[i][:, :, :], [P, NB, QB]
                then(nc.vector.tensor_reduce(am[:, :], wi, AX.X, ALU.max, apply_absolute_value=True))
                then(nc.vector.tensor_scalar(sc[:, :], am[:, :], 1.0 / 7.0, 1e-12, ALU.mult, ALU.max))
                then(nc.vector.reciprocal(rs[:, :], sc[:, :]))
                then(nc.vector.tensor_tensor(wi, wi, rs[:, :].unsqueeze(2).to_broadcast(per), ALU.mult))
                then(nc.vector.tensor_scalar(wi, wi, MAGIC, MAGIC, ALU.add, ALU.subtract))
                then(nc.vector.tensor_scalar(wi, wi, 7.0, -8.0, ALU.min, ALU.max))
                nc.vector.tensor_tensor(wi, wi, sc[:, :].unsqueeze(2).to_broadcast(per), ALU.mult).then_inc(ready, 1)
            m = 0
            for i, dst in enumerate((WgT, WuT)):
                for g in range(3):
                    m += 1
                    dve.wait_ge(made, m)
                    nc.vector.tensor_copy(dst[:, :, 2 * g * P:(2 * g + 2) * P],
                                          ring[:, (m - 1) % 4, :].rearrange("p (d n) -> p d n", d=DT)).then_inc(moved, 1)
            for g in range(3):
                m += 1
                dve.wait_ge(made, m)
                nc.vector.tensor_copy(WdT[:, 2 * g:2 * g + 2, :], ring[:, (m - 1) % 4, :]).then_inc(moved, 1)

        @block.tensor
        def _(pe):
            m = 0
            for i in range(3):
                pe.wait_ge(ready, i + 1)
                src = w[i][:, :, :].rearrange("p (o b) q -> p o (b q)", o=DT if i == 2 else FT)
                for g in range(3):
                    if m >= 4:
                        pe.wait_ge(moved, m - 3)
                    for a in range(2):
                        for b in range(2):
                            if i < 2:
                                blk = src[:, 2 * g + b, a * P:(a + 1) * P]
                            else:
                                blk = src[:, b, (2 * g + a) * P:(2 * g + a + 1) * P]
                            last = nc.tensor.transpose(ring[:, m % 4, (2 * a + b) * P:(2 * a + b + 1) * P], blk, ident[:, :])
                    last.then_inc(made, 1)
                    m += 1


def quantise_input(nc, x_res, mv, rstd, scale_x, xqT, ident):
    with Scope(nc, "qx") as s:
        xn = s.sb("xn", [P, NT, D])
        q = s.sb("q", [P, 2, D])
        am, gm, inv = s.sb("am", [P, 1]), s.sb("gm", [P, 1]), s.sb("inv", [P, 1])
        ps = [s.ps(f"ps{j}", [P, 512]) for j in range(2)]
        c, am_r, gm_r, q_r, t_r, e_r = (s.sem(n) for n in ("c", "am_r", "gm_r", "q_r", "t_r", "e_r"))
        block = s.block()

        @block.vector
        def _(dve):
            for t in range(NT):
                last = nc.vector.tensor_scalar(xn[:, t, :], x_res[:, t, :], mv[:, t, 0:1], rstd[:, t:t + 1],
                                               ALU.subtract, ALU.mult)
            last.then_inc(c, 1)
            dve.wait_ge(c, 1)
            nc.vector.tensor_reduce(am[:, :], xn[:, :, :], AX.XY, ALU.max, apply_absolute_value=True).then_inc(am_r, 1)
            dve.wait_ge(gm_r, 1)
            nc.vector.tensor_scalar(scale_x[:, :], gm[:, :], 1.0 / QACT, 1e-12, ALU.mult, ALU.max).then_inc(c, 1)
            dve.wait_ge(c, 2)
            nc.vector.reciprocal(inv[:, :], scale_x[:, :]).then_inc(c, 1)
            dve.wait_ge(c, 3)
            for j in range(2):
                nc.vector.tensor_scalar(q[:, j, :], xn[:, j, :], inv[:, 0:1], MAGIC, ALU.mult, ALU.add).then_inc(q_r, 1)
            with nc.vector.Fori(1, NT // 2, 1) as i:
                for j in range(2):
                    dve.wait_ge(t_r, 2 * i + j - 1)
                    nc.vector.tensor_scalar(q[:, j, :], xn[:, bass.ds(2 * i + j, 1), :].rearrange("p a d -> p (a d)"),
                                            inv[:, 0:1], MAGIC, ALU.mult, ALU.add).then_inc(q_r, 1)

        @block.gpsimd
        def _(pool):
            pool.wait_ge(am_r, 1)
            nc.gpsimd.partition_all_reduce(gm[:, :], am[:, :], P, RMAX).then_inc(gm_r, 1)

        @block.tensor
        def _(pe):
            def turn(t, j):
                pe.wait_ge(q_r, t + 1)
                for d in range(DT):
                    last = nc.tensor.transpose(ps[j][:, d * P:(d + 1) * P], q[:, j, d * P:(d + 1) * P], ident[:, :])
                last.then_inc(t_r, 1)

            turn(0, 0)
            turn(1, 1)
            with nc.tensor.Fori(1, NT // 2, 1) as i:
                for j in range(2):
                    pe.wait_ge(e_r, 2 * i + j - 1)
                    turn(2 * i + j, j)

        @block.scalar
        def _(act):
            with nc.scalar.Fori(0, NT // 2, 1) as i:
                for j in range(2):
                    act.wait_ge(t_r, 2 * i + j + 1)
                    nc.scalar.activation(xqT[:, :, bass.ds((2 * i + j) * P, P)],
                                         ps[j][:, 0:D].rearrange("p (d n) -> p d n", d=DT), ACT.Copy,
                                         bias=-MAGIC).then_inc(e_r, 1)


def gated_mlp(nc, x_res, stats, scale_x, xqT, WgT, WuT, WdT, up_dram, gate):
    HF = FT // 2
    U = HF * CH
    NU = 2 * NC

    with Scope(nc, "gm") as s:
        gmax, umax, pmax = s.sb("gmax", [P, NC]), s.sb("umax", [P, NU]), s.sb("pmax", [P, NU])
        red = s.sb("red", [P, 3])
        allr = s.sb("allr", [P, 3])
        sc = s.sb("sc", [P, 8])
        SG, SU, SP, IU, IP, IG = range(6)
        stg = [s.sb(f"stg{j}", [P, U]) for j in range(2)]
        gq = [s.sb(f"gq{j}", [P, U], I16) for j in range(2)]
        sq = [s.sb(f"sq{j}", [P, U], U16) for j in range(2)]
        uq = [x[:, :].bitcast(I16) for x in sq]
        bank = [s.ps(f"bank{i}", [P, CH]) for i in range(FT)]
        with Scope(nc, "gu") as z:
            g_mm, g_ev, gm_s, c = z.sem("g_mm"), z.sem("g_ev"), z.sem("gm_s"), z.sem("c")
            u_mm, u_ev, u_red = z.sem("u_mm"), z.sem("u_ev"), z.sem("u_red")
            u_st = [z.sem(f"u_st{h}") for h in range(2)]
            gq_r, sig_r, sq_r, pr_r = z.sem("gq_r"), z.sem("sig_r"), z.sem("sq_r"), z.sem("pr_r")
            gred, gall, sg_r, pm_s = z.sem("gred"), z.sem("gall"), z.sem("sg_r"), z.sem("pm_s")
            block = z.block()

            def unit(u):
                return gate[:, bass.ds(u * U, U)]

            @block.tensor
            def _(pe):
                def half(w, h, c0, mm):
                    for i in range(HF):
                        o = h * HF + i
                        for d in range(DT):
                            last = nc.tensor.matmul(bank[o][:, :], w[:, d, o * P:(o + 1) * P],
                                                    xqT[:, d, bass.ds(c0, CH)], start=(d == 0), stop=(d == DT - 1))
                        last.then_inc(mm, 1)

                for h in range(2):
                    half(WgT, h, 0, g_mm)
                with nc.tensor.Fori(1, NC, 1) as k:
                    for h in range(2):
                        pe.wait_ge(g_ev, FT * (k - 1) + HF * (h + 1))
                        half(WgT, h, k * CH, g_mm)
                for h in range(2):
                    pe.wait_ge(g_ev, FT * (NC - 1) + HF * (h + 1))
                    half(WuT, h, 0, u_mm)
                with nc.tensor.Fori(1, NC, 1) as k:
                    for h in range(2):
                        pe.wait_ge(u_ev, FT * (k - 1) + HF * (h + 1))
                        half(WuT, h, k * CH, u_mm)

            @block.scalar
            def _(act):
                with nc.scalar.Fori(0, NC, 1) as k:
                    for o in range(FT):
                        act.wait_ge(g_mm, FT * k + o + 1)
                        nc.scalar.activation(gate[:, bass.ds((FT * k + o) * CH, CH)], bank[o][:, :], ACT.Copy,
                                             scale=scale_x[:, 0:1]).then_inc(g_ev, 1)

                def up_half(k, h, first):
                    if not first:
                        act.wait_ge(u_st[h], 16 * k)
                        act.wait_ge(u_red, 2 * k + h - 1)
                    for i in range(HF):
                        act.wait_ge(u_mm, FT * k + h * HF + i + 1)
                        nc.scalar.activation(stg[h][:, i * CH:(i + 1) * CH], bank[h * HF + i][:, :], ACT.Copy,
                                             scale=scale_x[:, 0:1]).then_inc(u_ev, 1)

                def sigmoid(u, h):
                    act.wait_ge(gq_r, u + 1)
                    nc.scalar.activation(unit(u), gq[h][:, :], ACT.Sigmoid, scale=sc[:, SG:SG + 1]).then_inc(sig_r, 1)

                act.wait_ge(sg_r, 2)
                for h in range(2):
                    up_half(0, h, True)
                    sigmoid(h, h)
                with nc.scalar.Fori(1, NC, 1) as k:
                    for h in range(2):
                        up_half(k, h, False)
                        sigmoid(2 * k + h, h)

            @block.vector
            def _(dve):
                with nc.vector.Fori(0, NC, 1) as k:
                    dve.wait_ge(g_ev, FT * (k + 1))
                    nc.vector.tensor_reduce(gmax[:, bass.ds(k, 1)], gate[:, bass.ds(k * FT * CH, FT * CH)], AX.X, ALU.max,
                                            apply_absolute_value=True).then_inc(gm_s, 1)
                dve.wait_ge(gm_s, NC)
                nc.vector.tensor_reduce(red[:, 0:1], gmax[:, :], AX.X, ALU.max).then_inc(gred, 1)
                dve.wait_ge(gall, 1)
                nc.vector.tensor_scalar(sc[:, SG:SG + 1], allr[:, 0:1], 1.0 / QACT, 1e-12, ALU.mult, ALU.max).then_inc(sg_r, 1)
                dve.wait_ge(sg_r, 1)
                nc.vector.reciprocal(sc[:, IG:IG + 1], sc[:, SG:SG + 1]).then_inc(sg_r, 1)
                dve.wait_ge(sg_r, 2)

                def levels(u, h):
                    nc.vector.tensor_scalar(gq[h][:, :], unit(u), sc[:, IG:IG + 1], None, ALU.mult).then_inc(gq_r, 1)

                def sig_levels(u, h):
                    dve.wait_ge(sig_r, u + 1)
                    nc.vector.tensor_scalar(sq[h][:, :], unit(u), 65536.0, 65535.0, ALU.mult, ALU.min).then_inc(sq_r, 1)
                    dve.wait_ge(sq_r, u + 1)
                    nc.vector.tensor_tensor(unit(u), gq[h][:, :], sq[h][:, :], ALU.mult).then_inc(pr_r, 1)

                def up_max(k, h):
                    dve.wait_ge(u_ev, FT * k + HF * (h + 1))
                    nc.vector.tensor_reduce(umax[:, bass.ds(2 * k + h, 1)], stg[h][:, :], AX.X, ALU.max,
                                            apply_absolute_value=True).then_inc(u_red, 1)

                def prod_max(u):
                    dve.wait_ge(pr_r, u + 1)
                    nc.vector.tensor_reduce(pmax[:, bass.ds(u, 1)], unit(u), AX.X, ALU.max,
                                            apply_absolute_value=True).then_inc(pm_s, 1)

                levels(0, 0)
                levels(1, 1)
                up_max(0, 0)
                sig_levels(0, 0)
                up_max(0, 1)
                sig_levels(1, 1)
                with nc.vector.Fori(1, NC, 1) as k:
                    for h in range(2):
                        levels(2 * k + h, h)
                        up_max(k, h)
                        prod_max(2 * k + h - 2)
                        sig_levels(2 * k + h, h)
                for u in (NU - 2, NU - 1):
                    prod_max(u)
                dve.wait_ge(pm_s, NU)
                dve.wait_ge(u_red, NU)
                nc.vector.tensor_reduce(red[:, 1:2], umax[:, :], AX.X, ALU.max)
                nc.vector.tensor_reduce(red[:, 2:3], pmax[:, :], AX.X, ALU.max).then_inc(gred, 1)
                dve.wait_ge(gall, 2)
                nc.vector.tensor_scalar(sc[:, SU:SU + 1], allr[:, 1:2], 1.0 / QACT, 1e-12, ALU.mult, ALU.max)
                nc.vector.tensor_scalar(sc[:, SP:SP + 1], allr[:, 2:3], sc[:, SG:SG + 1], 1.0 / (65536.0 * QACT),
                                        ALU.mult, ALU.mult).then_inc(c, 1)
                dve.wait_ge(c, 1)
                nc.vector.tensor_scalar(sc[:, SP:SP + 1], sc[:, SP:SP + 1], 1e-12, None, ALU.max).then_inc(c, 1)
                dve.wait_ge(c, 2)
                nc.vector.reciprocal(sc[:, IU:IU + 1], sc[:, SU:SU + 1])
                nc.vector.reciprocal(sc[:, IP:IP + 1], sc[:, SP:SP + 1]).then_inc(c, 1)
                dve.wait_ge(c, 3)
                nc.vector.tensor_scalar(sc[:, IP:IP + 1], sc[:, IP:IP + 1], sc[:, SG:SG + 1], 1.0 / 65536.0,
                                        ALU.mult, ALU.mult)

            @block.gpsimd
            def _(pool):
                pool.wait_ge(gred, 1)
                nc.gpsimd.partition_all_reduce(allr[:, 0:1], red[:, 0:1], P, RMAX).then_inc(gall, 1)
                pool.wait_ge(gred, 2)
                nc.gpsimd.partition_all_reduce(allr[:, 1:3], red[:, 1:3], P, RMAX).then_inc(gall, 1)

            @block.sync
            def _(sp):
                with nc.sync.Fori(0, NC, 1) as k:
                    for h in range(2):
                        sp.wait_ge(u_ev, FT * k + HF * (h + 1))
                        sp.dma_start(up_dram[bass.ds(2 * k + h, 1), :, :].rearrange("a p n -> (a p) n"),
                                     stg[h][:, :]).then_inc(u_st[h], 16)
                for h in range(2):
                    sp.wait_ge(u_st[h], 16 * NC)

        with Scope(nc, "go") as z:
            ld = [z.sem(f"ld{j}") for j in range(2)]
            uq_r, gq_r, o_r, om_s, gred, gall, c = (z.sem(n) for n in ("uq_r", "gq_r", "o_r", "om_s", "gred", "gall", "c"))
            block = z.block()

            @block.sync
            def _(sp):
                for h in range(2):
                    sp.dma_start(stg[h][:, :], up_dram[h, :, :]).then_inc(ld[h], 16)
                with nc.sync.Fori(1, NC, 1) as k:
                    for h in range(2):
                        sp.wait_ge(uq_r, 2 * k + h - 1)
                        sp.dma_start(stg[h][:, :], up_dram[bass.ds(2 * k + h, 1), :, :].rearrange("a p n -> (a p) n")
                                     ).then_inc(ld[h], 16)

            @block.vector
            def _(dve):
                def quant(k, h):
                    u = 2 * k + h
                    nc.vector.tensor_scalar(gq[h][:, :], unit(u), sc[:, IP:IP + 1], None, ALU.mult)
                    dve.wait_ge(ld[h], 16 * (k + 1))
                    nc.vector.tensor_scalar(uq[h], stg[h][:, :],
                                            sc[:, IU:IU + 1], None, ALU.mult).then_inc(uq_r, 1)
                    dve.wait_ge(uq_r, u + 1)
                    nc.vector.tensor_tensor(unit(u), gq[h][:, :], uq[h], ALU.mult).then_inc(o_r, 1)

                def o_max(u):
                    dve.wait_ge(o_r, u + 1)
                    nc.vector.tensor_reduce(pmax[:, bass.ds(u, 1)], unit(u), AX.X, ALU.max,
                                            apply_absolute_value=True).then_inc(om_s, 1)

                quant(0, 0)
                quant(0, 1)
                with nc.vector.Fori(1, NC, 1) as k:
                    for h in range(2):
                        quant(k, h)
                        o_max(2 * k + h - 2)
                for u in (NU - 2, NU - 1):
                    o_max(u)
                dve.wait_ge(om_s, NU)
                nc.vector.tensor_reduce(red[:, 0:1], pmax[:, :], AX.X, ALU.max).then_inc(gred, 1)
                dve.wait_ge(gall, 1)
                nc.vector.tensor_scalar(sc[:, 6:7], sc[:, SU:SU + 1], sc[:, SP:SP + 1], None, ALU.mult).then_inc(c, 1)
                dve.wait_ge(c, 1)
                nc.vector.tensor_scalar(sc[:, 7:8], allr[:, 0:1], sc[:, 6:7], 1.0 / QACT, ALU.mult, ALU.mult).then_inc(c, 1)
                dve.wait_ge(c, 2)
                nc.vector.tensor_scalar(sc[:, 7:8], sc[:, 7:8], 1e-12, None, ALU.max).then_inc(c, 1)
                dve.wait_ge(c, 3)
                nc.vector.reciprocal(sc[:, IG:IG + 1], sc[:, 7:8]).then_inc(c, 1)
                dve.wait_ge(c, 4)
                nc.vector.tensor_scalar(sc[:, IG:IG + 1], sc[:, IG:IG + 1], sc[:, 6:7], None, ALU.mult)

            @block.gpsimd
            def _(pool):
                pool.wait_ge(gred, 1)
                nc.gpsimd.partition_all_reduce(allr[:, 0:1], red[:, 0:1], P, RMAX).then_inc(gall, 1)

        with Scope(nc, "gd") as z:
            o_mg, o_lv, mm, ev, st_r = (z.sem(n) for n in ("o_mg", "o_lv", "mm", "ev", "st_r"))
            new_c = z.sem("new_c")
            new = [x[:, 0:D] for x in stg]
            st = [z.sb(f"st{j}", [P, 6]) for j in range(2)]
            lv = [xqT[:, j, 0:FT * CH].rearrange("p (o n) -> p o n", o=FT) for j in range(DT)]
            block = z.block()
            TC = CH // P

            def tile(buf, t):
                return buf[:, bass.ds(t, 1), :].rearrange("p a d -> p (a d)")

            @block.scalar
            def _(act):
                with nc.scalar.Fori(0, NT // 2, 1) as i:
                    for j in range(2):
                        act.wait_ge(ev, 2 * i + j + 1)
                        nc.scalar.copy(tile(x_res, 2 * i + j), new[j]).then_inc(new_c, 1)

            @block.vector
            def _(dve):
                def levels(k, j, first):
                    if not first:
                        dve.wait_ge(mm, TC * (k - 1))
                    nc.vector.tensor_scalar(lv[j], gate[:, bass.ds(k * FT * CH, FT * CH)].rearrange("p (o n) -> p o n", o=FT),
                                            sc[:, IG:IG + 1], MAGIC, ALU.mult, ALU.add).then_inc(o_mg, 1)
                    dve.wait_ge(o_mg, k + 1)
                    nc.vector.tensor_scalar(lv[j], lv[j], MAGIC, None, ALU.subtract).then_inc(o_lv, 1)

                def residual(k, i, first=False):
                    t, j = TC * k + i, i % 2
                    dve.wait_ge(mm, t + 1)
                    if not (first and i < 2):
                        dve.wait_ge(new_c, t - 1)
                    nc.vector.scalar_tensor_tensor(out=new[j], in0=bank[j][:, 0:D], scalar=sc[:, 7:8],
                                                   in1=tile(x_res, t), op0=ALU.mult, op1=ALU.add).then_inc(ev, 1)
                    dve.wait_ge(ev, t + 1)
                    nc.vector.bn_stats(st[j][:, :], new[j]).then_inc(st_r, 1)
                    dve.wait_ge(st_r, t + 1)
                    nc.vector.tensor_copy(tile(stats, t), st[j][:, :])

                levels(0, 0, True)
                levels(1, 1, True)
                for i in range(TC):
                    residual(0, i, True)
                levels(2, 0, False)
                for i in range(TC):
                    residual(1, i)
                with nc.vector.Fori(1, NC // 2 - 1, 1) as m:
                    for j in range(2):
                        levels(2 * m + j + 1, 1 - j, False)
                        for i in range(TC):
                            residual(2 * m + j, i)
                levels(NC - 1, 1, False)
                for j in range(2):
                    for i in range(TC):
                        residual(NC - 2 + j, i)

            @block.tensor
            def _(pe):
                def chunk(k, j, first):
                    pe.wait_ge(o_lv, k + 1)
                    for i in range(TC):
                        t = TC * k + i
                        if not (first and i < 2):
                            pe.wait_ge(ev, t - 1)
                        for o in range(FT):
                            last = nc.tensor.matmul(bank[i % 2][:, 0:D], lv[j][:, o, i * P:(i + 1) * P], WdT[:, o, :],
                                                    start=(o == 0), stop=(o == FT - 1))
                        last.then_inc(mm, 1)

                chunk(0, 0, True)
                chunk(1, 1, False)
                with nc.tensor.Fori(1, NC // 2, 1) as m:
                    for j in range(2):
                        chunk(2 * m + j, j, False)


def route(nc, Wr, br, b1, b1T, x_res, mv, rstd, ident, xT, cw):
    with Scope(nc, "rt") as s:
        wr = s.sb("wr", [P, DT, E])
        brb = s.sb("brb", [P, E])
        b1r = s.sb("b1r", [E * HT, P])
        xn = s.sb("xn", [P, 2, D])
        xt = [s.sb(f"xt{j}", [P, DT, P]) for j in range(2)]
        scores = s.sb("scores", [P, NT, E])
        top = s.sb("top", [P, NT, 8])
        idx = s.sb("idx", [P, NT, 8], U32)
        idf = s.sb("idf", [P, NT, 2])
        eid = s.sb("eid", [P, E])
        oh = s.sb("oh", [P, 2, NT, E])
        wt = s.sb("wt", [P, 4, NT])
        ps_t = [s.ps(f"ps_t{j}", [P, CH]) for j in range(2)]
        ps_r = [s.ps(f"ps_r{j}", [P, CH]) for j in range(2)]
        w_in, id_r, xn_r, t_r, xt_r, xT_r, sc_mm, sc_r, c, e_r, d_r, b1_t, b1_c = (
            s.sem(n) for n in ("w_in", "id_r", "xn_r", "t_r", "xt_r", "xT_r", "sc_mm", "sc_r", "c", "e_r", "d_r", "b1_t", "b1_c"))
        block = s.block()

        @block.sync
        def _(sp):
            sp.dma_start(wr[:, :, :], Wr.rearrange("(t p) e -> p t e", p=P)).then_inc(w_in, 16)
            sp.dma_start(brb[:, :], br.unsqueeze(0).to_broadcast([P, E])).then_inc(w_in, 16)
            sp.dma_start(b1r[:, :], b1.rearrange("e (t p) -> (e t) p", p=P)).then_inc(w_in, 16)

        @block.gpsimd
        def _(pool):
            nc.gpsimd.iota(eid[:, :], pattern=[[1, E]], base=0, channel_multiplier=0,
                           allow_small_or_imprecise_dtypes=True).then_inc(id_r, 1)

        @block.tensor
        def _(pe):
            pe.wait_ge(w_in, 48)

            def tile(t, j, first):
                pe.wait_ge(xn_r, t + 1)
                if not first:
                    pe.wait_ge(xT_r, t - 1)
                for d in range(DT):
                    last = nc.tensor.transpose(ps_t[j][:, d * P:(d + 1) * P], xn[:, j, d * P:(d + 1) * P], ident[:, :])
                last.then_inc(t_r, 1)
                pe.wait_ge(xt_r, t + 1)
                if not first:
                    pe.wait_ge(sc_r, t - 1)
                for d in range(DT):
                    last = nc.tensor.matmul(ps_r[j][:, 0:E], xt[j][:, d, :], wr[:, d, :], start=(d == 0), stop=(d == DT - 1))
                last.then_inc(sc_mm, 1)

            nc.tensor.transpose(ps_r[0][:, 0:E * HT], b1r[:, :], ident[0:E * HT, 0:E * HT]).then_inc(b1_t, 1)
            pe.wait_ge(b1_c, 1)
            tile(0, 0, True)
            tile(1, 1, True)
            with nc.tensor.Fori(1, NT // 2, 1) as i:
                for j in range(2):
                    tile(2 * i + j, j, False)

        @block.scalar
        def _(act):
            def tile(t, j, first):
                act.wait_ge(t_r, t + 1)
                if not first:
                    act.wait_ge(sc_mm, t - 1)
                nc.scalar.copy(xt[j][:, :, :], ps_t[j][:, 0:D].rearrange("p (d n) -> p d n", d=DT)).then_inc(xt_r, 1)
                act.wait_ge(xt_r, t + 1)
                nc.scalar.copy(xT[:, :, bass.ds(t * P, P)], xt[j][:, :, :]).then_inc(xT_r, 1)

            tile(0, 0, True)
            tile(1, 1, True)
            with nc.scalar.Fori(1, NT // 2, 1) as i:
                for j in range(2):
                    tile(2 * i + j, j, False)
            act.wait_ge(d_r, 1)
            nc.scalar.activation(wt[:, 1, :], wt[:, 0, :], ACT.Exp).then_inc(e_r, 1)

        @block.vector
        def _(dve):
            dve.wait_ge(w_in, 48)

            def norm(t, j, first):
                if not first:
                    dve.wait_ge(t_r, t - 1)
                nc.vector.tensor_scalar(xn[:, j, :], x_res[:, bass.ds(t, 1), :].rearrange("p a d -> p (a d)"),
                                        mv[:, bass.ds(t, 1), 0:1].rearrange("p a b -> p (a b)"), rstd[:, bass.ds(t, 1)],
                                        ALU.subtract, ALU.mult).then_inc(xn_r, 1)

            def score(t, j):
                dve.wait_ge(sc_mm, t + 1)
                nc.vector.tensor_tensor(scores[:, bass.ds(t, 1), :].rearrange("p a e -> p (a e)"), ps_r[j][:, 0:E],
                                        brb[:, :], ALU.add).then_inc(sc_r, 1)

            dve.wait_ge(b1_t, 1)
            nc.vector.tensor_copy(b1T[:, :], ps_r[0][:, 0:E * HT]).then_inc(b1_c, 1)
            norm(0, 0, True)
            norm(1, 1, True)
            with nc.vector.Fori(1, NT // 2, 1) as i:
                for j in range(2):
                    norm(2 * i + j, j, False)
                    score(2 * i + j - 2, j)
            for j in range(2):
                score(NT - 2 + j, j)
            dve.wait_ge(sc_r, NT)
            n = [0]

            def then(ins):
                n[0] += 1
                ins.then_inc(c, 1)
                dve.wait_ge(c, n[0])

            for t in range(NT):
                last = nc.vector.max(out=top[:, t, :], in_=scores[:, t, :])
            then(last)
            for t in range(NT):
                last = nc.vector.max_index(out=idx[:, t, :], in_max=top[:, t, :], in_values=scores[:, t, :])
            then(last)
            then(nc.vector.tensor_copy(idf[:, :, :], idx[:, :, 0:2]))
            dve.wait_ge(id_r, 1)
            for k in range(2):
                last = nc.vector.tensor_tensor(oh[:, k, :, :], idf[:, :, k].unsqueeze(2).to_broadcast([P, NT, E]),
                                               eid[:, :].unsqueeze(1).to_broadcast([P, NT, E]), ALU.is_equal)
            then(last)
            nc.vector.tensor_tensor(wt[:, 0, :], top[:, :, 1], top[:, :, 0], ALU.subtract).then_inc(d_r, 1)
            dve.wait_ge(e_r, 1)
            then(nc.vector.tensor_scalar(wt[:, 0, :], wt[:, 1, :], 1.0, None, ALU.add))
            then(nc.vector.reciprocal(wt[:, 2, :], wt[:, 0, :]))
            then(nc.vector.tensor_tensor(wt[:, 3, :], wt[:, 1, :], wt[:, 2, :], ALU.mult))
            for k in range(2):
                last = nc.vector.tensor_tensor(oh[:, k, :, :], oh[:, k, :, :],
                                               wt[:, 2 + k, :].unsqueeze(2).to_broadcast([P, NT, E]), ALU.mult)
            then(last)
            nc.vector.tensor_tensor(cw[:, :, :], oh[:, 0, :, :], oh[:, 1, :, :], ALU.add)


def experts(nc, W1, b1T, W2, b2, x_res, xT, cw):
    TC = CH // P
    with Scope(nc, "ex") as s:
        w1 = [s.sb(f"w1_{j}", [P, DT, HID]) for j in range(2)]
        w2 = [s.sb(f"w2_{j}", [P, HT, D]) for j in range(2)]
        b2s = [s.sb(f"b2_{j}", [P, D]) for j in range(2)]
        hT = [s.sb(f"hT{j}", [P, HT, CH]) for j in range(2)]
        yb = [s.sb(f"yb{j}", [P, D]) for j in range(2)]
        ps_h = [s.ps(f"ps_h{j}", [P, CH]) for j in range(4)]
        ps_y = [s.ps(f"ps_y{j}", [P, CH]) for j in range(2)]
        w_in = [s.sem(f"w_in{j}") for j in range(2)]
        h_mm, h_ev, y_mm, y_ev, y_ad = (s.sem(n) for n in ("h_mm", "h_ev", "y_mm", "y_ev", "y_ad"))
        block = s.block()

        @block.sync
        def _(sp):
            for e in range(E):
                j = e % 2
                if e >= 2:
                    sp.wait_ge(y_ev, NT * (e - 1))
                sp.dma_start(w1[j][:, :, :], W1[e].rearrange("(t p) n -> p t n", p=P)).then_inc(w_in[j], 16)
                sp.dma_start(w2[j][:, :, :], W2[e].rearrange("(t p) n -> p t n", p=P)).then_inc(w_in[j], 16)
                sp.dma_start(b2s[j][:, :], b2[e:e + 1, :].to_broadcast([P, D])).then_inc(w_in[j], 16)

        @block.tensor
        def _(pe):
            def up(e, g, c0, j, first):
                for n in range(HT):
                    if not (first and n < 4):
                        pe.wait_ge(h_ev, HT * g + n - 3)
                    for d in range(DT):
                        last = nc.tensor.matmul(ps_h[n % 4][:, :], w1[e % 2][:, d, n * P:(n + 1) * P],
                                                xT[:, d, bass.ds(c0, CH)], start=(d == 0), stop=(d == DT - 1))
                    last.then_inc(h_mm, 1)

            def down(e, g, j, first):
                pe.wait_ge(h_ev, HT * (g + 1))
                for i in range(TC):
                    if not (first and i < 2):
                        pe.wait_ge(y_ev, TC * g + i - 1)
                    for n in range(HT):
                        last = nc.tensor.matmul(ps_y[i % 2][:, 0:D], hT[j][:, n, i * P:(i + 1) * P], w2[e % 2][:, n, :],
                                                start=(n == 0), stop=(n == HT - 1))
                    last.then_inc(y_mm, 1)

            for e in range(E):
                pe.wait_ge(w_in[e % 2], 48 * (e // 2 + 1))
                up(e, NC * e, 0, 0, e == 0)
                up(e, NC * e + 1, CH, 1, False)
                down(e, NC * e, 0, e == 0)
                with nc.tensor.Fori(1, NC // 2, 1) as m:
                    up(e, NC * e + 2 * m, 2 * m * CH, 0, False)
                    down(e, NC * e + 2 * m - 1, 1, False)
                    up(e, NC * e + 2 * m + 1, (2 * m + 1) * CH, 1, False)
                    down(e, NC * e + 2 * m, 0, False)
                down(e, NC * e + NC - 1, 1, False)

        @block.scalar
        def _(act):
            def relu(e, g, j, first):
                if not first:
                    act.wait_ge(y_mm, TC * (g - 1))
                for n in range(HT):
                    act.wait_ge(h_mm, HT * g + n + 1)
                    nc.scalar.activation(hT[j][:, n, :], ps_h[n % 4][:, :], ACT.Relu,
                                         bias=b1T[:, e * HT + n:e * HT + n + 1]).then_inc(h_ev, 1)

            for e in range(E):
                act.wait_ge(w_in[e % 2], 48 * (e // 2 + 1))
                relu(e, NC * e, 0, e == 0)
                relu(e, NC * e + 1, 1, e == 0)
                with nc.scalar.Fori(1, NC // 2, 1) as m:
                    for j in range(2):
                        relu(e, NC * e + 2 * m + j, j, False)

        @block.vector
        def _(dve):
            for e in range(E):
                dve.wait_ge(w_in[e % 2], 48 * (e // 2 + 1))
                with nc.vector.Fori(0, NT // 2, 1) as m:
                    for j in range(2):
                        t = 2 * m + j
                        dve.wait_ge(y_mm, NT * e + t + 1)
                        nc.vector.tensor_tensor(yb[j][:, :], ps_y[j][:, 0:D], b2s[e % 2][:, :], ALU.add).then_inc(y_ev, 1)
                        dve.wait_ge(y_ev, NT * e + t + 1)
                        tt = x_res[:, bass.ds(t, 1), :].rearrange("p a d -> p (a d)")
                        nc.vector.scalar_tensor_tensor(out=tt, in0=yb[j][:, :],
                                                       scalar=cw[:, bass.ds(t, 1), e:e + 1].rearrange("p a b -> p (a b)"),
                                                       in1=tt, op0=ALU.mult, op1=ALU.add).then_inc(y_ad, 1)


def store(nc, x_res, out):
    with Scope(nc, "so") as s:
        stored = s.sem("stored")
        ov = out.rearrange("b (t p) d -> p (b t) d", p=P)
        block = s.block()

        @block.sync
        def _(sp):
            for g in range(8):
                sp.dma_start(ov[:, 4 * g:4 * g + 4, :], x_res[:, 4 * g:4 * g + 4, :]).then_inc(stored, 16)
            sp.wait_ge(stored, 16 * 8)


def program(nc, w, out, stages=9):
    with Scope(nc, "main") as s:
        x_res = s.sb("x_res", [P, NT, D])
        mv, rstd = s.sb("mv", [P, NT, 2]), s.sb("rstd", [P, NT])
        stats = s.sb("stats", [P, NT, 6])
        ident = s.sb("ident", [P, P])
        ctxT = s.sb("ctxT", [P, 2, B * KV])
        load_and_stats(nc, w["x"], w["ctx_768"], x_res, stats, ident, ctxT)
        l0 = {"q": w["L0_xattn_w_q"], "k": w["L0_xattn_w_kv"][:, 0:INNER], "v": w["L0_xattn_w_kv"][:, INNER:2 * INNER],
              "o": w["L0_xattn_w_out"]}
        l1 = {k: w["L1_xattn_" + n] for k, n in (
            ("q", "Wq"), ("k", "Wk"), ("v", "Wv"), ("o", "Wo"), ("k_ipa", "Wk_ipa"), ("v_ipa", "Wv_ipa"),
            *((n, n) for n in ("q_down", "q_up", "q_alpha", "k_down", "k_up", "k_alpha",
                               "v_down", "v_up", "v_alpha", "o_down", "o_up", "o_alpha")))}

        def cross(layer, weights, groups, bias):
            with Scope(nc, f"c{layer}") as z:
                M = z.sb("M", [P, DT, B, INNER])
                VW = z.sb("VW", [P, B, NP, D])
                prepare_attention(nc, f"pa{layer}", weights, ctxT, ident, M, VW)
                rstd_of(nc, f"r{layer}", stats, mv, rstd)
                attention(nc, f"at{layer}", groups, bias, x_res, mv, rstd, stats, ident, M, VW)

        if stages >= 1:
            cross(0, l0, [(0, KV)], w["L0_xattn_b_out"])
        if stages >= 2:
            with Scope(nc, "f") as z:
                WgT, WuT = z.sb("WgT", [P, DT, FF]), z.sb("WuT", [P, DT, FF])
                WdT = z.sb("WdT", [P, FT, D])
                xqT = z.sb("xqT", [P, DT, T])
                scale_x = z.sb("scale_x", [P, 1])
                quantise_weights(nc, w["L0_ffn_w_gate"], w["L0_ffn_w_up"], w["L0_ffn_w_down"], WgT, WuT, WdT, ident)
                rstd_of(nc, "r2", stats, mv, rstd)
                quantise_input(nc, x_res, mv, rstd, scale_x, xqT, ident)
                gate = z.sb("gate", [P, NC * FT * CH])
                up_dram = nc.dram_tensor("up_scratch", (2 * NC, P, FT // 2 * CH), F32, kind="Internal").ap()
                gated_mlp(nc, x_res, stats, scale_x, xqT, WgT, WuT, WdT, up_dram, gate)
        if stages >= 3:
            cross(1, l1, [(0, KV - IPA), (KV - IPA, KV)], w["L1_xattn_bo"])
        if stages >= 4:
            with Scope(nc, "e") as z:
                xT = z.sb("xT", [P, DT, T])
                cw = z.sb("cw", [P, NT, E])
                b1T = z.sb("b1T", [P, E * HT])
                rstd_of(nc, "r4", stats, mv, rstd)
                route(nc, w["L1_ffn_Wr"], w["L1_ffn_br"], w["L1_ffn_b1"], b1T, x_res, mv, rstd, ident, xT, cw)
                experts(nc, w["L1_ffn_W1"], b1T, w["L1_ffn_W2"], w["L1_ffn_b2"], x_res, xT, cw)
        store(nc, x_res, out)


def kernel(**inputs):
    import numpy as np
    import concourse.bacc as bacc
    from concourse.bass_utils import run_bass_kernel_spmd

    nc = bacc.Bacc("TRN2", target_bir_lowering=False, num_devices=1)
    arrays, aps = {}, {}
    for name, a in inputs.items():
        a = np.ascontiguousarray(a)
        arrays[f"in_{name}"] = a
        aps[name] = nc.dram_tensor(f"in_{name}", a.shape, mybir.dt.from_np(a.dtype), kind="ExternalInput").ap()
    out = nc.dram_tensor("out_0", (B, S, D), F32, kind="ExternalOutput").ap()
    program(nc, aps, out)
    r = run_bass_kernel_spmd(nc, [arrays], core_ids=[0])
    return r.results[0]["out_0"]
```

```python
from contextlib import ExitStack

import concourse.bass as bass
from concourse import mybir

F32 = mybir.dt.float32
I16 = mybir.dt.int16
I32 = mybir.dt.int32
U16 = mybir.dt.uint16
U32 = mybir.dt.uint32
ALU = mybir.AluOpType
ACT = mybir.ActivationFunctionType
AX = mybir.AxisListType
RMAX = bass.bass_isa.ReduceOp.max

P = 128
B, S, D = 4, 1024, 256
T = B * S
NT = T // P
DT = D // P
KV, C = 64, 192
C1 = C - P
H, HD = 16, 64
INNER = H * HD
NP = INNER // P
IPA = 4
RANK = 32
FF, QB = 768, 32
FT = FF // P
CH = 512
NC = T // CH
E, HID = 8, 1024
HT = HID // P
CAP = T + P
ROW = D + 2
NTL = (2 * T + E * (P - 1)) // P + 1
NTL += NTL % 2
EPS = 1e-5
MAGIC = 12582912.0
QACT = 32767.0


class Scope:

    def __init__(self, nc, tag):
        self.nc, self.tag, self.ctx = nc, tag, ExitStack()

    def __enter__(self):
        self.ctx.__enter__()
        return self

    def __exit__(self, *a):
        return self.ctx.__exit__(*a)

    def sb(self, name, shape, dt=F32):
        return self.ctx.enter_context(self.nc.sbuf_tensor(f"{self.tag}_{name}", shape, dt))

    def ps(self, name, shape, dt=F32):
        return self.ctx.enter_context(self.nc.psum_tensor(f"{self.tag}_{name}", shape, dt))

    def sem(self, name):
        return self.ctx.enter_context(self.nc.semaphore(f"{self.tag}_{name}"))

    def block(self):
        return self.ctx.enter_context(self.nc.Block())


def load_and_stats(nc, x, ctx_in, x_res, stats, ident, ctxT):
    with Scope(nc, "ld") as s:
        crow = s.sb("crow", [P, 2, C])
        pT = s.ps("pT", [P, 4, P])
        xin, cin = s.sem("xin"), s.sem("cin")
        idz, idr, ctx_t = s.sem("idz"), s.sem("idr"), s.sem("ctx_t")
        xv = x.rearrange("b (t p) d -> p (b t) d", p=P)
        block = s.block()
        G = 4

        @block.sync
        def _(sp):
            sp.dma_start(crow[:, :, :], ctx_in.rearrange("(r b) k c -> (b k) r c", r=2)).then_inc(cin, 16)
            for g in range(NT // G):
                sp.dma_start(x_res[:, G * g:G * g + G, :], xv[:, G * g:G * g + G, :]).then_inc(xin, 16)
                sp.wait_ge(xin, 16 * (g + 1))

        @block.gpsimd
        def _(pool):
            nc.gpsimd.memset(ident[:, :], 0.0).then_inc(idz, 1)
            pool.wait_ge(idz, 1)
            nc.gpsimd.affine_select(out=ident[:, :], in_=ident[:, :], compare_op=ALU.not_equal, fill=1.0,
                                    base=0, pattern=[[-1, P]], channel_multiplier=1).then_inc(idr, 1)

        @block.tensor
        def _(pe):
            pe.wait_ge(idr, 1)
            pe.wait_ge(cin, 16)
            for r in range(2):
                nc.tensor.transpose(pT[:, 2 * r, :], crow[:, r, 0:P], ident[:, :])
                last = nc.tensor.transpose(pT[0:C1, 2 * r + 1, :], crow[:, r, P:C], ident[:, :])
            last.then_inc(ctx_t, 1)

        @block.vector
        def _(dve):
            dve.wait_ge(ctx_t, 1)
            for r in range(2):
                nc.vector.tensor_copy(ctxT[:, 0, r * P:(r + 1) * P], pT[:, 2 * r, :])
                nc.vector.tensor_copy(ctxT[0:C1, 1, r * P:(r + 1) * P], pT[0:C1, 2 * r + 1, :])
            for t in range(NT):
                if t % G == 0:
                    dve.wait_ge(xin, 16 * (t // G + 1))
                nc.vector.bn_stats(stats[:, t, :], x_res[:, t, :])


def prepare_attention(nc, tag, w, ctxT, ident, M, VW):
    lora = "q_down" in w
    RING = 6
    with Scope(nc, tag) as s:
        wq, wk, wv = (s.sb(n, [P, 2, INNER]) for n in ("wq", "wk", "wv"))
        wo = s.sb("wo", [P, NP, D])
        WqT = s.sb("WqT", [P, NP, D])
        Kd = s.sb("Kd", [P, NP, B, P])
        Vd = s.sb("Vd", [P, NP, B, P])
        if lora:
            wki, wvi = (s.sb(n, [P, 2, INNER]) for n in ("wki", "wvi"))
            down = s.sb("down", [P, 3, 2, RANK])
            odown = s.sb("odown", [P, NP, RANK])
            up = s.sb("up", [RANK, INNER])
            oup = s.sb("oup", [RANK, D])
            downT = s.sb("downT", [RANK, 4, P])
            odownT = s.sb("odownT", [RANK, NP, P])
            alpha = s.sb("alpha", [P, 4])
            alpha_r = s.sb("alpha_r", [P, 4])
            ups = {"q": up}
        ring = s.ps("ring", [P, RING, CH])
        loaded, up_in, made, moved, zero = (s.sem(n) for n in ("loaded", "up_in", "made", "moved", "zero"))
        used, alpha_s = s.sem("used"), s.sem("alpha_s")
        block = s.block()
        loads = [(wq[:, :, :], w["q"].rearrange("(t p) n -> p t n", p=P)),
                 (wo[:, :, :], w["o"].rearrange("(t p) n -> p t n", p=P))]
        for dst, key in ((wk, "k"), (wv, "v")) + (((wki, "k_ipa"), (wvi, "v_ipa")) if lora else ()):
            loads += [(dst[:, 0, :], w[key][0:P, :]), (dst[0:C1, 1, :], w[key][P:C, :])]
        if lora:
            loads += [(down[:, 0, :, :], w["q_down"].rearrange("(t p) r -> p t r", p=P))]
            for n, key in ((1, "k_down"), (2, "v_down")):
                loads += [(down[:, n, 0, :], w[key][0:P, :]), (down[0:C1, n, 1, :], w[key][P:C, :])]
            loads += [(odown[:, :, :], w["o_down"].rearrange("(t p) r -> p t r", p=P)), (oup[:, :], w["o_up"])]
            for n, key in enumerate(("q_alpha", "k_alpha", "v_alpha", "o_alpha")):
                loads += [(alpha[:, n:n + 1], w[key].unsqueeze(0).to_broadcast([P, 1]))]
        rows = {"q": (P, P), "k": (P, C1), "v": (P, C1)}

        @block.sync
        def _(sp):
            for dst, src in loads:
                sp.dma_start(dst, src).then_inc(loaded, 16)
            if lora:
                for n, key in enumerate(("q_up", "k_up", "v_up")):
                    if n:
                        sp.wait_ge(used, n)
                    sp.dma_start(up[:, :], w[key]).then_inc(up_in, 16)

        @block.gpsimd
        def _(pool):
            nc.gpsimd.memset(Kd[:, :, :, :], 0.0).then_inc(zero, 1)
            nc.gpsimd.memset(Vd[:, :, :, :], 0.0).then_inc(zero, 1)

        @block.tensor
        def _(pe):
            n = [0]

            def bank():
                if n[0] >= RING:
                    pe.wait_ge(moved, n[0] - RING + 1)
                n[0] += 1
                return (n[0] - 1) % RING

            pe.wait_ge(loaded, 16 * len(loads))
            if lora:
                for i in range(3):
                    b = bank()
                    for t in range(2):
                        m = rows["qkv"[i]][t]
                        last = nc.tensor.transpose(ring[0:RANK, b, t * P:t * P + m], down[0:m, i, t, :], ident[0:m, 0:m])
                    last.then_inc(made, 1)
                    pe.wait_ge(moved, n[0])
                    pe.wait_ge(up_in, 16 * (i + 1))
                    for t in range(2):
                        m = rows["qkv"[i]][t]
                        for c in range(2):
                            b = bank()
                            last = nc.tensor.matmul(ring[0:m, b, :], downT[:, t, 0:m], up[:, c * CH:(c + 1) * CH],
                                                    start=True, stop=True)
                            last.then_inc(made, 1)
                    pe.wait_ge(moved, n[0])
                    pe.sem_inc(used, 1)
                for g in range(2):
                    b = bank()
                    for t in range(4):
                        last = nc.tensor.transpose(ring[0:RANK, b, t * P:(t + 1) * P], odown[:, 4 * g + t, :], ident[:, :])
                    last.then_inc(made, 1)
                pe.wait_ge(moved, n[0])
                for g in range(4):
                    b = bank()
                    for t in range(2):
                        last = nc.tensor.matmul(ring[:, b, t * D:(t + 1) * D], odownT[:, 2 * g + t, :], oup[:, :],
                                                start=True, stop=True)
                    last.then_inc(made, 1)
                pe.wait_ge(moved, n[0])
            for g in range(NP // 2):
                b = bank()
                for i in range(2):
                    for t in range(2):
                        last = nc.tensor.transpose(ring[:, b, i * D + t * P:i * D + (t + 1) * P],
                                                   wq[:, t, (2 * g + i) * P:(2 * g + i + 1) * P], ident[:, :])
                last.then_inc(made, 1)
            for base, ipa in ((wk, wki if lora else None), (wv, wvi if lora else None)):
                for j in range(NP):
                    b = bank()
                    parts = [(base, 0, KV - IPA), (ipa, KV - IPA, KV)] if lora else [(base, 0, KV)]
                    for wt, lo, hi in parts:
                        for t in range(2):
                            m = (P, C1)[t]
                            last = nc.tensor.matmul(
                                ring[:, b, 0:B * KV].rearrange("p (b k) -> p b k", b=B)[:, :, lo:hi],
                                wt[0:m, t, j * P:(j + 1) * P],
                                ctxT[0:m, t, :].rearrange("p (b k) -> p b k", b=B)[:, :, lo:hi],
                                start=(t == 0), stop=(t == 1))
                    last.then_inc(made, 1)
            pe.wait_ge(moved, n[0])
            for j in range(NP):
                for t in range(DT):
                    b = bank()
                    nc.tensor.matmul(ring[:, b, :], WqT[:, j, t * P:(t + 1) * P], Kd[:, j, :, :],
                                     start=True, stop=True).then_inc(made, 1)
            for j in range(NP):
                for g in range(2):
                    b = bank()
                    for i in range(2):
                        last = nc.tensor.matmul(ring[:, b, i * D:(i + 1) * D], Vd[:, j, 2 * g + i, :], wo[:, j, :],
                                                start=True, stop=True)
                    last.then_inc(made, 1)

        @block.vector
        def _(dve):
            n = [0]

            def bank():
                n[0] += 1
                dve.wait_ge(made, n[0])
                return (n[0] - 1) % RING

            dve.wait_ge(loaded, 16 * len(loads))
            dve.wait_ge(zero, 2)
            if lora:
                nc.vector.tensor_scalar(alpha_r[:, :], alpha[:, :], 1.0 / RANK, None, ALU.mult).then_inc(alpha_s, 1)
                dve.wait_ge(alpha_s, 1)
                for i, wt in enumerate((wq, wk, wv)):
                    b = bank()
                    if i == 0:
                        nc.vector.tensor_copy(downT[:, 0:2, :], ring[0:RANK, b, 0:2 * P]).then_inc(moved, 1)
                    else:
                        nc.vector.tensor_copy(downT[:, 0:2, :].rearrange("r t p -> r (t p)")[:, 0:C],
                                              ring[0:RANK, b, 0:C]).then_inc(moved, 1)
                    for t in range(2):
                        m = rows["qkv"[i]][t]
                        for c in range(2):
                            b = bank()
                            part = wt[0:m, t, c * CH:(c + 1) * CH]
                            nc.vector.scalar_tensor_tensor(out=part, in0=ring[0:m, b, :], scalar=alpha_r[0:m, i:i + 1],
                                                           in1=part, op0=ALU.mult, op1=ALU.add).then_inc(moved, 1)
                for g in range(2):
                    b = bank()
                    nc.vector.tensor_copy(odownT[:, 4 * g:4 * g + 4, :], ring[0:RANK, b, :]).then_inc(moved, 1)
                for g in range(4):
                    b = bank()
                    part = wo[:, 2 * g:2 * g + 2, :]
                    nc.vector.scalar_tensor_tensor(out=part, in0=ring[:, b, :].rearrange("p (t n) -> p t n", t=2),
                                                   scalar=alpha_r[:, 3:4], in1=part,
                                                   op0=ALU.mult, op1=ALU.add).then_inc(moved, 1)
            for g in range(NP // 2):
                b = bank()
                nc.vector.tensor_copy(WqT[:, 2 * g:2 * g + 2, :], ring[:, b, :]).then_inc(moved, 1)
            for dst in (Kd, Vd):
                for j in range(NP):
                    b = bank()
                    for h in range(2):
                        last = nc.vector.tensor_copy(dst[h * HD:(h + 1) * HD, j, :, h * KV:(h + 1) * KV],
                                                     ring[h * HD:(h + 1) * HD, b, 0:B * KV].rearrange("p (b k) -> p b k", b=B))
                    last.then_inc(moved, 1)
            for j in range(NP):
                for t in range(DT):
                    b = bank()
                    nc.vector.tensor_scalar(M[:, t, :, j * P:(j + 1) * P],
                                            ring[:, b, :].rearrange("p (b k) -> p b k", b=B),
                                            HD ** -0.5, None, ALU.mult).then_inc(moved, 1)
            for j in range(NP):
                for g in range(2):
                    b = bank()
                    nc.vector.tensor_copy(VW[:, 2 * g:2 * g + 2, j, :],
                                          ring[:, b, :].rearrange("p (b n) -> p b n", b=2)).then_inc(moved, 1)


def rstd_of(nc, tag, stats, mv, rstd):
    with Scope(nc, tag) as s:
        ve, sd = s.sb("ve", [P, NT]), s.sb("sd", [P, NT])
        m, a, b = s.sem("m"), s.sem("a"), s.sem("b")
        block = s.block()

        @block.vector
        def _(dve):
            for t in range(NT):
                last = nc.vector.bn_aggr(mv[:, t, :], stats[:, t, :])
            last.then_inc(m, 1)
            dve.wait_ge(m, 1)
            nc.vector.tensor_scalar(ve[:, :], mv[:, :, 1], EPS, None, ALU.add).then_inc(a, 1)
            dve.wait_ge(b, 1)
            nc.vector.reciprocal(rstd[:, :], sd[:, :])

        @block.scalar
        def _(act):
            act.wait_ge(a, 1)
            nc.scalar.activation(sd[:, :], ve[:, :], ACT.Sqrt).then_inc(b, 1)


def attention(nc, tag, groups, bias_in, x_res, mv, rstd, stats, ident, M, VW):
    NG = len(groups)
    with Scope(nc, tag) as s:
        xn = s.sb("xn", [P, 2, D])
        xnT = [s.sb(f"xnT{j}", [P, DT, P]) for j in range(2)]
        sc = [s.sb(f"sc{j}", [P, H, KV]) for j in range(2)]
        mx = s.sb("mx", [P, 2, H, NG])
        sm = s.sb("sm", [P, 2, H, NG])
        ri = s.sb("ri", [P, 2, H, NG])
        pT = [s.sb(f"pT{j}", [P, NP, P]) for j in range(2)]
        bias = s.sb("bias", [P, D])
        new = [s.sb(f"new{j}", [P, D]) for j in range(2)]
        st = [s.sb(f"st{j}", [P, 6]) for j in range(2)]
        ps_xT = s.ps("ps_xT", [P, DT, P])
        ps_s = [s.ps(f"ps_s{j}", [P, INNER]) for j in range(2)]
        ps_p = s.ps("ps_p", [P, NP, P])
        ps_y = s.ps("ps_y", [P, D])
        names = ("bias_in", "xn_r", "xb_r", "xT_r", "xnT_r", "sc_r", "mx_r", "sub_r", "exp_r", "sum_r", "ri_r",
                 "prob_r", "pT_r", "pTs_r", "y_r", "res_r", "st_r", "new_c")
        (bias_s, xn_r, xb_r, xT_r, xnT_r, sc_r, mx_r, sub_r, exp_r, sum_r, ri_r,
         prob_r, pT_r, pTs_r, y_r, res_r, st_r, new_c) = (s.sem(n) for n in names)
        block = s.block()

        def steps(eng, step):
            step(0, 0, 2, True)
            step(1, 1, 2, True)
            with eng.Fori(1, NT // 2 - 1, 1) as i:
                for j in range(2):
                    step(2 * i + j, j, 2, False)
            step(NT - 2, 0, 1, False)
            step(NT - 1, 1, 0, False)

        def tile(buf, t):
            return buf[:, bass.ds(t, 1), :].rearrange("p o d -> p (o d)")

        @block.sync
        def _(sp):
            sp.dma_start(bias[:, :], bias_in.unsqueeze(0).to_broadcast([P, D])).then_inc(bias_s, 16)

        @block.tensor
        def _(pe):
            def turn_x(t, j, first):
                pe.wait_ge(xn_r, t + 1)
                if not first:
                    pe.wait_ge(xnT_r, t)
                for d in range(DT):
                    last = nc.tensor.transpose(ps_xT[:, d, :], xn[:, j, d * P:(d + 1) * P], ident[:, :])
                last.then_inc(xT_r, 1)

            def scores(t, j, first):
                pe.wait_ge(xnT_r, t + 1)
                if not first:
                    pe.wait_ge(sub_r, t - 1)
                off = t // (NT // B) * INNER
                for c in range(2):
                    for d in range(DT):
                        last = nc.tensor.matmul(ps_s[j][:, c * CH:(c + 1) * CH], xnT[j][:, d, :],
                                                M[:, d, :, :].rearrange("p b n -> p (b n)")[:, bass.ds(off + c * CH, CH)],
                                                start=(d == 0), stop=(d == DT - 1))
                last.then_inc(sc_r, 1)

            def turn_probs(t, j, first):
                pe.wait_ge(prob_r, t + 1)
                if not first:
                    pe.wait_ge(pTs_r, 2 * t)
                for g in range(2):
                    for i in range(4):
                        n = 4 * g + i
                        last = nc.tensor.transpose(ps_p[:, n, :], sc[j][:, 2 * n:2 * n + 2, :], ident[:, :])
                    last.then_inc(pT_r, 1)

            def output(t, j, first):
                if not first:
                    pe.wait_ge(res_r, t)
                off = t // (NT // B) * (NP * D)
                vw = VW[:, :, :, :].rearrange("p b j n -> p (b j n)")
                for n in range(NP):
                    if n % 4 == 0:
                        pe.wait_ge(pTs_r, 2 * t + n // 4 + 1)
                    last = nc.tensor.matmul(ps_y[:, :], pT[j][:, n, :], vw[:, bass.ds(off + n * D, D)],
                                            start=(n == 0), stop=(n == NP - 1))
                last.then_inc(y_r, 1)

            def step(k, j, more, head):
                if more >= 1:
                    scores(k + 1, 1 - j, head and k == 0)
                turn_probs(k, j, head and k == 0)
                if more >= 2:
                    turn_x(k + 2, j, False)
                output(k, j, head and k == 0)

            turn_x(0, 0, True)
            turn_x(1, 1, False)
            scores(0, 0, True)
            steps(nc.tensor, step)

        @block.scalar
        def _(act):
            def copy_xT(t, j, first):
                act.wait_ge(xT_r, t + 1)
                if not first:
                    act.wait_ge(sc_r, t - 1)
                nc.scalar.copy(xnT[j][:, :, :], ps_xT[:, :, :]).then_inc(xnT_r, 1)

            def copy_pT(t, j, first):
                if not first:
                    act.wait_ge(y_r, t - 1)
                for g in range(2):
                    act.wait_ge(pT_r, 2 * t + g + 1)
                    nc.scalar.copy(pT[j][:, 4 * g:4 * g + 4, :], ps_p[:, 4 * g:4 * g + 4, :]).then_inc(pTs_r, 1)

            def exps(t, j):
                act.wait_ge(sub_r, t + 1)
                nc.scalar.activation(sc[j][:, :, :], sc[j][:, :, :], ACT.Exp).then_inc(exp_r, 1)

            def keep(t, j):
                act.wait_ge(res_r, t + 1)
                nc.scalar.copy(tile(x_res, t), new[j][:, :]).then_inc(new_c, 1)

            def step(k, j, more, head):
                if not (head and k == 0):
                    keep(k - 1, 1 - j)
                copy_pT(k, j, head)
                if more >= 2:
                    copy_xT(k + 2, j, False)
                if more >= 1:
                    exps(k + 1, 1 - j)

            copy_xT(0, 0, True)
            copy_xT(1, 1, True)
            exps(0, 0)
            steps(nc.scalar, step)
            keep(NT - 1, 1)

        @block.vector
        def _(dve):
            def norm(t, j, first):
                if not first:
                    dve.wait_ge(xT_r, t - 1)
                tt = tile(x_res, t)
                nc.vector.tensor_scalar(xn[:, j, :], tt, mv[:, bass.ds(t, 1), 0:1].rearrange("p a b -> p (a b)"),
                                        rstd[:, bass.ds(t, 1)], ALU.subtract, ALU.mult).then_inc(xn_r, 1)
                nc.vector.tensor_tensor(tt, tt, bias[:, :], ALU.add).then_inc(xb_r, 1)

            def softmax_in(t, j, first):
                dve.wait_ge(sc_r, t + 1)
                scv = ps_s[j][:, :].rearrange("p (h k) -> p h k", h=H)
                for g, (lo, hi) in enumerate(groups):
                    last = nc.vector.tensor_reduce(mx[:, j, :, g], scv[:, :, lo:hi], AX.X, ALU.max)
                last.then_inc(mx_r, 1)
                dve.wait_ge(mx_r, t + 1)
                if not first:
                    dve.wait_ge(pT_r, 2 * (t - 1))
                for g, (lo, hi) in enumerate(groups):
                    last = nc.vector.tensor_tensor(sc[j][:, :, lo:hi], scv[:, :, lo:hi],
                                                   mx[:, j, :, g].unsqueeze(2).to_broadcast([P, H, hi - lo]),
                                                   ALU.subtract)
                last.then_inc(sub_r, 1)

            def sums(t, j, first):
                dve.wait_ge(exp_r, t + 1)
                for g, (lo, hi) in enumerate(groups):
                    last = nc.vector.tensor_reduce(sm[:, j, :, g], sc[j][:, :, lo:hi], AX.X, ALU.add)
                last.then_inc(sum_r, 1)
                dve.wait_ge(sum_r, t + 1)
                if not first:
                    dve.wait_ge(prob_r, t - 1)
                nc.vector.reciprocal(ri[:, j, :, :], sm[:, j, :, :]).then_inc(ri_r, 1)

            def residual(t, j, first):
                dve.wait_ge(y_r, t + 1)
                dve.wait_ge(xb_r, t + 1)
                if not first:
                    dve.wait_ge(new_c, t - 1)
                nc.vector.tensor_tensor(new[j][:, :], ps_y[:, :], tile(x_res, t), ALU.add).then_inc(res_r, 1)
                dve.wait_ge(res_r, t + 1)
                nc.vector.bn_stats(st[j][:, :], new[j][:, :]).then_inc(st_r, 1)
                dve.wait_ge(st_r, t + 1)
                nc.vector.tensor_copy(tile(stats, t), st[j][:, :])

            def step(k, j, more, head):
                if more >= 2:
                    norm(k + 2, j, False)
                if more >= 1:
                    softmax_in(k + 1, 1 - j, head and k == 0)
                    sums(k + 1, 1 - j, head and k == 0)
                residual(k, j, head)

            dve.wait_ge(bias_s, 16)
            norm(0, 0, True)
            norm(1, 1, True)
            softmax_in(0, 0, True)
            sums(0, 0, True)
            steps(nc.vector, step)

        @block.gpsimd
        def _(pool):
            def step(k, j, more, head):
                pool.wait_ge(ri_r, k + 1)
                for g, (lo, hi) in enumerate(groups):
                    part = sc[j][:, :, lo:hi]
                    last = nc.gpsimd.tensor_tensor(part, part, ri[:, j, :, g].unsqueeze(2).to_broadcast([P, H, hi - lo]),
                                                   ALU.mult)
                last.then_inc(prob_r, 1)

            steps(nc.gpsimd, step)


def quantise_weights(nc, w_gate, w_up, w_down, WgT, WuT, WdT, ident):
    NB = FF * D // (P * QB)
    with Scope(nc, "qw") as s:
        w = [s.sb(f"w{i}", [P, NB, QB]) for i in range(3)]
        am, sc, rs = s.sb("am", [P, NB]), s.sb("sc", [P, NB]), s.sb("rs", [P, NB])
        ring = s.ps("ring", [P, 4, CH])
        loaded = [s.sem(f"loaded{i}") for i in range(3)]
        c, ready, made, moved = s.sem("c"), s.sem("ready"), s.sem("made"), s.sem("moved")
        block = s.block()

        @block.sync
        def _(sp):
            for i, src in enumerate((w_gate, w_up, w_down)):
                sp.dma_start(w[i][:, :, :].rearrange("p (o b) q -> p o (b q)", o=src.shape[0] // P),
                             src.rearrange("(o p) i -> p o i", p=P)).then_inc(loaded[i], 16)

        @block.vector
        def _(dve):
            n = [0]

            def then(ins):
                n[0] += 1
                ins.then_inc(c, 1)
                dve.wait_ge(c, n[0])

            for i in range(3):
                dve.wait_ge(loaded[i], 16)
                wi, per = w[i][:, :, :], [P, NB, QB]
                then(nc.vector.tensor_reduce(am[:, :], wi, AX.X, ALU.max, apply_absolute_value=True))
                then(nc.vector.tensor_scalar(sc[:, :], am[:, :], 1.0 / 7.0, 1e-12, ALU.mult, ALU.max))
                then(nc.vector.reciprocal(rs[:, :], sc[:, :]))
                then(nc.vector.tensor_tensor(wi, wi, rs[:, :].unsqueeze(2).to_broadcast(per), ALU.mult))
                then(nc.vector.tensor_scalar(wi, wi, MAGIC, MAGIC, ALU.add, ALU.subtract))
                then(nc.vector.tensor_scalar(wi, wi, 7.0, -8.0, ALU.min, ALU.max))
                nc.vector.tensor_tensor(wi, wi, sc[:, :].unsqueeze(2).to_broadcast(per), ALU.mult).then_inc(ready, 1)
            m = 0
            for i, dst in enumerate((WgT, WuT)):
                for g in range(3):
                    m += 1
                    dve.wait_ge(made, m)
                    nc.vector.tensor_copy(dst[:, :, 2 * g * P:(2 * g + 2) * P],
                                          ring[:, (m - 1) % 4, :].rearrange("p (d n) -> p d n", d=DT)).then_inc(moved, 1)
            for g in range(3):
                m += 1
                dve.wait_ge(made, m)
                nc.vector.tensor_copy(WdT[:, 2 * g:2 * g + 2, :], ring[:, (m - 1) % 4, :]).then_inc(moved, 1)

        @block.tensor
        def _(pe):
            m = 0
            for i in range(3):
                pe.wait_ge(ready, i + 1)
                src = w[i][:, :, :].rearrange("p (o b) q -> p o (b q)", o=DT if i == 2 else FT)
                for g in range(3):
                    if m >= 4:
                        pe.wait_ge(moved, m - 3)
                    for a in range(2):
                        for b in range(2):
                            if i < 2:
                                blk = src[:, 2 * g + b, a * P:(a + 1) * P]
                            else:
                                blk = src[:, b, (2 * g + a) * P:(2 * g + a + 1) * P]
                            last = nc.tensor.transpose(ring[:, m % 4, (2 * a + b) * P:(2 * a + b + 1) * P], blk, ident[:, :])
                    last.then_inc(made, 1)
                    m += 1


def quantise_input(nc, x_res, mv, rstd, scale_x, xqT, ident):
    with Scope(nc, "qx") as s:
        xn = s.sb("xn", [P, NT, D])
        q = s.sb("q", [P, 2, D])
        am, gm, inv = s.sb("am", [P, 1]), s.sb("gm", [P, 1]), s.sb("inv", [P, 1])
        ps = [s.ps(f"ps{j}", [P, 512]) for j in range(2)]
        c, am_r, gm_r, q_r, t_r, e_r = (s.sem(n) for n in ("c", "am_r", "gm_r", "q_r", "t_r", "e_r"))
        block = s.block()

        @block.vector
        def _(dve):
            for t in range(NT):
                last = nc.vector.tensor_scalar(xn[:, t, :], x_res[:, t, :], mv[:, t, 0:1], rstd[:, t:t + 1],
                                               ALU.subtract, ALU.mult)
            last.then_inc(c, 1)
            dve.wait_ge(c, 1)
            nc.vector.tensor_reduce(am[:, :], xn[:, :, :], AX.XY, ALU.max, apply_absolute_value=True).then_inc(am_r, 1)
            dve.wait_ge(gm_r, 1)
            nc.vector.tensor_scalar(scale_x[:, :], gm[:, :], 1.0 / QACT, 1e-12, ALU.mult, ALU.max).then_inc(c, 1)
            dve.wait_ge(c, 2)
            nc.vector.reciprocal(inv[:, :], scale_x[:, :]).then_inc(c, 1)
            dve.wait_ge(c, 3)
            for j in range(2):
                nc.vector.tensor_scalar(q[:, j, :], xn[:, j, :], inv[:, 0:1], MAGIC, ALU.mult, ALU.add).then_inc(q_r, 1)
            with nc.vector.Fori(1, NT // 2, 1) as i:
                for j in range(2):
                    dve.wait_ge(t_r, 2 * i + j - 1)
                    nc.vector.tensor_scalar(q[:, j, :], xn[:, bass.ds(2 * i + j, 1), :].rearrange("p a d -> p (a d)"),
                                            inv[:, 0:1], MAGIC, ALU.mult, ALU.add).then_inc(q_r, 1)

        @block.gpsimd
        def _(pool):
            pool.wait_ge(am_r, 1)
            nc.gpsimd.partition_all_reduce(gm[:, :], am[:, :], P, RMAX).then_inc(gm_r, 1)

        @block.tensor
        def _(pe):
            def turn(t, j):
                pe.wait_ge(q_r, t + 1)
                for d in range(DT):
                    last = nc.tensor.transpose(ps[j][:, d * P:(d + 1) * P], q[:, j, d * P:(d + 1) * P], ident[:, :])
                last.then_inc(t_r, 1)

            turn(0, 0)
            turn(1, 1)
            with nc.tensor.Fori(1, NT // 2, 1) as i:
                for j in range(2):
                    pe.wait_ge(e_r, 2 * i + j - 1)
                    turn(2 * i + j, j)

        @block.scalar
        def _(act):
            with nc.scalar.Fori(0, NT // 2, 1) as i:
                for j in range(2):
                    act.wait_ge(t_r, 2 * i + j + 1)
                    nc.scalar.activation(xqT[:, :, bass.ds((2 * i + j) * P, P)],
                                         ps[j][:, 0:D].rearrange("p (d n) -> p d n", d=DT), ACT.Copy,
                                         bias=-MAGIC).then_inc(e_r, 1)


def gated_mlp(nc, x_res, stats, scale_x, xqT, WgT, WuT, WdT, up_dram, gate):
    HF = FT // 2
    U = HF * CH
    NU = 2 * NC

    with Scope(nc, "gm") as s:
        gmax, umax, pmax = s.sb("gmax", [P, NC]), s.sb("umax", [P, NU]), s.sb("pmax", [P, NU])
        red = s.sb("red", [P, 3])
        allr = s.sb("allr", [P, 3])
        sc = s.sb("sc", [P, 8])
        SG, SU, SP, IU, IP, IG = range(6)
        stg = [s.sb(f"stg{j}", [P, U]) for j in range(2)]
        gq = [s.sb(f"gq{j}", [P, U], I16) for j in range(2)]
        sq = [s.sb(f"sq{j}", [P, U], U16) for j in range(2)]
        uq = [x[:, :].bitcast(I16) for x in sq]
        bank = [s.ps(f"bank{i}", [P, CH]) for i in range(FT)]
        with Scope(nc, "gu") as z:
            g_mm, g_ev, gm_s, c = z.sem("g_mm"), z.sem("g_ev"), z.sem("gm_s"), z.sem("c")
            u_mm, u_ev, u_red = z.sem("u_mm"), z.sem("u_ev"), z.sem("u_red")
            u_st = [z.sem(f"u_st{h}") for h in range(2)]
            gq_r, sig_r, sq_r, pr_r = z.sem("gq_r"), z.sem("sig_r"), z.sem("sq_r"), z.sem("pr_r")
            gred, gall, sg_r, pm_s = z.sem("gred"), z.sem("gall"), z.sem("sg_r"), z.sem("pm_s")
            block = z.block()

            def unit(u):
                return gate[:, bass.ds(u * U, U)]

            @block.tensor
            def _(pe):
                def half(w, h, c0, mm):
                    for i in range(HF):
                        o = h * HF + i
                        for d in range(DT):
                            last = nc.tensor.matmul(bank[o][:, :], w[:, d, o * P:(o + 1) * P],
                                                    xqT[:, d, bass.ds(c0, CH)], start=(d == 0), stop=(d == DT - 1))
                        last.then_inc(mm, 1)

                for h in range(2):
                    half(WgT, h, 0, g_mm)
                with nc.tensor.Fori(1, NC, 1) as k:
                    for h in range(2):
                        pe.wait_ge(g_ev, FT * (k - 1) + HF * (h + 1))
                        half(WgT, h, k * CH, g_mm)
                for h in range(2):
                    pe.wait_ge(g_ev, FT * (NC - 1) + HF * (h + 1))
                    half(WuT, h, 0, u_mm)
                with nc.tensor.Fori(1, NC, 1) as k:
                    for h in range(2):
                        pe.wait_ge(u_ev, FT * (k - 1) + HF * (h + 1))
                        half(WuT, h, k * CH, u_mm)

            @block.scalar
            def _(act):
                with nc.scalar.Fori(0, NC, 1) as k:
                    for o in range(FT):
                        act.wait_ge(g_mm, FT * k + o + 1)
                        nc.scalar.activation(gate[:, bass.ds((FT * k + o) * CH, CH)], bank[o][:, :], ACT.Copy,
                                             scale=scale_x[:, 0:1]).then_inc(g_ev, 1)

                def up_half(k, h, first):
                    if not first:
                        act.wait_ge(u_st[h], 16 * k)
                        act.wait_ge(u_red, 2 * k + h - 1)
                    for i in range(HF):
                        act.wait_ge(u_mm, FT * k + h * HF + i + 1)
                        nc.scalar.activation(stg[h][:, i * CH:(i + 1) * CH], bank[h * HF + i][:, :], ACT.Copy,
                                             scale=scale_x[:, 0:1]).then_inc(u_ev, 1)

                def sigmoid(u, h):
                    act.wait_ge(gq_r, u + 1)
                    nc.scalar.activation(unit(u), gq[h][:, :], ACT.Sigmoid, scale=sc[:, SG:SG + 1]).then_inc(sig_r, 1)

                act.wait_ge(sg_r, 2)
                for h in range(2):
                    up_half(0, h, True)
                    sigmoid(h, h)
                with nc.scalar.Fori(1, NC, 1) as k:
                    for h in range(2):
                        up_half(k, h, False)
                        sigmoid(2 * k + h, h)

            @block.vector
            def _(dve):
                with nc.vector.Fori(0, NC, 1) as k:
                    dve.wait_ge(g_ev, FT * (k + 1))
                    nc.vector.tensor_reduce(gmax[:, bass.ds(k, 1)], gate[:, bass.ds(k * FT * CH, FT * CH)], AX.X, ALU.max,
                                            apply_absolute_value=True).then_inc(gm_s, 1)
                dve.wait_ge(gm_s, NC)
                nc.vector.tensor_reduce(red[:, 0:1], gmax[:, :], AX.X, ALU.max).then_inc(gred, 1)
                dve.wait_ge(gall, 1)
                nc.vector.tensor_scalar(sc[:, SG:SG + 1], allr[:, 0:1], 1.0 / QACT, 1e-12, ALU.mult, ALU.max).then_inc(sg_r, 1)
                dve.wait_ge(sg_r, 1)
                nc.vector.reciprocal(sc[:, IG:IG + 1], sc[:, SG:SG + 1]).then_inc(sg_r, 1)
                dve.wait_ge(sg_r, 2)

                def levels(u, h):
                    nc.vector.tensor_scalar(gq[h][:, :], unit(u), sc[:, IG:IG + 1], None, ALU.mult).then_inc(gq_r, 1)

                def sig_levels(u, h):
                    dve.wait_ge(sig_r, u + 1)
                    nc.vector.tensor_scalar(sq[h][:, :], unit(u), 65536.0, 65535.0, ALU.mult, ALU.min).then_inc(sq_r, 1)
                    dve.wait_ge(sq_r, u + 1)
                    nc.vector.tensor_tensor(unit(u), gq[h][:, :], sq[h][:, :], ALU.mult).then_inc(pr_r, 1)

                def up_max(k, h):
                    dve.wait_ge(u_ev, FT * k + HF * (h + 1))
                    nc.vector.tensor_reduce(umax[:, bass.ds(2 * k + h, 1)], stg[h][:, :], AX.X, ALU.max,
                                            apply_absolute_value=True).then_inc(u_red, 1)

                def prod_max(u):
                    dve.wait_ge(pr_r, u + 1)
                    nc.vector.tensor_reduce(pmax[:, bass.ds(u, 1)], unit(u), AX.X, ALU.max,
                                            apply_absolute_value=True).then_inc(pm_s, 1)

                levels(0, 0)
                levels(1, 1)
                up_max(0, 0)
                sig_levels(0, 0)
                up_max(0, 1)
                sig_levels(1, 1)
                with nc.vector.Fori(1, NC, 1) as k:
                    for h in range(2):
                        levels(2 * k + h, h)
                        up_max(k, h)
                        prod_max(2 * k + h - 2)
                        sig_levels(2 * k + h, h)
                for u in (NU - 2, NU - 1):
                    prod_max(u)
                dve.wait_ge(pm_s, NU)
                dve.wait_ge(u_red, NU)
                nc.vector.tensor_reduce(red[:, 1:2], umax[:, :], AX.X, ALU.max)
                nc.vector.tensor_reduce(red[:, 2:3], pmax[:, :], AX.X, ALU.max).then_inc(gred, 1)
                dve.wait_ge(gall, 2)
                nc.vector.tensor_scalar(sc[:, SU:SU + 1], allr[:, 1:2], 1.0 / QACT, 1e-12, ALU.mult, ALU.max)
                nc.vector.tensor_scalar(sc[:, SP:SP + 1], allr[:, 2:3], sc[:, SG:SG + 1], 1.0 / (65536.0 * QACT),
                                        ALU.mult, ALU.mult).then_inc(c, 1)
                dve.wait_ge(c, 1)
                nc.vector.tensor_scalar(sc[:, SP:SP + 1], sc[:, SP:SP + 1], 1e-12, None, ALU.max).then_inc(c, 1)
                dve.wait_ge(c, 2)
                nc.vector.reciprocal(sc[:, IU:IU + 1], sc[:, SU:SU + 1])
                nc.vector.reciprocal(sc[:, IP:IP + 1], sc[:, SP:SP + 1]).then_inc(c, 1)
                dve.wait_ge(c, 3)
                nc.vector.tensor_scalar(sc[:, IP:IP + 1], sc[:, IP:IP + 1], sc[:, SG:SG + 1], 1.0 / 65536.0,
                                        ALU.mult, ALU.mult)

            @block.gpsimd
            def _(pool):
                pool.wait_ge(gred, 1)
                nc.gpsimd.partition_all_reduce(allr[:, 0:1], red[:, 0:1], P, RMAX).then_inc(gall, 1)
                pool.wait_ge(gred, 2)
                nc.gpsimd.partition_all_reduce(allr[:, 1:3], red[:, 1:3], P, RMAX).then_inc(gall, 1)

            @block.sync
            def _(sp):
                with nc.sync.Fori(0, NC, 1) as k:
                    for h in range(2):
                        sp.wait_ge(u_ev, FT * k + HF * (h + 1))
                        sp.dma_start(up_dram[bass.ds(2 * k + h, 1), :, :].rearrange("a p n -> (a p) n"),
                                     stg[h][:, :]).then_inc(u_st[h], 16)
                for h in range(2):
                    sp.wait_ge(u_st[h], 16 * NC)

        with Scope(nc, "go") as z:
            ld = [z.sem(f"ld{j}") for j in range(2)]
            uq_r, gq_r, o_r, om_s, gred, gall, c = (z.sem(n) for n in ("uq_r", "gq_r", "o_r", "om_s", "gred", "gall", "c"))
            block = z.block()

            @block.sync
            def _(sp):
                for h in range(2):
                    sp.dma_start(stg[h][:, :], up_dram[h, :, :]).then_inc(ld[h], 16)
                with nc.sync.Fori(1, NC, 1) as k:
                    for h in range(2):
                        sp.wait_ge(uq_r, 2 * k + h - 1)
                        sp.dma_start(stg[h][:, :], up_dram[bass.ds(2 * k + h, 1), :, :].rearrange("a p n -> (a p) n")
                                     ).then_inc(ld[h], 16)

            @block.vector
            def _(dve):
                def quant(k, h):
                    u = 2 * k + h
                    nc.vector.tensor_scalar(gq[h][:, :], unit(u), sc[:, IP:IP + 1], None, ALU.mult)
                    dve.wait_ge(ld[h], 16 * (k + 1))
                    nc.vector.tensor_scalar(uq[h], stg[h][:, :],
                                            sc[:, IU:IU + 1], None, ALU.mult).then_inc(uq_r, 1)
                    dve.wait_ge(uq_r, u + 1)
                    nc.vector.tensor_tensor(unit(u), gq[h][:, :], uq[h], ALU.mult).then_inc(o_r, 1)

                def o_max(u):
                    dve.wait_ge(o_r, u + 1)
                    nc.vector.tensor_reduce(pmax[:, bass.ds(u, 1)], unit(u), AX.X, ALU.max,
                                            apply_absolute_value=True).then_inc(om_s, 1)

                quant(0, 0)
                quant(0, 1)
                with nc.vector.Fori(1, NC, 1) as k:
                    for h in range(2):
                        quant(k, h)
                        o_max(2 * k + h - 2)
                for u in (NU - 2, NU - 1):
                    o_max(u)
                dve.wait_ge(om_s, NU)
                nc.vector.tensor_reduce(red[:, 0:1], pmax[:, :], AX.X, ALU.max).then_inc(gred, 1)
                dve.wait_ge(gall, 1)
                nc.vector.tensor_scalar(sc[:, 6:7], sc[:, SU:SU + 1], sc[:, SP:SP + 1], None, ALU.mult).then_inc(c, 1)
                dve.wait_ge(c, 1)
                nc.vector.tensor_scalar(sc[:, 7:8], allr[:, 0:1], sc[:, 6:7], 1.0 / QACT, ALU.mult, ALU.mult).then_inc(c, 1)
                dve.wait_ge(c, 2)
                nc.vector.tensor_scalar(sc[:, 7:8], sc[:, 7:8], 1e-12, None, ALU.max).then_inc(c, 1)
                dve.wait_ge(c, 3)
                nc.vector.reciprocal(sc[:, IG:IG + 1], sc[:, 7:8]).then_inc(c, 1)
                dve.wait_ge(c, 4)
                nc.vector.tensor_scalar(sc[:, IG:IG + 1], sc[:, IG:IG + 1], sc[:, 6:7], None, ALU.mult)

            @block.gpsimd
            def _(pool):
                pool.wait_ge(gred, 1)
                nc.gpsimd.partition_all_reduce(allr[:, 0:1], red[:, 0:1], P, RMAX).then_inc(gall, 1)

        with Scope(nc, "gd") as z:
            o_mg, o_lv, mm, ev, st_r = (z.sem(n) for n in ("o_mg", "o_lv", "mm", "ev", "st_r"))
            new_c = z.sem("new_c")
            new = [x[:, 0:D] for x in stg]
            st = [z.sb(f"st{j}", [P, 6]) for j in range(2)]
            lv = [xqT[:, j, 0:FT * CH].rearrange("p (o n) -> p o n", o=FT) for j in range(DT)]
            block = z.block()
            TC = CH // P

            def tile(buf, t):
                return buf[:, bass.ds(t, 1), :].rearrange("p a d -> p (a d)")

            @block.scalar
            def _(act):
                with nc.scalar.Fori(0, NT // 2, 1) as i:
                    for j in range(2):
                        act.wait_ge(ev, 2 * i + j + 1)
                        nc.scalar.copy(tile(x_res, 2 * i + j), new[j]).then_inc(new_c, 1)

            @block.vector
            def _(dve):
                def levels(k, j, first):
                    if not first:
                        dve.wait_ge(mm, TC * (k - 1))
                    nc.vector.tensor_scalar(lv[j], gate[:, bass.ds(k * FT * CH, FT * CH)].rearrange("p (o n) -> p o n", o=FT),
                                            sc[:, IG:IG + 1], MAGIC, ALU.mult, ALU.add).then_inc(o_mg, 1)
                    dve.wait_ge(o_mg, k + 1)
                    nc.vector.tensor_scalar(lv[j], lv[j], MAGIC, None, ALU.subtract).then_inc(o_lv, 1)

                def residual(k, i, first=False):
                    t, j = TC * k + i, i % 2
                    dve.wait_ge(mm, t + 1)
                    if not (first and i < 2):
                        dve.wait_ge(new_c, t - 1)
                    nc.vector.scalar_tensor_tensor(out=new[j], in0=bank[j][:, 0:D], scalar=sc[:, 7:8],
                                                   in1=tile(x_res, t), op0=ALU.mult, op1=ALU.add).then_inc(ev, 1)
                    dve.wait_ge(ev, t + 1)
                    nc.vector.bn_stats(st[j][:, :], new[j]).then_inc(st_r, 1)
                    dve.wait_ge(st_r, t + 1)
                    nc.vector.tensor_copy(tile(stats, t), st[j][:, :])

                levels(0, 0, True)
                levels(1, 1, True)
                for i in range(TC):
                    residual(0, i, True)
                levels(2, 0, False)
                for i in range(TC):
                    residual(1, i)
                with nc.vector.Fori(1, NC // 2 - 1, 1) as m:
                    for j in range(2):
                        levels(2 * m + j + 1, 1 - j, False)
                        for i in range(TC):
                            residual(2 * m + j, i)
                levels(NC - 1, 1, False)
                for j in range(2):
                    for i in range(TC):
                        residual(NC - 2 + j, i)

            @block.tensor
            def _(pe):
                def chunk(k, j, first):
                    pe.wait_ge(o_lv, k + 1)
                    for i in range(TC):
                        t = TC * k + i
                        if not (first and i < 2):
                            pe.wait_ge(ev, t - 1)
                        for o in range(FT):
                            last = nc.tensor.matmul(bank[i % 2][:, 0:D], lv[j][:, o, i * P:(i + 1) * P], WdT[:, o, :],
                                                    start=(o == 0), stop=(o == FT - 1))
                        last.then_inc(mm, 1)

                chunk(0, 0, True)
                chunk(1, 1, False)
                with nc.tensor.Fori(1, NC // 2, 1) as m:
                    for j in range(2):
                        chunk(2 * m + j, j, False)


def load_experts(nc, sp, W1, W2, b2, w1, w2, b2s, w_in):
    for e in range(E):
        sp.dma_start(w1[:, e, :, :], W1[e].rearrange("(t p) n -> p t n", p=P)).then_inc(w_in, 16)
        sp.dma_start(w2[:, e, :, :], W2[e].rearrange("(t p) n -> p t n", p=P)).then_inc(w_in, 16)
    sp.dma_start(b2s[:, :, :], b2.unsqueeze(0).to_broadcast([P, E, D])).then_inc(w_in, 16)


def route(nc, w, b1T, x_res, mv, rstd, ident, w1, w2, b2s, w_in, xs, acc, table):
    with Scope(nc, "rt") as s:
        wr = s.sb("wr", [P, DT, E])
        brb = s.sb("brb", [P, E])
        b1r = s.sb("b1r", [E * HT, P])
        xn = s.sb("xn", [P, 2, D])
        xt = [s.sb(f"xt{j}", [P, DT, P]) for j in range(2)]
        scores = s.sb("scores", [P, NT, E])
        top = s.sb("top", [P, NT, 8])
        idx = s.sb("idx", [P, NT, 8], U32)
        idf = s.sb("idf", [P, NT, 2])
        eid = s.sb("eid", [P, E])
        oh = s.sb("oh", [P, 2, NT, E])
        ind, tot, incl = s.sb("ind", [P, NT, E]), s.sb("tot", [P, NT, E]), s.sb("incl", [P, NT, E])
        ones = s.sb("ones", [P, P])
        tri = s.sb("tri", [P, P])
        wt = s.sb("wt", [P, 2, NT])
        meta = s.sb("meta", [P, NT, 2, 2])
        posf = s.sb("posf", [P, NT, 2])
        pos = s.sb("pos", [P, NT, 2], U32)
        tok = s.sb("tok", [P, NT], U32)
        base = s.sb("base", [P, E])
        pay = [s.sb(f"pay{j}", [P, 2, ROW]) for j in range(2)]
        row_i = [s.sb(f"row{j}", [P, 2], U32) for j in range(2)]
        pad = s.sb("pad", [P, ROW])
        ntf, nti, jump = s.sb("ntf", [P, E]), s.sb("nti", [P, E], I32), s.sb("jump", [P, E])
        cum = s.sb("cum", [P, E])
        tid = s.sb("tid", [P, NTL])
        ge = s.sb("ge", [P, NTL, E])
        tf = s.sb("tf", [P, 2, NTL])
        cnt = s.sb("cnt", [P, E], I32)
        ps_t = [s.ps(f"ps_t{j}", [P, CH]) for j in range(2)]
        ps_r = [s.ps(f"ps_r{j}", [P, CH]) for j in range(2)]
        ps_c = [s.ps(f"ps_c{j}", [P, CH]) for j in range(2)]
        (r_in, cst, xn_r, t_r, xt_r, sc_mm, sc_r, c, e_r, d_r, b1_t, b1_c, ind_r, rank_mm, cnt_r, padded,
         pos_r, pay0, pay1, meta_r, acc_in) = (s.sem(n) for n in (
            "r_in", "cst", "xn_r", "t_r", "xt_r", "sc_mm", "sc_r", "c", "e_r", "d_r", "b1_t", "b1_c", "ind_r",
            "rank_mm", "cnt_r", "padded", "pos_r", "pay0", "pay1", "meta_r", "acc_in"))
        sent = [s.sem(f"sent{j}") for j in range(2)]
        begun = s.sem("begun")
        CONSTS = 10
        block = s.block()

        def tile(buf, t):
            return buf[:, bass.ds(t, 1), :].rearrange("p a d -> p (a d)")

        @block.sync
        def _(sp):
            sp.dma_start(wr[:, :, :], w["L1_ffn_Wr"].rearrange("(t p) e -> p t e", p=P)).then_inc(r_in, 16)
            sp.dma_start(brb[:, :], w["L1_ffn_br"].unsqueeze(0).to_broadcast([P, E])).then_inc(r_in, 16)
            sp.dma_start(b1r[:, :], w["L1_ffn_b1"].rearrange("e (t p) -> (e t) p", p=P)).then_inc(r_in, 16)
            for g in range(4):
                sp.dma_start(acc[g * T // 4:(g + 1) * T // 4, :].rearrange("(t p) d -> p t d", p=P),
                             x_res[:, g * NT // 4:(g + 1) * NT // 4, :]).then_inc(acc_in, 16)
            load_experts(nc, sp, w["L1_ffn_W1"], w["L1_ffn_W2"], w["L1_ffn_b2"], w1, w2, b2s, w_in)
            sp.wait_ge(cst, CONSTS)
            sp.dma_start(acc[T:T + P, :], pad[:, 0:D]).then_inc(acc_in, 16)
            sp.dma_start(xs[E * CAP:E * CAP + P, :], pad[:, :]).then_inc(padded, 16)
            sp.wait_ge(cnt_r, 1)
            for e in range(E):
                n = nc.sync.value_load(cnt[0:1, e:e + 1], min_val=0, max_val=T)
                sp.dma_start(xs[bass.ds(n + e * CAP, P), :], pad[:, :]).then_inc(padded, 16)
            sp.wait_ge(padded, 16 * (E + 1))
            sp.wait_ge(acc_in, 16 * 5)

        @block.gpsimd
        def _(pool):
            g = nc.gpsimd
            g.iota(eid[:, :], pattern=[[1, E]], base=0, channel_multiplier=0,
                   allow_small_or_imprecise_dtypes=True).then_inc(cst, 1)
            g.iota(base[:, :], pattern=[[CAP, E]], base=0, channel_multiplier=0,
                   allow_small_or_imprecise_dtypes=True).then_inc(cst, 1)
            g.iota(tid[:, :], pattern=[[1, NTL]], base=0, channel_multiplier=0,
                   allow_small_or_imprecise_dtypes=True).then_inc(cst, 1)
            g.iota(tok[:, :].bitcast(I32), pattern=[[P, NT]], base=0, channel_multiplier=1).then_inc(cst, 1)
            g.memset(ones[:, :], 1.0).then_inc(cst, 1)
            g.memset(pad[:, 0:ROW - 1], 0.0).then_inc(cst, 1)
            g.iota(pad[:, ROW - 1:ROW].bitcast(I32), pattern=[[0, 1]], base=T, channel_multiplier=1).then_inc(cst, 1)
            g.memset(tri[:, :], 1.0).then_inc(cst, 1)
            pool.wait_ge(cst, 8)
            g.affine_select(out=tri[:, :], in_=tri[:, :], compare_op=ALU.is_gt, fill=0.0, base=0,
                            pattern=[[1, P]], channel_multiplier=-1).then_inc(cst, 1)
            g.memset(tot[:, :, :], 0.0).then_inc(cst, 1)

            last_row = g.to_reg(E * CAP - 1)

            def send(t, j):
                pool.wait_ge(meta_r, t + 1)
                pool.wait_ge(pay0, t + 1)
                pool.wait_ge(pay1, t + 1)
                pool.sem_inc(begun, 1)
                for k in range(2):
                    g.indirect_dma_start(out=xs[:, :], out_offset=bass.IndirectOffsetOnAxis(ap=row_i[j][:, k:k + 1], axis=0),
                                         in_=pay[j][:, k, :], in_offset=None, bounds_check=last_row,
                                         oob_is_err=True).then_inc(sent[j], 16)

            with g.Fori(0, NT // 2, 1) as i:
                for j in range(2):
                    send(2 * i + j, j)
            for j in range(2):
                pool.wait_ge(sent[j], 16 * NT)

        @block.tensor
        def _(pe):
            pe.wait_ge(r_in, 48)
            nc.tensor.transpose(ps_r[0][:, 0:E * HT], b1r[:, :], ident[0:E * HT, 0:E * HT]).then_inc(b1_t, 1)
            pe.wait_ge(b1_c, 1)

            def turn(t, j, first):
                pe.wait_ge(xn_r, t + 1)
                if not first:
                    pe.wait_ge(xt_r, t - 1)
                for d in range(DT):
                    last = nc.tensor.transpose(ps_t[j][:, d * P:(d + 1) * P], xn[:, j, d * P:(d + 1) * P], ident[:, :])
                last.then_inc(t_r, 1)

            def score(t, j, first):
                pe.wait_ge(xt_r, t + 1)
                if not first:
                    pe.wait_ge(sc_r, t - 1)
                for d in range(DT):
                    last = nc.tensor.matmul(ps_r[j][:, 0:E], xt[j][:, d, :], wr[:, d, :], start=(d == 0), stop=(d == DT - 1))
                last.then_inc(sc_mm, 1)

            turn(0, 0, True)
            turn(1, 1, True)
            score(0, 0, True)
            turn(2, 0, False)
            score(1, 1, True)
            with nc.tensor.Fori(1, NT // 2 - 1, 1) as i:
                for j in range(2):
                    turn(2 * i + j + 1, 1 - j, False)
                    score(2 * i + j, j, False)
            turn(NT - 1, 1, False)
            for j in range(2):
                score(NT - 2 + j, j, False)
            pe.wait_ge(ind_r, 1)
            pe.wait_ge(cst, CONSTS)
            nc.tensor.matmul(ps_c[0][:, 0:NT * E], tri[:, :], ind[:, :, :], start=True, stop=True).then_inc(rank_mm, 1)
            nc.tensor.matmul(ps_c[1][:, 0:NT * E], ones[:, :], ind[:, :, :], start=True, stop=True).then_inc(rank_mm, 1)

        @block.scalar
        def _(act):
            def copy(t, j, first):
                act.wait_ge(t_r, t + 1)
                if not first:
                    act.wait_ge(sc_mm, t - 1)
                nc.scalar.copy(xt[j][:, :, :], ps_t[j][:, 0:D].rearrange("p (d n) -> p d n", d=DT)).then_inc(xt_r, 1)

            copy(0, 0, True)
            copy(1, 1, True)
            with nc.scalar.Fori(1, NT // 2, 1) as i:
                for j in range(2):
                    copy(2 * i + j, j, False)
            act.wait_ge(d_r, 1)
            nc.scalar.activation(wt[:, 1, :], wt[:, 0, :], ACT.Exp).then_inc(e_r, 1)
            with nc.scalar.Fori(0, NT // 2, 1) as i:
                for j in range(2):
                    act.wait_ge(pay0, 2 * i + j + 1)
                    nc.scalar.copy(pay[j][:, 1, 0:D], pay[j][:, 0, 0:D]).then_inc(pay1, 1)

        @block.vector
        def _(dve):
            v = nc.vector
            dve.wait_ge(r_in, 48)

            def layer_norm(dst, t):
                return v.tensor_scalar(dst, tile(x_res, t), mv[:, bass.ds(t, 1), 0:1].rearrange("p a b -> p (a b)"),
                                       rstd[:, bass.ds(t, 1)], ALU.subtract, ALU.mult)

            def norm(t, j, first):
                if not first:
                    dve.wait_ge(t_r, t - 1)
                layer_norm(xn[:, j, :], t).then_inc(xn_r, 1)

            def score(t, j):
                dve.wait_ge(sc_mm, t + 1)
                v.tensor_tensor(tile(scores, t), ps_r[j][:, 0:E], brb[:, :], ALU.add).then_inc(sc_r, 1)

            dve.wait_ge(b1_t, 1)
            v.tensor_copy(b1T[:, :], ps_r[0][:, 0:E * HT]).then_inc(b1_c, 1)
            norm(0, 0, True)
            norm(1, 1, True)
            with v.Fori(1, NT // 2, 1) as i:
                for j in range(2):
                    norm(2 * i + j, j, False)
                    score(2 * i + j - 2, j)
            for j in range(2):
                score(NT - 2 + j, j)
            dve.wait_ge(sc_r, NT)
            n = [0]

            def then(ins):
                n[0] += 1
                ins.then_inc(c, 1)
                dve.wait_ge(c, n[0])

            for t in range(NT):
                last = v.max(out=top[:, t, :], in_=scores[:, t, :])
            then(last)
            v.tensor_tensor(wt[:, 0, :], top[:, :, 1], top[:, :, 0], ALU.subtract).then_inc(d_r, 1)
            for t in range(NT):
                last = v.max_index(out=idx[:, t, :], in_max=top[:, t, :], in_values=scores[:, t, :])
            then(last)
            then(v.tensor_copy(idf[:, :, :], idx[:, :, 0:2]))
            dve.wait_ge(cst, CONSTS)
            for k in range(2):
                last = v.tensor_tensor(oh[:, k, :, :], idf[:, :, k].unsqueeze(2).to_broadcast([P, NT, E]),
                                       eid[:, :].unsqueeze(1).to_broadcast([P, NT, E]), ALU.is_equal)
            then(last)
            v.tensor_tensor(ind[:, :, :], oh[:, 0, :, :], oh[:, 1, :, :], ALU.add).then_inc(ind_r, 1)
            dve.wait_ge(e_r, 1)
            then(v.tensor_scalar(wt[:, 0, :], wt[:, 1, :], 1.0, None, ALU.add))
            then(v.reciprocal(meta[:, :, 0, 0], wt[:, 0, :]))
            v.tensor_tensor(meta[:, :, 1, 0], wt[:, 1, :], meta[:, :, 0, 0], ALU.mult)
            for k in range(2):
                v.tensor_copy(meta[:, :, k, 1].bitcast(U32), tok[:, :])
            dve.wait_ge(rank_mm, 2)
            then(v.tensor_copy(tot[:, :, :], ps_c[1][:, 0:NT * E].rearrange("p (t e) -> p t e", e=E)))
            for e in range(E):
                last = v.tensor_tensor_scan(incl[:, :, e], ones[:, 0:NT], tot[:, :, e], 0.0, ALU.mult, ALU.add)
            then(last)
            v.tensor_copy(cnt[:, :], incl[:, NT - 1, :]).then_inc(cnt_r, 1)
            then(v.tensor_tensor(tot[:, :, :], incl[:, :, :], tot[:, :, :], ALU.subtract))
            then(v.tensor_tensor(tot[:, :, :], ps_c[0][:, 0:NT * E].rearrange("p (t e) -> p t e", e=E), tot[:, :, :], ALU.add))
            then(v.tensor_tensor(tot[:, :, :], tot[:, :, :], base[:, :].unsqueeze(1).to_broadcast([P, NT, E]), ALU.add))
            for k in range(2):
                last = v.tensor_tensor(oh[:, k, :, :], oh[:, k, :, :], tot[:, :, :], ALU.mult)
            then(last)
            for k in range(2):
                last = v.tensor_reduce(posf[:, :, k], oh[:, k, :, :], AX.X, ALU.add)
            then(last)
            then(v.tensor_copy(pos[:, :, :], posf[:, :, :]))

            def rows(t, j, first):
                if not first:
                    dve.wait_ge(sent[j], 16 * (t - j))
                layer_norm(pay[j][:, 0, 0:D], t).then_inc(pay0, 1)
                v.tensor_copy(pay[j][:, :, D:ROW], meta[:, bass.ds(t, 1), :, :].rearrange("p a k m -> p (a k) m"))
                v.tensor_copy(row_i[j][:, :], tile(pos, t)).then_inc(meta_r, 1)

            rows(0, 0, True)
            rows(1, 1, True)
            then(v.tensor_scalar(nti[:, :], incl[:, NT - 1, :], float(P - 1), None, ALU.add))
            then(v.tensor_scalar(nti[:, :], nti[:, :], 7, None, ALU.logical_shift_right))
            then(v.tensor_copy(ntf[:, :], nti[:, :]))
            then(v.tensor_tensor_scan(cum[:, :], ones[:, 0:E], ntf[:, :], 0.0, ALU.mult, ALU.add))
            v.tensor_scalar(jump[:, :], ntf[:, :], -1.0, float(CAP // P), ALU.mult, ALU.add)
            then(v.tensor_tensor(ge[:, :, :], tid[:, :].unsqueeze(2).to_broadcast([P, NTL, E]),
                                 cum[:, :].unsqueeze(1).to_broadcast([P, NTL, E]), ALU.is_ge))
            then(v.tensor_reduce(tf[:, 1, :], ge[:, :, :], AX.X, ALU.add))
            then(v.tensor_tensor(ge[:, :, :], ge[:, :, :], jump[:, :].unsqueeze(1).to_broadcast([P, NTL, E]), ALU.mult))
            then(v.tensor_reduce(tf[:, 0, :], ge[:, :, :], AX.X, ALU.add))
            then(v.tensor_tensor(tf[:, 0, :], tf[:, 0, :], tid[:, :], ALU.add))
            v.tensor_scalar(table[:, 0, :], tf[:, 0, :], float(E * CAP // P), None, ALU.min)
            v.tensor_scalar(table[:, 1, :], tf[:, 1, :], float(E - 1), None, ALU.min)
            with v.Fori(1, NT // 2, 1) as i:
                for j in range(2):
                    rows(2 * i + j, j, False)


def experts(nc, b1T, w1, w2, b2s, w_in, ident, xs, acc, table):
    with Scope(nc, "ex") as s:
        row = [s.sb(f"row{j}", [P, ROW]) for j in range(2)]
        mt = [s.sb(f"mt{j}", [P, 2]) for j in range(2)]
        xT = [s.sb(f"xT{j}", [P, DT, P]) for j in range(2)]
        h = [s.sb(f"h{j}", [P, HID]) for j in range(2)]
        hT = [s.sb(f"hT{j}", [P, HT, P]) for j in range(2)]
        yb = [s.sb(f"yb{j}", [P, D]) for j in range(2)]
        yo = [s.sb(f"yo{j}", [P, D]) for j in range(2)]
        ps_t = s.ps("ps_t", [P, CH])
        ps_h = [s.ps(f"ps_h{j}", [P, HID]) for j in range(2)]
        ps_u = s.ps("ps_u", [P, HT, P])
        ps_y = s.ps("ps_y", [P, CH])
        t_r, xT_r, h_mm, h_r, u_r, hT_r, y_mm, mt_r, yb_r, yo_r, added = (
            s.sem(n) for n in ("t_r", "xT_r", "h_mm", "h_r", "u_r", "hT_r", "y_mm", "mt_r", "yb_r", "yo_r", "added"))
        row_in = [s.sem(f"row_in{j}") for j in range(2)]
        begun = s.sem("begun")
        block = s.block()

        def steps(eng, step):
            step(0, 0, 2, True)
            step(1, 1, 2, False)
            with eng.Fori(1, NTL // 2 - 1, 1) as i:
                for j in range(2):
                    step(2 * i + j, j, 2, False)
            step(NTL - 2, 0, 1, False)
            step(NTL - 1, 1, 0, False)

        def look_up(eng, what, i, top):
            return eng.value_load(table[0:1, what, bass.ds(i, 1)], min_val=0, max_val=top)

        @block.sync
        def _(sp):
            def load(i, j, first):
                r = look_up(nc.sync, 0, i, E * CAP // P)
                if not first:
                    sp.wait_ge(t_r, i - 1)
                    sp.wait_ge(mt_r, i - 1)
                sp.dma_start(row[j][:, :], xs[bass.ds(r * P, P), :]).then_inc(row_in[j], 16)

            load(0, 0, True)
            load(1, 1, True)
            with nc.sync.Fori(1, NTL // 2, 1) as m:
                for j in range(2):
                    load(2 * m + j, j, False)

        @block.tensor
        def _(pe):
            def turn_x(i, j, first):
                pe.wait_ge(row_in[j], 16 * (i // 2 + 1))
                if not first:
                    pe.wait_ge(xT_r, i)
                for d in range(DT):
                    last = nc.tensor.transpose(ps_t[:, d * P:(d + 1) * P], row[j][:, d * P:(d + 1) * P], ident[:, :])
                last.then_inc(t_r, 1)

            def up(i, j, first):
                e = look_up(nc.tensor, 1, i, E - 1)
                pe.wait_ge(xT_r, i + 1)
                if not first:
                    pe.wait_ge(h_r, i - 1)
                w = w1[:, :, :, :].rearrange("p e t n -> p (e t n)")
                for c in range(2):
                    for d in range(DT):
                        last = nc.tensor.matmul(ps_h[j][:, c * CH:(c + 1) * CH], xT[j][:, d, :],
                                                w[:, bass.ds(e * (DT * HID) + d * HID + c * CH, CH)],
                                                start=(d == 0), stop=(d == DT - 1))
                last.then_inc(h_mm, 1)

            def turn_h(i, j, first):
                pe.wait_ge(h_r, i + 1)
                for g in range(2):
                    if not first:
                        pe.wait_ge(hT_r, 2 * (i - 1) + g + 1)
                    for n in range(4 * g, 4 * g + 4):
                        last = nc.tensor.transpose(ps_u[:, n, :], h[j][:, n * P:(n + 1) * P], ident[:, :])
                    last.then_inc(u_r, 1)

            def down(i, j, first):
                e = look_up(nc.tensor, 1, i, E - 1)
                if not first:
                    pe.wait_ge(yb_r, i)
                w = w2[:, :, :, :].rearrange("p e t n -> p (e t n)")
                for n in range(HT):
                    if n % 4 == 0:
                        pe.wait_ge(hT_r, 2 * i + n // 4 + 1)
                    last = nc.tensor.matmul(ps_y[:, 0:D], hT[j][:, n, :], w[:, bass.ds(e * (HT * D) + n * D, D)],
                                            start=(n == 0), stop=(n == HT - 1))
                last.then_inc(y_mm, 1)

            def step(k, j, more, first):
                turn_h(k, j, first)
                if more >= 1:
                    up(k + 1, 1 - j, first)
                if more >= 2:
                    turn_x(k + 2, j, False)
                down(k, j, first)

            pe.wait_ge(w_in, 16 * (2 * E + 1))
            turn_x(0, 0, True)
            turn_x(1, 1, False)
            up(0, 0, True)
            steps(nc.tensor, step)

        @block.scalar
        def _(act):
            def copy_xT(i, j, first):
                act.wait_ge(t_r, i + 1)
                if not first:
                    act.wait_ge(h_mm, i - 1)
                nc.scalar.copy(xT[j][:, :, :], ps_t[:, 0:D].rearrange("p (d n) -> p d n", d=DT)).then_inc(xT_r, 1)

            def relu(i, j, first):
                e = look_up(nc.scalar, 1, i, E - 1)
                if not first:
                    act.wait_ge(y_mm, i - 1)
                for g in range(2):
                    act.wait_ge(u_r, 2 * i + g + 1)
                    for n in range(4 * g, 4 * g + 4):
                        last = nc.scalar.activation(hT[j][:, n, :], ps_u[:, n, :], ACT.Relu,
                                                    bias=b1T[:, bass.ds(e * HT + n, 1)])
                    last.then_inc(hT_r, 1)

            def step(k, j, more, first):
                relu(k, j, first or (isinstance(k, int) and k == 1))
                if more >= 2:
                    copy_xT(k + 2, j, False)

            copy_xT(0, 0, True)
            copy_xT(1, 1, True)
            steps(nc.scalar, step)

        @block.vector
        def _(dve):
            def take_h(i, j, first):
                dve.wait_ge(h_mm, i + 1)
                if not first:
                    dve.wait_ge(u_r, 2 * (i - 1))
                nc.vector.tensor_copy(h[j][:, :], ps_h[j][:, :]).then_inc(h_r, 1)

            def take_meta(i, j, first):
                dve.wait_ge(row_in[j], 16 * (i // 2 + 1))
                if not first:
                    dve.wait_ge(added, 16 * (i - 1))
                nc.vector.tensor_copy(mt[j][:, :], row[j][:, D:ROW]).then_inc(mt_r, 1)

            def weigh(i, j):
                e = look_up(nc.vector, 1, i, E - 1)
                dve.wait_ge(y_mm, i + 1)
                nc.vector.tensor_tensor(yb[j][:, :], ps_y[:, 0:D],
                                        b2s[:, bass.ds(e, 1), :].rearrange("p a d -> p (a d)"), ALU.add).then_inc(yb_r, 1)
                dve.wait_ge(yb_r, i + 1)
                dve.wait_ge(mt_r, i + 1)
                nc.vector.tensor_scalar(yo[j][:, :], yb[j][:, :], mt[j][:, 0:1], None, ALU.mult).then_inc(yo_r, 1)

            def step(k, j, more, first):
                if more >= 1:
                    take_h(k + 1, 1 - j, first)
                    take_meta(k + 1, 1 - j, first)
                weigh(k, j)

            dve.wait_ge(w_in, 16 * (2 * E + 1))
            take_h(0, 0, True)
            take_meta(0, 0, True)
            steps(nc.vector, step)

        @block.gpsimd
        def _(pool):
            last_row = nc.gpsimd.to_reg(T + P - 1)

            def add(i, j, first):
                pool.wait_ge(yo_r, i + 1)
                if not first:
                    pool.wait_ge(added, 16 * i)
                pool.sem_inc(begun, 1)
                nc.gpsimd.indirect_dma_start(out=acc[:, :],
                                             out_offset=bass.IndirectOffsetOnAxis(ap=mt[j][:, 1:2].bitcast(U32), axis=0),
                                             in_=yo[j][:, :], in_offset=None, bounds_check=last_row, oob_is_err=True,
                                             compute_op=ALU.add).then_inc(added, 16)

            add(0, 0, True)
            add(1, 1, False)
            with nc.gpsimd.Fori(1, NTL // 2, 1) as m:
                for j in range(2):
                    add(2 * m + j, j, False)
            pool.wait_ge(added, 16 * NTL)


def store_acc(nc, acc, out):
    with Scope(nc, "sa") as s:
        stored = s.sem("stored")
        ov = out.rearrange("b s d -> (b s) d")
        block = s.block()

        @block.sync
        def _(sp):
            for g in range(4):
                sp.dma_start(ov[g * T // 4:(g + 1) * T // 4, :], acc[g * T // 4:(g + 1) * T // 4, :]).then_inc(stored, 16)
            sp.wait_ge(stored, 16 * 4)


def store(nc, x_res, out):
    with Scope(nc, "so") as s:
        stored = s.sem("stored")
        ov = out.rearrange("b (t p) d -> p (b t) d", p=P)
        block = s.block()

        @block.sync
        def _(sp):
            for g in range(8):
                sp.dma_start(ov[:, 4 * g:4 * g + 4, :], x_res[:, 4 * g:4 * g + 4, :]).then_inc(stored, 16)
            sp.wait_ge(stored, 16 * 8)


def program(nc, w, out, stages=9):
    with Scope(nc, "main") as s:
        x_res = s.sb("x_res", [P, NT, D])
        mv, rstd = s.sb("mv", [P, NT, 2]), s.sb("rstd", [P, NT])
        stats = s.sb("stats", [P, NT, 6])
        ident = s.sb("ident", [P, P])
        ctxT = s.sb("ctxT", [P, 2, B * KV])
        load_and_stats(nc, w["x"], w["ctx_768"], x_res, stats, ident, ctxT)
        l0 = {"q": w["L0_xattn_w_q"], "k": w["L0_xattn_w_kv"][:, 0:INNER], "v": w["L0_xattn_w_kv"][:, INNER:2 * INNER],
              "o": w["L0_xattn_w_out"]}
        l1 = {k: w["L1_xattn_" + n] for k, n in (
            ("q", "Wq"), ("k", "Wk"), ("v", "Wv"), ("o", "Wo"), ("k_ipa", "Wk_ipa"), ("v_ipa", "Wv_ipa"),
            *((n, n) for n in ("q_down", "q_up", "q_alpha", "k_down", "k_up", "k_alpha",
                               "v_down", "v_up", "v_alpha", "o_down", "o_up", "o_alpha")))}

        def cross(layer, weights, groups, bias):
            with Scope(nc, f"c{layer}") as z:
                M = z.sb("M", [P, DT, B, INNER])
                VW = z.sb("VW", [P, B, NP, D])
                prepare_attention(nc, f"pa{layer}", weights, ctxT, ident, M, VW)
                rstd_of(nc, f"r{layer}", stats, mv, rstd)
                attention(nc, f"at{layer}", groups, bias, x_res, mv, rstd, stats, ident, M, VW)

        if stages >= 1:
            cross(0, l0, [(0, KV)], w["L0_xattn_b_out"])
        if stages >= 2:
            with Scope(nc, "f") as z:
                WgT, WuT = z.sb("WgT", [P, DT, FF]), z.sb("WuT", [P, DT, FF])
                WdT = z.sb("WdT", [P, FT, D])
                xqT = z.sb("xqT", [P, DT, T])
                scale_x = z.sb("scale_x", [P, 1])
                quantise_weights(nc, w["L0_ffn_w_gate"], w["L0_ffn_w_up"], w["L0_ffn_w_down"], WgT, WuT, WdT, ident)
                rstd_of(nc, "r2", stats, mv, rstd)
                quantise_input(nc, x_res, mv, rstd, scale_x, xqT, ident)
                gate = z.sb("gate", [P, NC * FT * CH])
                up_dram = nc.dram_tensor("up_scratch", (2 * NC, P, FT // 2 * CH), F32, kind="Internal").ap()
                gated_mlp(nc, x_res, stats, scale_x, xqT, WgT, WuT, WdT, up_dram, gate)
        if stages >= 3:
            cross(1, l1, [(0, KV - IPA), (KV - IPA, KV)], w["L1_xattn_bo"])
        if stages < 4:
            store(nc, x_res, out)
            return
        with Scope(nc, "e") as z:
            w1 = z.sb("w1", [P, E, DT, HID])
            w2 = z.sb("w2", [P, E, HT, D])
            b2s = z.sb("b2s", [P, E, D])
            b1T = z.sb("b1T", [P, E * HT])
            table = z.sb("table", [P, 2, NTL], I32)
            w_in = z.sem("w_in")
            xs = nc.dram_tensor("xs", (E * CAP + P, ROW), F32, kind="Internal").ap()
            acc = nc.dram_tensor("acc", (T + P, D), F32, kind="Internal").ap()
            rstd_of(nc, "r4", stats, mv, rstd)
            route(nc, w, b1T, x_res, mv, rstd, ident, w1, w2, b2s, w_in, xs, acc, table)
            experts(nc, b1T, w1, w2, b2s, w_in, ident, xs, acc, table)
            store_acc(nc, acc, out)


def kernel(**inputs):
    import numpy as np
    import concourse.bacc as bacc
    from concourse.bass_utils import run_bass_kernel_spmd

    nc = bacc.Bacc("TRN2", target_bir_lowering=False, num_devices=1)
    arrays, aps = {}, {}
    for name, a in inputs.items():
        a = np.ascontiguousarray(a)
        arrays[f"in_{name}"] = a
        aps[name] = nc.dram_tensor(f"in_{name}", a.shape, mybir.dt.from_np(a.dtype), kind="ExternalInput").ap()
    out = nc.dram_tensor("out_0", (B, S, D), F32, kind="ExternalOutput").ap()
    program(nc, aps, out)
    r = run_bass_kernel_spmd(nc, [arrays], core_ids=[0])
    return r.results[0]["out_0"]
```

```python
from contextlib import ExitStack

import concourse.bass as bass
from concourse import mybir

F32 = mybir.dt.float32
I16 = mybir.dt.int16
I32 = mybir.dt.int32
U16 = mybir.dt.uint16
U32 = mybir.dt.uint32
F16 = mybir.dt.float16
ALU = mybir.AluOpType
ACT = mybir.ActivationFunctionType
AX = mybir.AxisListType
RMAX = bass.bass_isa.ReduceOp.max

P = 128
B, S, D = 4, 1024, 256
T = B * S
NT = T // P
DT = D // P
KV, C = 64, 192
C1 = C - P
H, HD = 16, 64
INNER = H * HD
NP = INNER // P
IPA = 4
RANK = 32
FF, QB = 768, 32
FT = FF // P
CH = 512
NC = T // CH
E, HID = 8, 1024
HT = HID // P
WN = D * HID // P
CAP = T + P
ROW = D + 2
NTL = (2 * T + E * (P - 1)) // P + 1
NTL += NTL % 2
EPS = 1e-5
EXPONENT = 0x7F800000
XN_SCALE = 1024.0
P_SCALE = 32768.0
MAGIC = 12582912.0
QACT = 32767.0


class Scope:
    taken = []

    def __init__(self, nc, tag):
        self.nc, self.tag, self.ctx = nc, tag, ExitStack()

    def __enter__(self):
        self.ctx.__enter__()
        return self

    def __exit__(self, *a):
        return self.ctx.__exit__(*a)

    def sb(self, name, shape, dt=F32):
        return self.ctx.enter_context(self.nc.sbuf_tensor(f"{self.tag}_{name}", shape, dt))

    def ps(self, name, shape, dt=F32):
        return self.ctx.enter_context(self.nc.psum_tensor(f"{self.tag}_{name}", shape, dt))

    def sem(self, name):
        sem = self.ctx.enter_context(self.nc.semaphore(f"{self.tag}_{name}"))
        self.taken.append(sem)
        return sem

    def block(self):
        return self.ctx.enter_context(self.nc.Block())


def clear_semaphores(nc, sems):
    with nc.Block() as block:
        @block.sync
        def _(sp):
            for sem in sems:
                sp.sem_clear(sem)
    sems.clear()


def need(eng, sem, n):
    if not (isinstance(n, int) and n <= 0):
        eng.wait_ge(sem, n)


def in_steps(eng, n, lead, lag, step):
    for k in range(-lead, 4):
        step(k, k % 2)
    with eng.Fori(2, n // 2 - 2, 1) as i:
        for j in range(2):
            step(2 * i + j, j)
    for k in range(n - 4, n + lag):
        step(k, k % 2)


def there(t, n):
    return not isinstance(t, int) or 0 <= t < n


def load(nc, ctx_in, ident, ctxT):
    with Scope(nc, "ld") as s:
        crow = s.sb("crow", [P, 2, C])
        pT = s.ps("pT", [P, 4, P])
        cin = s.sem("cin")
        idz, idr, ctx_t = s.sem("idz"), s.sem("idr"), s.sem("ctx_t")
        block = s.block()

        @block.sync
        def _(sp):
            sp.dma_start(crow[:, :, :], ctx_in.rearrange("(r b) k c -> (b k) r c", r=2)).then_inc(cin, 16)

        @block.gpsimd
        def _(pool):
            nc.gpsimd.memset(ident[:, :], 0.0).then_inc(idz, 1)
            pool.wait_ge(idz, 1)
            nc.gpsimd.affine_select(out=ident[:, :], in_=ident[:, :], compare_op=ALU.not_equal, fill=1.0,
                                    base=0, pattern=[[-1, P]], channel_multiplier=1).then_inc(idr, 1)

        @block.tensor
        def _(pe):
            pe.wait_ge(idr, 1)
            pe.wait_ge(cin, 16)
            for r in range(2):
                nc.tensor.transpose(pT[:, 2 * r, :], crow[:, r, 0:P], ident[:, :])
                last = nc.tensor.transpose(pT[0:C1, 2 * r + 1, :], crow[:, r, P:C], ident[:, :])
            last.then_inc(ctx_t, 1)

        @block.vector
        def _(dve):
            dve.wait_ge(ctx_t, 1)
            for r in range(2):
                nc.vector.tensor_copy(ctxT[:, 0, r * P:(r + 1) * P], pT[:, 2 * r, :])
                nc.vector.tensor_copy(ctxT[0:C1, 1, r * P:(r + 1) * P], pT[0:C1, 2 * r + 1, :])


def prepare_attention(nc, tag, w, ctxT, ident, M, VW, unscale, x=None, x_res=None, stats=None, x_in=()):
    lora = "q_down" in w
    RING = 6
    with Scope(nc, tag) as s:
        wq, wk, wv = (s.sb(n, [P, 2, INNER]) for n in ("wq", "wk", "wv"))
        wo = s.sb("wo", [P, NP, D])
        WqT = s.sb("WqT", [P, NP, D])
        Kd = s.sb("Kd", [P, NP, B, P])
        Vd = s.sb("Vd", [P, NP, B, P])
        if lora:
            wki, wvi = (s.sb(n, [P, 2, INNER]) for n in ("wki", "wvi"))
            down = s.sb("down", [P, 3, 2, RANK])
            odown = s.sb("odown", [P, NP, RANK])
            up = s.sb("up", [RANK, INNER])
            oup = s.sb("oup", [RANK, D])
            downT = s.sb("downT", [RANK, 4, P])
            odownT = s.sb("odownT", [RANK, NP, P])
            alpha = s.sb("alpha", [P, 4])
            alpha_r = s.sb("alpha_r", [P, 4])
        ring = s.ps("ring", [P, RING, CH])
        early, late, up_in, made, moved, zero = (s.sem(n) for n in ("early", "late", "up_in", "made", "moved", "zero"))
        used, alpha_s, hi_r, chain, am_r, gm_r, sc_r = (
            s.sem(n) for n in ("used", "alpha_s", "hi_r", "chain", "am_r", "gm_r", "sc_r"))
        am, gm = s.sb("am", [P, 4]), s.sb("gm", [P, 4])
        bound, scale = s.sb("bound", [P, 2]), s.sb("scale", [P, 2])
        block = s.block()
        first, second = [], []
        if lora:
            first += [(down[:, 0, :, :], w["q_down"].rearrange("(t p) r -> p t r", p=P))]
            for n, key in ((1, "k_down"), (2, "v_down")):
                first += [(down[:, n, 0, :], w[key][0:P, :]), (down[0:C1, n, 1, :], w[key][P:C, :])]
            for n, key in enumerate(("q_alpha", "k_alpha", "v_alpha", "o_alpha")):
                first += [(alpha[:, n:n + 1], w[key].unsqueeze(0).to_broadcast([P, 1]))]
            second += [(odown[:, :, :], w["o_down"].rearrange("(t p) r -> p t r", p=P)), (oup[:, :], w["o_up"])]
        first += [(wq[:, :, :], w["q"].rearrange("(t p) n -> p t n", p=P))]
        for loads, dst, key in ((first, wk, "k"), (second, wv, "v")) + (
                ((second, wki, "k_ipa"), (second, wvi, "v_ipa")) if lora else ()):
            loads += [(dst[:, 0, :], w[key][0:P, :]), (dst[0:C1, 1, :], w[key][P:C, :])]
        second += [(wo[:, :, :], w["o"].rearrange("(t p) n -> p t n", p=P))]
        results = [(M[0][:, t, :, j * P:(j + 1) * P], M[1][:, t, :, j * P:(j + 1) * P], 0)
                   for j in range(NP) for t in range(DT)]
        results += [(VW[0][:, 2 * g:2 * g + 2, j, :], VW[1][:, 2 * g:2 * g + 2, j, :], 1)
                    for j in range(NP) for g in range(2)]
        steps_before = (3 + 12 + 2 + 4 if lora else 0) + NP // 2 + 2 * NP
        rows = {"q": (P, P), "k": (P, C1), "v": (P, C1)}

        @block.sync
        def _(sp):
            for loads, sem in ((first, early), (second, late)):
                if lora and loads is second:
                    sp.dma_start(up[:, :], w["q_up"]).then_inc(up_in, 16)
                for dst, src in loads:
                    sp.dma_start(dst, src).then_inc(sem, 16)
            for g, sem in enumerate(x_in):
                per = NT // (2 * B)
                sp.dma_start(x_res[:, per * g:per * g + per, :],
                             x.rearrange("b (p t) d -> p b t d", p=P)[:, g // 2, per * (g % 2):per * (g % 2 + 1), :]
                             ).then_inc(sem, 16)
            if lora:
                for n, key in enumerate(("k_up", "v_up")):
                    sp.wait_ge(used, n + 1)
                    sp.dma_start(up[:, :], w[key]).then_inc(up_in, 16)

        @block.gpsimd
        def _(pool):
            nc.gpsimd.memset(Kd[:, :, :, :], 0.0).then_inc(zero, 1)
            nc.gpsimd.memset(Vd[:, :, :, :], 0.0).then_inc(zero, 1)
            pool.wait_ge(am_r, 1)
            nc.gpsimd.partition_all_reduce(gm[:, :], am[:, :], P, RMAX).then_inc(gm_r, 1)

        @block.tensor
        def _(pe):
            n = [0]

            def bank():
                if n[0] >= RING:
                    pe.wait_ge(moved, n[0] - RING + 1)
                n[0] += 1
                return (n[0] - 1) % RING

            pe.wait_ge(early, 16 * len(first))
            if lora:
                for i in range(3):
                    if i == 2:
                        pe.wait_ge(late, 16 * len(second))
                    b = bank()
                    for t in range(2):
                        m = rows["qkv"[i]][t]
                        last = nc.tensor.transpose(ring[0:RANK, b, t * P:t * P + m], down[0:m, i, t, :], ident[0:m, 0:m])
                    last.then_inc(made, 1)
                    pe.wait_ge(moved, n[0])
                    pe.wait_ge(up_in, 16 * (i + 1))
                    for t in range(2):
                        m = rows["qkv"[i]][t]
                        for c in range(2):
                            b = bank()
                            last = nc.tensor.matmul(ring[0:m, b, :], downT[:, t, 0:m], up[:, c * CH:(c + 1) * CH],
                                                    start=True, stop=True)
                            last.then_inc(made, 1)
                    pe.wait_ge(moved, n[0])
                    pe.sem_inc(used, 1)
                for g in range(2):
                    b = bank()
                    for t in range(4):
                        last = nc.tensor.transpose(ring[0:RANK, b, t * P:(t + 1) * P], odown[:, 4 * g + t, :], ident[:, :])
                    last.then_inc(made, 1)
                pe.wait_ge(moved, n[0])
                for g in range(4):
                    b = bank()
                    for t in range(2):
                        last = nc.tensor.matmul(ring[:, b, t * D:(t + 1) * D], odownT[:, 2 * g + t, :], oup[:, :],
                                                start=True, stop=True)
                    last.then_inc(made, 1)
                pe.wait_ge(moved, n[0])
            for g in range(NP // 2):
                b = bank()
                for i in range(2):
                    for t in range(2):
                        last = nc.tensor.transpose(ring[:, b, i * D + t * P:i * D + (t + 1) * P],
                                                   wq[:, t, (2 * g + i) * P:(2 * g + i + 1) * P], ident[:, :])
                last.then_inc(made, 1)
            for base, ipa in ((wk, wki if lora else None), (wv, wvi if lora else None)):
                if base is wv:
                    pe.wait_ge(late, 16 * len(second))
                for j in range(NP):
                    b = bank()
                    parts = [(base, 0, KV - IPA), (ipa, KV - IPA, KV)] if lora else [(base, 0, KV)]
                    for wt, lo, hi in parts:
                        for t in range(2):
                            m = (P, C1)[t]
                            last = nc.tensor.matmul(
                                ring[:, b, 0:B * KV].rearrange("p (b k) -> p b k", b=B)[:, :, lo:hi],
                                wt[0:m, t, j * P:(j + 1) * P],
                                ctxT[0:m, t, :].rearrange("p (b k) -> p b k", b=B)[:, :, lo:hi],
                                start=(t == 0), stop=(t == 1))
                    last.then_inc(made, 1)
            pe.wait_ge(moved, n[0])
            for j in range(NP):
                for t in range(DT):
                    b = bank()
                    nc.tensor.matmul(ring[:, b, :], WqT[:, j, t * P:(t + 1) * P], Kd[:, j, :, :],
                                     start=True, stop=True).then_inc(made, 1)
            for j in range(NP):
                for g in range(2):
                    b = bank()
                    for i in range(2):
                        last = nc.tensor.matmul(ring[:, b, i * D:(i + 1) * D], Vd[:, j, 2 * g + i, :], wo[:, j, :],
                                                start=True, stop=True)
                    last.then_inc(made, 1)

        @block.vector
        def _(dve):
            n = [0]

            def bank():
                n[0] += 1
                dve.wait_ge(made, n[0])
                return (n[0] - 1) % RING

            dve.wait_ge(early, 16 * len(first))
            if lora:
                nc.vector.tensor_scalar(alpha_r[:, :], alpha[:, :], 1.0 / RANK, None, ALU.mult).then_inc(alpha_s, 1)
                dve.wait_ge(alpha_s, 1)
                for i, wt in enumerate((wq, wk, wv)):
                    if i == 2:
                        dve.wait_ge(late, 16 * len(second))
                    b = bank()
                    if i == 0:
                        nc.vector.tensor_copy(downT[:, 0:2, :], ring[0:RANK, b, 0:2 * P]).then_inc(moved, 1)
                    else:
                        nc.vector.tensor_copy(downT[:, 0:2, :].rearrange("r t p -> r (t p)")[:, 0:C],
                                              ring[0:RANK, b, 0:C]).then_inc(moved, 1)
                    for t in range(2):
                        m = rows["qkv"[i]][t]
                        for c in range(2):
                            b = bank()
                            part = wt[0:m, t, c * CH:(c + 1) * CH]
                            nc.vector.scalar_tensor_tensor(out=part, in0=ring[0:m, b, :], scalar=alpha_r[0:m, i:i + 1],
                                                           in1=part, op0=ALU.mult, op1=ALU.add).then_inc(moved, 1)
                for g in range(2):
                    b = bank()
                    nc.vector.tensor_copy(odownT[:, 4 * g:4 * g + 4, :], ring[0:RANK, b, :]).then_inc(moved, 1)
                for g in range(4):
                    b = bank()
                    part = wo[:, 2 * g:2 * g + 2, :]
                    nc.vector.scalar_tensor_tensor(out=part, in0=ring[:, b, :].rearrange("p (t n) -> p t n", t=2),
                                                   scalar=alpha_r[:, 3:4], in1=part,
                                                   op0=ALU.mult, op1=ALU.add).then_inc(moved, 1)
            for g in range(NP // 2):
                b = bank()
                nc.vector.tensor_copy(WqT[:, 2 * g:2 * g + 2, :], ring[:, b, :]).then_inc(moved, 1)

            def absmax(i, src):
                dve.wait_ge(moved, n[0])
                return nc.vector.tensor_reduce(am[:, i:i + 1], src, AX.XYZ if i in (1, 2) else AX.XY, ALU.max,
                                               apply_absolute_value=True)

            absmax(0, WqT[:, :, :])
            dve.wait_ge(zero, 2)
            for dst in (Kd, Vd):
                for j in range(NP):
                    b = bank()
                    for h in range(2):
                        last = nc.vector.tensor_copy(dst[h * HD:(h + 1) * HD, j, :, h * KV:(h + 1) * KV],
                                                     ring[h * HD:(h + 1) * HD, b, 0:B * KV].rearrange("p (b k) -> p b k", b=B))
                    last.then_inc(moved, 1)
                if dst is Kd:
                    absmax(1, Kd[:, :, :, :])
                    dve.wait_ge(late, 16 * len(second))
                    absmax(3, wo[:, :, :])
            absmax(2, Vd[:, :, :, :]).then_inc(am_r, 1)
            dve.wait_ge(gm_r, 1)
            k = [0]

            def then(ins):
                k[0] += 1
                ins.then_inc(chain, 1)
                dve.wait_ge(chain, k[0])

            nc.vector.tensor_scalar(bound[:, 0:1], gm[:, 0:1], gm[:, 1:2], HD ** 0.5, ALU.mult, ALU.mult)
            then(nc.vector.tensor_scalar(bound[:, 1:2], gm[:, 2:3], gm[:, 3:4], float(HD), ALU.mult, ALU.mult))
            then(nc.vector.tensor_scalar(bound[:, :], bound[:, :], 1e-20, None, ALU.max))
            then(nc.vector.tensor_scalar(bound[:, :].bitcast(I32), bound[:, :].bitcast(I32), EXPONENT, None, ALU.bitwise_and))
            then(nc.vector.reciprocal(scale[:, :], bound[:, :]))
            then(nc.vector.tensor_scalar(scale[:, :], scale[:, :], 16384.0, None, ALU.mult))
            nc.vector.tensor_scalar(unscale[:, 0:1], bound[:, 0:1], 2.0 ** -14 / XN_SCALE, None, ALU.mult)
            nc.vector.tensor_scalar(unscale[:, 1:2], bound[:, 1:2], 2.0 ** -14 / P_SCALE, None, ALU.mult)
            then(nc.vector.tensor_scalar(scale[:, 0:1], scale[:, 0:1], HD ** -0.5, None, ALU.mult))
            dve.sem_inc(sc_r, 1)
            m = 0
            for hi, lo, col in results:
                b = bank()
                m += 1
                dve.wait_ge(hi_r, m)
                nc.vector.scalar_tensor_tensor(out=lo, in0=ring[:, b, :].rearrange("p (b n) -> p b n", b=hi.shape[1]),
                                               scalar=scale[:, col:col + 1], in1=hi,
                                               op0=ALU.mult, op1=ALU.subtract).then_inc(moved, 1)
                if x_in:
                    t = m - 1
                    per = NT // len(x_in)
                    if t % per == 0:
                        dve.wait_ge(x_in[t // per], 16)
                    nc.vector.bn_stats(stats[:, t, :], x_res[:, t, :])

        @block.scalar
        def _(act):
            act.wait_ge(sc_r, 1)
            for m, (hi, lo, col) in enumerate(results):
                act.wait_ge(made, steps_before + m + 1)
                b = (steps_before + m) % RING
                nc.scalar.activation(hi, ring[:, b, :].rearrange("p (b n) -> p b n", b=hi.shape[1]), ACT.Copy,
                                     scale=scale[:, col:col + 1]).then_inc(hi_r, 1)


def rstd_of(nc, tag, stats, mv, rstd):
    with Scope(nc, tag) as s:
        ve, sd = s.sb("ve", [P, NT]), s.sb("sd", [P, NT])
        m, a, b = s.sem("m"), s.sem("a"), s.sem("b")
        block = s.block()

        @block.vector
        def _(dve):
            for t in range(NT):
                last = nc.vector.bn_aggr(mv[:, t, :], stats[:, t, :])
            last.then_inc(m, 1)
            dve.wait_ge(m, 1)
            nc.vector.tensor_scalar(ve[:, :], mv[:, :, 1], EPS, None, ALU.add).then_inc(a, 1)
            dve.wait_ge(b, 1)
            nc.vector.reciprocal(rstd[:, :], sd[:, :])

        @block.scalar
        def _(act):
            act.wait_ge(a, 1)
            nc.scalar.activation(sd[:, :], ve[:, :], ACT.Sqrt).then_inc(b, 1)


def attention(nc, tag, groups, bias_in, x_res, mv, rstd, stats, ident, M, VW, unscale, experts_w=None, ssq=None):
    assert NT == 4 * E
    NG = len(groups)
    with Scope(nc, tag) as s:
        xn = s.sb("xn", [P, 2, D])
        xnT = s.sb("xnT", [P, DT, P])
        xnT_hi, xnT_lo = ([s.sb(f"xnT_{n}{j}", [P, DT, P], F16) for j in range(2)] for n in ("hi", "lo"))
        sc = [s.sb(f"sc{j}", [P, H, KV]) for j in range(2)]
        mx = s.sb("mx", [P, 2, H, NG])
        sm = s.sb("sm", [P, 2, H, NG])
        ri = s.sb("ri", [P, 2, H, NG])
        pT = s.sb("pT", [P, NP, P])
        pT_hi, pT_lo = ([s.sb(f"pT_{n}{j}", [P, NP, P], F16) for j in range(2)] for n in ("hi", "lo"))
        bias = s.sb("bias", [P, D])
        new = [s.sb(f"new{j}", [P, D]) for j in range(2)]
        st = [s.sb(f"st{j}", [P, 6]) for j in range(2)]
        ps_xT = s.ps("ps_xT", [P, CH])
        ps_s = [s.ps(f"ps_s{j}", [P, INNER]) for j in range(2)]
        ps_p = s.ps("ps_p", [P, NP, P])
        ps_y = s.ps("ps_y", [P, CH])
        names = ("bias_s", "xn_r", "xb_r", "xT_r", "xf_r", "xhi_r", "xlo_r", "sc_r", "mx_r", "sub_r", "exp_r", "sum_r",
                 "ri_r", "prob_r", "pT_r", "pf_r", "phi_r", "plo_r", "y_r", "res_r", "st_r", "new_c")
        (bias_s, xn_r, xb_r, xT_r, xf_r, xhi_r, xlo_r, sc_r, mx_r, sub_r, exp_r, sum_r,
         ri_r, prob_r, pT_r, pf_r, phi_r, plo_r, y_r, res_r, st_r, new_c) = (s.sem(n) for n in names)
        if experts_w:
            half = [s.sb(f"half{j}", [P, WN // 2]) for j in range(2)]
            half_in = [s.sem(f"half_in{j}") for j in range(2)]
            ssq_r, arrived = s.sem("ssq_r"), s.sem("arrived")
        block = s.block()

        def tile(buf, t):
            return buf[:, bass.ds(t, 1), :].rearrange("p o d -> p (o d)")

        def turned(ps):
            return ps[:, 0:D].rearrange("p (d n) -> p d n", d=DT)

        @block.sync
        def _(sp):
            sp.dma_start(bias[:, :], bias_in.unsqueeze(0).to_broadcast([P, D])).then_inc(bias_s, 16)

            def load_half(m, e, j):
                src = experts_w[m]
                rows = src.shape[1] // 2
                sp.dma_start(half[j][:, :].rearrange("p (t n) -> p t n", n=src.shape[2]),
                             src[bass.ds(e, 1), j * rows:(j + 1) * rows, :].rearrange("o (t p) n -> p (o t) n", p=P)
                             ).then_inc(half_in[j], 16)

            if experts_w:
                for j in range(2):
                    load_half(0, 0, j)
                for m in range(2):
                    with nc.sync.Fori(1 - m, E, 1) as e:
                        for j in range(2):
                            sp.wait_ge(ssq_r, 2 * (m * E + e) + j - 1)
                            load_half(m, e, j)

        @block.tensor
        def _(pe):
            def turn_x(t, j):
                need(pe, xn_r, t + 1)
                need(pe, xf_r, t)
                need(pe, xhi_r, t)
                for d in range(DT):
                    last = nc.tensor.transpose(ps_xT[:, d * P:(d + 1) * P], xn[:, j, d * P:(d + 1) * P], ident[:, :])
                last.then_inc(xT_r, 1)

            def scores(t, j):
                need(pe, xhi_r, t + 1)
                need(pe, xlo_r, t + 1)
                need(pe, sub_r, t - 1)
                off = t // (NT // B) * INNER
                m = [x[:, :, :, :].rearrange("p d b n -> p d (b n)") for x in M]
                parts = [(xnT_hi[j], m[0]), (xnT_hi[j], m[1]), (xnT_lo[j], m[0])]
                for c in range(2):
                    for n, (d, (a, b)) in enumerate((d, p) for d in range(DT) for p in parts):
                        last = nc.tensor.matmul(ps_s[j][:, c * CH:(c + 1) * CH], a[:, d, :],
                                                b[:, d, bass.ds(off + c * CH, CH)],
                                                start=(n == 0), stop=(n == 3 * DT - 1))
                last.then_inc(sc_r, 1)

            def turn_probs(t, j):
                need(pe, prob_r, t + 1)
                need(pe, pf_r, 2 * t)
                need(pe, phi_r, 2 * t)
                for g in range(2):
                    for n in range(4 * g, 4 * g + 4):
                        last = nc.tensor.transpose(ps_p[:, n, :], sc[j][:, 2 * n:2 * n + 2, :], ident[:, :])
                    last.then_inc(pT_r, 1)

            def output(t, j):
                need(pe, phi_r, 2 * t + 2)
                need(pe, plo_r, t + 1)
                need(pe, res_r, t)
                off = t // (NT // B) * (NP * D)
                v = [x[:, :, :, :].rearrange("p b j n -> p (b j n)") for x in VW]
                for n in range(NP):
                    for i, (a, b) in enumerate(((pT_hi, v[0]), (pT_hi, v[1]), (pT_lo, v[0]))):
                        last = nc.tensor.matmul(ps_y[:, 0:D], a[j][:, n, :], b[:, bass.ds(off + n * D, D)],
                                                start=(n == 0 and i == 0), stop=(n == NP - 1 and i == 2))
                last.then_inc(y_r, 1)

            def step(k, j):
                if there(k + 2, NT):
                    scores(k + 2, j)
                if there(k + 3, NT):
                    turn_x(k + 3, 1 - j)
                if there(k, NT):
                    turn_probs(k, j)
                if there(k - 1, NT):
                    output(k - 1, 1 - j)

            in_steps(nc.tensor, NT, 3, 1, step)

        @block.scalar
        def _(act):
            def split_x(t, j):
                need(act, xT_r, t + 1)
                need(act, xlo_r, t)
                nc.scalar.mul(xnT[:, :, :], turned(ps_xT), XN_SCALE).then_inc(xf_r, 1)
                need(act, sc_r, t - 1)
                nc.scalar.mul(xnT_hi[j][:, :, :], turned(ps_xT), XN_SCALE).then_inc(xhi_r, 1)

            def split_p(t, j):
                need(act, plo_r, t)
                need(act, y_r, t - 1)
                for g in range(2):
                    act.wait_ge(pT_r, 2 * t + g + 1)
                    nc.scalar.mul(pT[:, 4 * g:4 * g + 4, :], ps_p[:, 4 * g:4 * g + 4, :], P_SCALE).then_inc(pf_r, 1)
                    nc.scalar.mul(pT_hi[j][:, 4 * g:4 * g + 4, :], ps_p[:, 4 * g:4 * g + 4, :], P_SCALE).then_inc(phi_r, 1)

            def exps(t, j):
                act.wait_ge(sub_r, t + 1)
                nc.scalar.activation(sc[j][:, :, :], sc[j][:, :, :], ACT.Exp, scale=unscale[:, 0:1]).then_inc(exp_r, 1)

            def keep(t, j):
                act.wait_ge(res_r, t + 1)
                nc.scalar.copy(tile(x_res, t), new[j][:, :]).then_inc(new_c, 1)

            def squares(t, j):
                act.wait_ge(half_in[j], 16 * (t // 2 + 1))
                act.sem_inc(arrived, 1)
                nc.scalar.activation(half[j][:, :], half[j][:, :], ACT.Square, accum_out=ssq[:, bass.ds(t, 1)]
                                     ).then_inc(ssq_r, 1)

            def step(k, j):
                if there(k + 3, NT):
                    split_x(k + 3, 1 - j)
                if there(k, NT):
                    split_p(k, j)
                if there(k + 2, NT):
                    exps(k + 2, j)
                if there(k - 2, NT):
                    keep(k - 2, j)
                if experts_w and there(k, NT):
                    squares(k, j)

            in_steps(nc.scalar, NT, 3, 2, step)

        @block.vector
        def _(dve):
            def norm(t, j):
                need(dve, xT_r, t - 1)
                tt = tile(x_res, t)
                nc.vector.tensor_scalar(xn[:, j, :], tt, mv[:, bass.ds(t, 1), 0:1].rearrange("p a b -> p (a b)"),
                                        rstd[:, bass.ds(t, 1)], ALU.subtract, ALU.mult).then_inc(xn_r, 1)

            def softmax_in(t, j):
                dve.wait_ge(sc_r, t + 1)
                scv = ps_s[j][:, :].rearrange("p (h k) -> p h k", h=H)
                for g, (lo, hi) in enumerate(groups):
                    last = nc.vector.tensor_reduce(mx[:, j, :, g], scv[:, :, lo:hi], AX.X, ALU.max)
                last.then_inc(mx_r, 1)
                dve.wait_ge(mx_r, t + 1)
                need(dve, pT_r, 2 * (t - 1))
                for g, (lo, hi) in enumerate(groups):
                    last = nc.vector.tensor_tensor(sc[j][:, :, lo:hi], scv[:, :, lo:hi],
                                                   mx[:, j, :, g].unsqueeze(2).to_broadcast([P, H, hi - lo]),
                                                   ALU.subtract)
                last.then_inc(sub_r, 1)

            def sums(t, j):
                dve.wait_ge(exp_r, t + 1)
                for g, (lo, hi) in enumerate(groups):
                    last = nc.vector.tensor_reduce(sm[:, j, :, g], sc[j][:, :, lo:hi], AX.X, ALU.add)
                last.then_inc(sum_r, 1)
                dve.wait_ge(sum_r, t + 1)
                need(dve, prob_r, t - 1)
                nc.vector.reciprocal(ri[:, j, :, :], sm[:, j, :, :]).then_inc(ri_r, 1)

            def residual(t, j):
                dve.wait_ge(y_r, t + 1)
                dve.wait_ge(xb_r, t + 1)
                need(dve, new_c, t - 1)
                nc.vector.scalar_tensor_tensor(out=new[j][:, :], in0=ps_y[:, 0:D], scalar=unscale[:, 1:2],
                                               in1=tile(x_res, t), op0=ALU.mult, op1=ALU.add).then_inc(res_r, 1)

            def statistics(t, j):
                dve.wait_ge(res_r, t + 1)
                nc.vector.bn_stats(st[j][:, :], new[j][:, :]).then_inc(st_r, 1)
                dve.wait_ge(st_r, t + 1)
                nc.vector.tensor_copy(tile(stats, t), st[j][:, :])

            def step(k, j):
                if there(k - 2, NT):
                    residual(k - 2, j)
                if there(k + 2, NT):
                    softmax_in(k + 2, j)
                if there(k + 4, NT):
                    norm(k + 4, j)
                if there(k - 2, NT):
                    statistics(k - 2, j)
                if there(k + 2, NT):
                    sums(k + 2, j)

            in_steps(nc.vector, NT, 4, 2, step)

        @block.gpsimd
        def _(pool):
            def normalise(t, j):
                pool.wait_ge(ri_r, t + 1)
                for g, (lo, hi) in enumerate(groups):
                    part = sc[j][:, :, lo:hi]
                    last = nc.gpsimd.tensor_tensor(part, part, ri[:, j, :, g].unsqueeze(2).to_broadcast([P, H, hi - lo]),
                                                   ALU.mult)
                last.then_inc(prob_r, 1)

            def rest_p(t, j):
                pool.wait_ge(pf_r, 2 * t + 2)
                pool.wait_ge(phi_r, 2 * t + 2)
                need(pool, y_r, t - 1)
                nc.gpsimd.tensor_tensor(pT_lo[j][:, :, :], pT[:, :, :], pT_hi[j][:, :, :], ALU.subtract).then_inc(plo_r, 1)

            def rest_x(t, j):
                pool.wait_ge(xf_r, t + 1)
                pool.wait_ge(xhi_r, t + 1)
                need(pool, sc_r, t - 1)
                nc.gpsimd.tensor_tensor(xnT_lo[j][:, :, :], xnT[:, :, :], xnT_hi[j][:, :, :], ALU.subtract).then_inc(xlo_r, 1)

            def add_bias(t):
                pool.wait_ge(xn_r, t + 1)
                nc.gpsimd.tensor_tensor(tile(x_res, t), tile(x_res, t), bias[:, :], ALU.add).then_inc(xb_r, 1)

            def step(k, j):
                if there(k + 3, NT):
                    rest_x(k + 3, 1 - j)
                if there(k + 2, NT):
                    add_bias(k + 2)
                if there(k + 1, NT):
                    normalise(k + 1, 1 - j)
                if there(k, NT):
                    rest_p(k, j)

            pool.wait_ge(bias_s, 16)
            in_steps(nc.gpsimd, NT, 3, 1, step)


def quantise_weights(nc, w_gate, w_up, w_down, WgT, WuT, WdT, ident):
    NB = FF * D // (P * QB)
    with Scope(nc, "qw") as s:
        w = [s.sb(f"w{i}", [P, NB, QB]) for i in range(3)]
        am, sc, rs = s.sb("am", [P, NB]), s.sb("sc", [P, NB]), s.sb("rs", [P, NB])
        ring = s.ps("ring", [P, 4, CH])
        loaded = [s.sem(f"loaded{i}") for i in range(3)]
        c, ready, made, moved = s.sem("c"), s.sem("ready"), s.sem("made"), s.sem("moved")
        block = s.block()

        @block.sync
        def _(sp):
            for i, src in enumerate((w_gate, w_up, w_down)):
                sp.dma_start(w[i][:, :, :].rearrange("p (o b) q -> p o (b q)", o=src.shape[0] // P),
                             src.rearrange("(o p) i -> p o i", p=P)).then_inc(loaded[i], 16)

        @block.vector
        def _(dve):
            n = [0]

            def then(ins):
                n[0] += 1
                ins.then_inc(c, 1)
                dve.wait_ge(c, n[0])

            for i in range(3):
                dve.wait_ge(loaded[i], 16)
                wi, per = w[i][:, :, :], [P, NB, QB]
                then(nc.vector.tensor_reduce(am[:, :], wi, AX.X, ALU.max, apply_absolute_value=True))
                then(nc.vector.tensor_scalar(sc[:, :], am[:, :], 1.0 / 7.0, 1e-12, ALU.mult, ALU.max))
                then(nc.vector.reciprocal(rs[:, :], sc[:, :]))
                then(nc.vector.tensor_tensor(wi, wi, rs[:, :].unsqueeze(2).to_broadcast(per), ALU.mult))
                then(nc.vector.tensor_scalar(wi, wi, MAGIC, MAGIC, ALU.add, ALU.subtract))
                then(nc.vector.tensor_scalar(wi, wi, 7.0, -8.0, ALU.min, ALU.max))
                nc.vector.tensor_tensor(wi, wi, sc[:, :].unsqueeze(2).to_broadcast(per), ALU.mult).then_inc(ready, 1)
            m = 0
            for i, dst in enumerate((WgT, WuT)):
                for g in range(3):
                    m += 1
                    dve.wait_ge(made, m)
                    nc.vector.tensor_copy(dst[:, :, 2 * g * P:(2 * g + 2) * P],
                                          ring[:, (m - 1) % 4, :].rearrange("p (d n) -> p d n", d=DT)).then_inc(moved, 1)
            for g in range(3):
                m += 1
                dve.wait_ge(made, m)
                nc.vector.tensor_copy(WdT[:, 2 * g:2 * g + 2, :], ring[:, (m - 1) % 4, :]).then_inc(moved, 1)

        @block.tensor
        def _(pe):
            m = 0
            for i in range(3):
                pe.wait_ge(ready, i + 1)
                src = w[i][:, :, :].rearrange("p (o b) q -> p o (b q)", o=DT if i == 2 else FT)
                for g in range(3):
                    if m >= 4:
                        pe.wait_ge(moved, m - 3)
                    for a in range(2):
                        for b in range(2):
                            if i < 2:
                                blk = src[:, 2 * g + b, a * P:(a + 1) * P]
                            else:
                                blk = src[:, b, (2 * g + a) * P:(2 * g + a + 1) * P]
                            last = nc.tensor.transpose(ring[:, m % 4, (2 * a + b) * P:(2 * a + b + 1) * P], blk, ident[:, :])
                    last.then_inc(made, 1)
                    m += 1


def quantise_input(nc, x_res, mv, rstd, scale_x, xqT, ident):
    TC = CH // P
    with Scope(nc, "qx") as s:
        xn = [s.sb(f"xn{j}", [P, TC, D]) for j in range(2)]
        am, top, gm, inv = s.sb("am", [P, NC]), s.sb("top", [P, 1]), s.sb("gm", [P, 1]), s.sb("inv", [P, 1])
        ps = [s.ps(f"ps{j}", [P, DT, CH]) for j in range(2)]
        c, xn_r, am_r, top_r, gm_r, t_r, e_r, m_r = (
            s.sem(n) for n in ("c", "xn_r", "am_r", "top_r", "gm_r", "t_r", "e_r", "m_r"))
        block = s.block()

        @block.vector
        def _(dve):
            def norm(g, j):
                need(dve, t_r, g - 1)
                for i in range(TC):
                    t = TC * g + i
                    last = nc.vector.tensor_scalar(xn[j][:, i, :], x_res[:, bass.ds(t, 1), :].rearrange("p a d -> p (a d)"),
                                                   mv[:, bass.ds(t, 1), 0:1].rearrange("p a b -> p (a b)"),
                                                   rstd[:, bass.ds(t, 1)], ALU.subtract, ALU.mult)
                last.then_inc(xn_r, 1)
                dve.wait_ge(xn_r, g + 1)
                nc.vector.tensor_reduce(am[:, bass.ds(g, 1)], xn[j][:, :, :], AX.XY, ALU.max,
                                        apply_absolute_value=True).then_inc(am_r, 1)

            for j in range(2):
                norm(j, j)
            with nc.vector.Fori(1, NC // 2, 1) as i:
                for j in range(2):
                    norm(2 * i + j, j)
            dve.wait_ge(am_r, NC)
            nc.vector.tensor_reduce(top[:, :], am[:, :], AX.X, ALU.max).then_inc(top_r, 1)
            dve.wait_ge(gm_r, 1)
            nc.vector.tensor_scalar(scale_x[:, :], gm[:, :], 1.0 / QACT, 1e-12, ALU.mult, ALU.max).then_inc(c, 1)
            dve.wait_ge(c, 1)
            nc.vector.reciprocal(inv[:, :], scale_x[:, :]).then_inc(c, 1)
            dve.wait_ge(c, 2)
            dve.wait_ge(e_r, NC)
            for n in range(4):
                part = xqT[:, :, n * (T // 4):(n + 1) * (T // 4)]
                nc.vector.tensor_scalar(part, part, inv[:, 0:1], MAGIC, ALU.mult, ALU.add).then_inc(m_r, 1)
            for n in range(4):
                part = xqT[:, :, n * (T // 4):(n + 1) * (T // 4)]
                dve.wait_ge(m_r, n + 1)
                nc.vector.tensor_scalar(part, part, MAGIC, None, ALU.subtract)

        @block.gpsimd
        def _(pool):
            pool.wait_ge(top_r, 1)
            nc.gpsimd.partition_all_reduce(gm[:, :], top[:, :], P, RMAX).then_inc(gm_r, 1)

        @block.tensor
        def _(pe):
            def turn(g, j):
                pe.wait_ge(xn_r, g + 1)
                need(pe, e_r, g - 1)
                for d in range(DT):
                    for i in range(TC):
                        last = nc.tensor.transpose(ps[j][:, d, i * P:(i + 1) * P], xn[j][:, i, d * P:(d + 1) * P],
                                                   ident[:, :])
                last.then_inc(t_r, 1)

            for j in range(2):
                turn(j, j)
            with nc.tensor.Fori(1, NC // 2, 1) as i:
                for j in range(2):
                    turn(2 * i + j, j)

        @block.scalar
        def _(act):
            with nc.scalar.Fori(0, NC // 2, 1) as i:
                for j in range(2):
                    act.wait_ge(t_r, 2 * i + j + 1)
                    nc.scalar.copy(xqT[:, :, bass.ds((2 * i + j) * CH, CH)], ps[j][:, :, :]).then_inc(e_r, 1)


def gated_mlp(nc, x_res, stats, scale_x, xqT, WgT, WuT, WdT, up_dram, gate):
    HF = FT // 2
    U = HF * CH
    NU = 2 * NC

    with Scope(nc, "gm") as s:
        gmax, umax, pmax = s.sb("gmax", [P, NC]), s.sb("umax", [P, NU]), s.sb("pmax", [P, NU])
        red = s.sb("red", [P, 3])
        allr = s.sb("allr", [P, 3])
        sc = s.sb("sc", [P, 8])
        SG, SU, SP, IU, IP, IG = range(6)
        stg = [s.sb(f"stg{j}", [P, U]) for j in range(2)]
        gq = [s.sb(f"gq{j}", [P, U], I16) for j in range(2)]
        sq = [s.sb(f"sq{j}", [P, U], U16) for j in range(2)]
        bank = [s.ps(f"bank{i}", [P, CH]) for i in range(FT)]
        with Scope(nc, "gu") as z:
            g_mm, g_ev, gm_s, c = z.sem("g_mm"), z.sem("g_ev"), z.sem("gm_s"), z.sem("c")
            u_mm, u_ev, u_red = z.sem("u_mm"), z.sem("u_ev"), z.sem("u_red")
            u_st = [z.sem(f"u_st{h}") for h in range(2)]
            gq_r, sig_r, sq_r, pr_r = z.sem("gq_r"), z.sem("sig_r"), z.sem("sq_r"), z.sem("pr_r")
            gred, gall, sg_r, pm_s = z.sem("gred"), z.sem("gall"), z.sem("sg_r"), z.sem("pm_s")
            block = z.block()

            def unit(u):
                return gate[:, bass.ds(u * U, U)]

            @block.tensor
            def _(pe):
                def half(w, h, c0, mm):
                    for i in range(HF):
                        o = h * HF + i
                        for d in range(DT):
                            last = nc.tensor.matmul(bank[o][:, :], w[:, d, o * P:(o + 1) * P],
                                                    xqT[:, d, bass.ds(c0, CH)], start=(d == 0), stop=(d == DT - 1))
                        last.then_inc(mm, 1)

                for h in range(2):
                    half(WgT, h, 0, g_mm)
                with nc.tensor.Fori(1, NC, 1) as k:
                    for h in range(2):
                        pe.wait_ge(g_ev, FT * (k - 1) + HF * (h + 1))
                        half(WgT, h, k * CH, g_mm)
                for h in range(2):
                    pe.wait_ge(g_ev, FT * (NC - 1) + HF * (h + 1))
                    half(WuT, h, 0, u_mm)
                with nc.tensor.Fori(1, NC, 1) as k:
                    for h in range(2):
                        pe.wait_ge(u_ev, FT * (k - 1) + HF * (h + 1))
                        half(WuT, h, k * CH, u_mm)

            @block.scalar
            def _(act):
                with nc.scalar.Fori(0, NC, 1) as k:
                    for o in range(FT):
                        act.wait_ge(g_mm, FT * k + o + 1)
                        nc.scalar.activation(gate[:, bass.ds((FT * k + o) * CH, CH)], bank[o][:, :], ACT.Copy,
                                             scale=scale_x[:, 0:1]).then_inc(g_ev, 1)

                def up_half(k, h, first):
                    if not first:
                        act.wait_ge(u_st[h], 16 * k)
                        act.wait_ge(u_red, 2 * k + h - 1)
                    for i in range(HF):
                        act.wait_ge(u_mm, FT * k + h * HF + i + 1)
                        nc.scalar.activation(stg[h][:, i * CH:(i + 1) * CH], bank[h * HF + i][:, :], ACT.Copy,
                                             scale=scale_x[:, 0:1]).then_inc(u_ev, 1)

                def sigmoid(u, h):
                    act.wait_ge(gq_r, u + 1)
                    nc.scalar.activation(unit(u), gq[h][:, :], ACT.Sigmoid, scale=sc[:, SG:SG + 1]).then_inc(sig_r, 1)

                act.wait_ge(sg_r, 2)
                for h in range(2):
                    up_half(0, h, True)
                    sigmoid(h, h)
                with nc.scalar.Fori(1, NC, 1) as k:
                    for h in range(2):
                        up_half(k, h, False)
                        sigmoid(2 * k + h, h)

            @block.vector
            def _(dve):
                with nc.vector.Fori(0, NC, 1) as k:
                    dve.wait_ge(g_ev, FT * (k + 1))
                    nc.vector.tensor_reduce(gmax[:, bass.ds(k, 1)], gate[:, bass.ds(k * FT * CH, FT * CH)], AX.X, ALU.max,
                                            apply_absolute_value=True).then_inc(gm_s, 1)
                dve.wait_ge(gm_s, NC)
                nc.vector.tensor_reduce(red[:, 0:1], gmax[:, :], AX.X, ALU.max).then_inc(gred, 1)
                dve.wait_ge(gall, 1)
                nc.vector.tensor_scalar(sc[:, SG:SG + 1], allr[:, 0:1], 1.0 / QACT, 1e-12, ALU.mult, ALU.max).then_inc(sg_r, 1)
                dve.wait_ge(sg_r, 1)
                nc.vector.reciprocal(sc[:, IG:IG + 1], sc[:, SG:SG + 1]).then_inc(sg_r, 1)
                dve.wait_ge(sg_r, 2)

                def levels(u, h):
                    nc.vector.tensor_scalar(gq[h][:, :], unit(u), sc[:, IG:IG + 1], None, ALU.mult).then_inc(gq_r, 1)

                def sig_levels(u, h):
                    dve.wait_ge(sig_r, u + 1)
                    nc.vector.tensor_scalar(sq[h][:, :], unit(u), 65536.0, 65535.0, ALU.mult, ALU.min).then_inc(sq_r, 1)

                def product(u, h):
                    dve.wait_ge(sq_r, u + 1)
                    nc.vector.tensor_tensor(unit(u), gq[h][:, :], sq[h][:, :], ALU.mult).then_inc(pr_r, 1)

                def up_max(k, h):
                    dve.wait_ge(u_ev, FT * k + HF * (h + 1))
                    nc.vector.tensor_reduce(umax[:, bass.ds(2 * k + h, 1)], stg[h][:, :], AX.X, ALU.max,
                                            apply_absolute_value=True).then_inc(u_red, 1)

                def prod_max(u):
                    dve.wait_ge(pr_r, u + 1)
                    nc.vector.tensor_reduce(pmax[:, bass.ds(u, 1)], unit(u), AX.X, ALU.max,
                                            apply_absolute_value=True).then_inc(pm_s, 1)

                levels(0, 0)
                levels(1, 1)
                for h in range(2):
                    up_max(0, h)
                    sig_levels(h, h)
                    product(h, h)
                with nc.vector.Fori(1, NC, 1) as k:
                    for h in range(2):
                        levels(2 * k + h, h)
                        up_max(k, h)
                        sig_levels(2 * k + h, h)
                        prod_max(2 * k + h - 2)
                        product(2 * k + h, h)
                for u in (NU - 2, NU - 1):
                    prod_max(u)
                dve.wait_ge(pm_s, NU)
                dve.wait_ge(u_red, NU)
                nc.vector.tensor_reduce(red[:, 1:2], umax[:, :], AX.X, ALU.max)
                nc.vector.tensor_reduce(red[:, 2:3], pmax[:, :], AX.X, ALU.max).then_inc(gred, 1)
                dve.wait_ge(gall, 2)
                nc.vector.tensor_scalar(sc[:, SU:SU + 1], allr[:, 1:2], 1.0 / QACT, 1e-12, ALU.mult, ALU.max)
                nc.vector.tensor_scalar(sc[:, SP:SP + 1], allr[:, 2:3], sc[:, SG:SG + 1], 1.0 / (65536.0 * QACT),
                                        ALU.mult, ALU.mult).then_inc(c, 1)
                dve.wait_ge(c, 1)
                nc.vector.tensor_scalar(sc[:, SP:SP + 1], sc[:, SP:SP + 1], 1e-12, None, ALU.max).then_inc(c, 1)
                dve.wait_ge(c, 2)
                nc.vector.reciprocal(sc[:, IU:IU + 1], sc[:, SU:SU + 1])
                nc.vector.reciprocal(sc[:, IP:IP + 1], sc[:, SP:SP + 1]).then_inc(c, 1)
                dve.wait_ge(c, 3)
                nc.vector.tensor_scalar(sc[:, IP:IP + 1], sc[:, IP:IP + 1], sc[:, SG:SG + 1], 1.0 / 65536.0,
                                        ALU.mult, ALU.mult)

            @block.gpsimd
            def _(pool):
                pool.wait_ge(gred, 1)
                nc.gpsimd.partition_all_reduce(allr[:, 0:1], red[:, 0:1], P, RMAX).then_inc(gall, 1)
                pool.wait_ge(gred, 2)
                nc.gpsimd.partition_all_reduce(allr[:, 1:3], red[:, 1:3], P, RMAX).then_inc(gall, 1)

            @block.sync
            def _(sp):
                with nc.sync.Fori(0, NC, 1) as k:
                    for h in range(2):
                        sp.wait_ge(u_ev, FT * k + HF * (h + 1))
                        sp.dma_start(up_dram[bass.ds(2 * k + h, 1), :, :].rearrange("a p n -> (a p) n"),
                                     stg[h][:, :]).then_inc(u_st[h], 16)
                for h in range(2):
                    sp.wait_ge(u_st[h], 16 * NC)

        with Scope(nc, "go") as z:
            ld = [z.sem(f"ld{j}") for j in range(2)]
            um_r, uq_r, gq_r, o_r, om_s, gred, gall, c = (
                z.sem(n) for n in ("um_r", "uq_r", "gq_r", "o_r", "om_s", "gred", "gall", "c"))
            uf = [xqT[:, h, 0:U] for h in range(2)]
            block = z.block()

            @block.sync
            def _(sp):
                for h in range(2):
                    sp.dma_start(stg[h][:, :], up_dram[h, :, :]).then_inc(ld[h], 16)
                with nc.sync.Fori(1, NC, 1) as k:
                    for h in range(2):
                        sp.wait_ge(um_r, 2 * k + h - 1)
                        sp.dma_start(stg[h][:, :], up_dram[bass.ds(2 * k + h, 1), :, :].rearrange("a p n -> (a p) n")
                                     ).then_inc(ld[h], 16)

            @block.scalar
            def _(act):
                def up_levels(k, h, first):
                    u = 2 * k + h
                    act.wait_ge(ld[h], 16 * (k + 1))
                    if not first:
                        act.wait_ge(o_r, u - 1)
                    nc.scalar.activation(uf[h], stg[h][:, :], ACT.Copy, scale=sc[:, IU:IU + 1],
                                         bias=MAGIC).then_inc(um_r, 1)
                    act.wait_ge(um_r, u + 1)
                    nc.scalar.activation(uf[h], uf[h], ACT.Copy, bias=-MAGIC).then_inc(uq_r, 1)

                for h in range(2):
                    up_levels(0, h, True)
                with nc.scalar.Fori(1, NC, 1) as k:
                    for h in range(2):
                        up_levels(k, h, False)

            @block.vector
            def _(dve):
                def levels(u, h):
                    nc.vector.tensor_scalar(gq[h][:, :], unit(u), sc[:, IP:IP + 1], None, ALU.mult).then_inc(gq_r, 1)

                def product(u, h):
                    dve.wait_ge(gq_r, u + 1)
                    dve.wait_ge(uq_r, u + 1)
                    nc.vector.tensor_tensor(unit(u), gq[h][:, :], uf[h], ALU.mult).then_inc(o_r, 1)

                def o_max(u):
                    dve.wait_ge(o_r, u + 1)
                    nc.vector.tensor_reduce(pmax[:, bass.ds(u, 1)], unit(u), AX.X, ALU.max,
                                            apply_absolute_value=True).then_inc(om_s, 1)

                for h in range(2):
                    levels(h, h)
                for h in range(2):
                    product(h, h)
                with nc.vector.Fori(1, NC, 1) as k:
                    for h in range(2):
                        dve.wait_ge(o_r, 2 * k + h - 1)
                        levels(2 * k + h, h)
                        o_max(2 * k + h - 2)
                        product(2 * k + h, h)
                for u in (NU - 2, NU - 1):
                    o_max(u)
                dve.wait_ge(om_s, NU)
                nc.vector.tensor_reduce(red[:, 0:1], pmax[:, :], AX.X, ALU.max).then_inc(gred, 1)
                dve.wait_ge(gall, 1)
                nc.vector.tensor_scalar(sc[:, 6:7], sc[:, SU:SU + 1], sc[:, SP:SP + 1], None, ALU.mult).then_inc(c, 1)
                dve.wait_ge(c, 1)
                nc.vector.tensor_scalar(sc[:, 7:8], allr[:, 0:1], sc[:, 6:7], 1.0 / QACT, ALU.mult, ALU.mult).then_inc(c, 1)
                dve.wait_ge(c, 2)
                nc.vector.tensor_scalar(sc[:, 7:8], sc[:, 7:8], 1e-12, None, ALU.max).then_inc(c, 1)
                dve.wait_ge(c, 3)
                nc.vector.reciprocal(sc[:, IG:IG + 1], sc[:, 7:8]).then_inc(c, 1)
                dve.wait_ge(c, 4)
                nc.vector.tensor_scalar(sc[:, IG:IG + 1], sc[:, IG:IG + 1], sc[:, 6:7], None, ALU.mult)

            @block.gpsimd
            def _(pool):
                pool.wait_ge(gred, 1)
                nc.gpsimd.partition_all_reduce(allr[:, 0:1], red[:, 0:1], P, RMAX).then_inc(gall, 1)

        with Scope(nc, "gd") as z:
            o_mg, o_lv, mm, ev, st_r = (z.sem(n) for n in ("o_mg", "o_lv", "mm", "ev", "st_r"))
            new_c = z.sem("new_c")
            new = [x[:, 0:D] for x in stg]
            st = [z.sb(f"st{j}", [P, 6]) for j in range(2)]
            lv = [xqT[:, j, 0:FT * CH].rearrange("p (o n) -> p o n", o=FT) for j in range(DT)]
            block = z.block()
            TC = CH // P

            def tile(buf, t):
                return buf[:, bass.ds(t, 1), :].rearrange("p a d -> p (a d)")

            @block.scalar
            def _(act):
                with nc.scalar.Fori(0, NT // 2, 1) as i:
                    for j in range(2):
                        act.wait_ge(ev, 2 * i + j + 1)
                        nc.scalar.copy(tile(x_res, 2 * i + j), new[j]).then_inc(new_c, 1)

            @block.vector
            def _(dve):
                def levels(k, j, first):
                    if not first:
                        dve.wait_ge(mm, TC * (k - 1))
                    nc.vector.tensor_scalar(lv[j], gate[:, bass.ds(k * FT * CH, FT * CH)].rearrange("p (o n) -> p o n", o=FT),
                                            sc[:, IG:IG + 1], MAGIC, ALU.mult, ALU.add).then_inc(o_mg, 1)
                    dve.wait_ge(o_mg, k + 1)
                    nc.vector.tensor_scalar(lv[j], lv[j], MAGIC, None, ALU.subtract).then_inc(o_lv, 1)

                def residual(k, i, first=False):
                    t, j = TC * k + i, i % 2
                    dve.wait_ge(mm, t + 1)
                    if not (first and i < 2):
                        dve.wait_ge(new_c, t - 1)
                    nc.vector.scalar_tensor_tensor(out=new[j], in0=bank[j][:, 0:D], scalar=sc[:, 7:8],
                                                   in1=tile(x_res, t), op0=ALU.mult, op1=ALU.add).then_inc(ev, 1)
                    dve.wait_ge(ev, t + 1)
                    nc.vector.bn_stats(st[j][:, :], new[j]).then_inc(st_r, 1)
                    dve.wait_ge(st_r, t + 1)
                    nc.vector.tensor_copy(tile(stats, t), st[j][:, :])

                levels(0, 0, True)
                levels(1, 1, True)
                for i in range(TC):
                    residual(0, i, True)
                levels(2, 0, False)
                for i in range(TC):
                    residual(1, i)
                with nc.vector.Fori(1, NC // 2 - 1, 1) as m:
                    for j in range(2):
                        levels(2 * m + j + 1, 1 - j, False)
                        for i in range(TC):
                            residual(2 * m + j, i)
                levels(NC - 1, 1, False)
                for j in range(2):
                    for i in range(TC):
                        residual(NC - 2 + j, i)

            @block.tensor
            def _(pe):
                def chunk(k, j, first):
                    pe.wait_ge(o_lv, k + 1)
                    for i in range(TC):
                        t = TC * k + i
                        if not (first and i < 2):
                            pe.wait_ge(ev, t - 1)
                        for o in range(FT):
                            last = nc.tensor.matmul(bank[i % 2][:, 0:D], lv[j][:, o, i * P:(i + 1) * P], WdT[:, o, :],
                                                    start=(o == 0), stop=(o == FT - 1))
                        last.then_inc(mm, 1)

                chunk(0, 0, True)
                chunk(1, 1, False)
                with nc.tensor.Fori(1, NC // 2, 1) as m:
                    for j in range(2):
                        chunk(2 * m + j, j, False)


def route(nc, w, b1T, x_res, mv, rstd, ident, w1, w2, ssq, unscale, xs, acc, table):
    TK = 8
    NK = NT // TK
    NB = 4
    assert E == 2 * NK
    with Scope(nc, "rt") as s:
        wr = s.sb("wr", [P, DT, E])
        brb = s.sb("brb", [P, E])
        b1r = s.sb("b1r", [E * HT, P])
        xn = s.sb("xn", [P, 2, D])
        xt = [s.sb(f"xt{j}", [P, DT, P]) for j in range(2)]
        scores = s.sb("scores", [P, TK, E])
        top = s.sb("top", [P, TK, 8])
        idx = s.sb("idx", [P, TK, 8], U32)
        idf = s.sb("idf", [P, TK, 2])
        eid = s.sb("eid", [P, E])
        oh = s.sb("oh", [P, 2, TK, E])
        ind, tot, incl = s.sb("ind", [P, TK, E]), s.sb("tot", [P, TK, E]), s.sb("incl", [P, TK, E])
        run = s.sb("run", [P, E])
        ones = s.sb("ones", [P, P])
        tri = s.sb("tri", [P, P])
        wt = s.sb("wt", [P, 2, TK])
        meta = s.sb("meta", [P, TK, 2, 2])
        posf = s.sb("posf", [P, TK, 2])
        pos = s.sb("pos", [P, TK, 2], U32)
        tok = s.sb("tok", [P, NT], U32)
        base = s.sb("base", [P, E])
        stage = [s.sb(f"stage{j}", [P, WN // 2]) for j in range(4)]
        bm, bmr = s.sb("bm", [P, 3, E]), s.sb("bmr", [P, 3, E])
        wpow = s.sb("wpow", [P, 2, E])
        wsc = s.sb("wsc", [P, 2, E])
        hp, hs = s.sb("hp", [P, E]), s.sb("hs", [P, E])
        pay = [s.sb(f"pay{j}", [P, 2, ROW]) for j in range(NB)]
        row_i = [s.sb(f"row{j}", [P, 2], U32) for j in range(NB)]
        pad = s.sb("pad", [P, ROW])
        ntf, nti, jump = s.sb("ntf", [P, E]), s.sb("nti", [P, E], I32), s.sb("jump", [P, E])
        cum = s.sb("cum", [P, E])
        tid = s.sb("tid", [P, NTL])
        ge = s.sb("ge", [P, NTL, E])
        tf = s.sb("tf", [P, 2, NTL])
        cnt = s.sb("cnt", [P, E], I32)
        ps_t = [s.ps(f"ps_t{j}", [P, CH]) for j in range(2)]
        ps_r = [s.ps(f"ps_r{j}", [P, CH]) for j in range(2)]
        ps_c = [s.ps(f"ps_c{j}", [P, CH]) for j in range(2)]
        (r_in, cst, xn_r, t_r, xt_r, sc_mm, sc_r, c, e_r, d_r, b1_t, b1_c, ind_r, rank_mm, cnt_r, padded,
         pay0, pay1, meta_r, acc_in) = (s.sem(n) for n in (
            "r_in", "cst", "xn_r", "t_r", "xt_r", "sc_mm", "sc_r", "c", "e_r", "d_r", "b1_t", "b1_c", "ind_r",
            "rank_mm", "cnt_r", "padded", "pay0", "pay1", "meta_r", "acc_in"))
        sent = [s.sem(f"sent{j}") for j in range(NB)]
        begun, arrived = s.sem("begun"), s.sem("arrived")
        half_in = [s.sem(f"half_in{j}") for j in range(4)]
        wsc_r, whi_r, wlo_r, bm_r, bmr_r, link, linked = (
            s.sem(n) for n in ("wsc_r", "whi_r", "wlo_r", "bm_r", "bmr_r", "link", "linked"))
        CONSTS = 10
        block = s.block()

        def tile(buf, t):
            return buf[:, bass.ds(t, 1), :].rearrange("p a d -> p (a d)")

        def split_half(part, e, m, h):
            return (w1, w2)[m][part][:, bass.ds(e, 1), h * (WN // 2):(h + 1) * (WN // 2)].rearrange("p a n -> p (a n)")

        def walk(eng, tile_step, chunk_step, all_counted=None):
            for i in range(TK):
                tile_step(i, None, i, (0, i // 4, i // 2 % 2) if i % 2 else None)
            chunk_step(0)
            with eng.Fori(1, NK, 1) as c:
                for i in range(TK):
                    tile_step(i, TK * (c - 1) + i, TK * c + i, (2 * c - 1 + i // 4, i // 2 % 2, i % 2))
                chunk_step(c)
            if all_counted:
                all_counted()
            for i in range(TK):
                tile_step(i, NT - TK + i, None, (E - 1, i // 4, i // 2 % 2) if i % 2 else None)

        @block.sync
        def _(sp):
            sp.dma_start(wr[:, :, :], w["L1_ffn_Wr"].rearrange("(t p) e -> p t e", p=P)).then_inc(r_in, 16)
            sp.dma_start(brb[:, :], w["L1_ffn_br"].unsqueeze(0).to_broadcast([P, E])).then_inc(r_in, 16)
            sp.dma_start(b1r[:, :], w["L1_ffn_b1"].rearrange("e (t p) -> (e t) p", p=P)).then_inc(r_in, 16)
            def load_matrix(e, m):
                src = (w["L1_ffn_W1"], w["L1_ffn_W2"])[m]
                rows = src.shape[1] // 2
                for h in range(2):
                    q = 4 * e + 2 * m + h
                    need(sp, wlo_r, q - 3)
                    sp.dma_start(stage[2 * m + h][:, :].rearrange("p (t n) -> p t n", n=src.shape[2]),
                                 src[bass.ds(e, 1), h * rows:(h + 1) * rows, :].rearrange("o (t p) n -> p (o t) n", p=P)
                                 ).then_inc(half_in[2 * m + h], 16)

            for j in range(2):
                load_matrix(0, j)
            with nc.sync.Fori(1, 2, 1) as e:
                for j in range(2):
                    load_matrix(e, j)
            for g in range(B):
                sp.dma_start(acc[g * S:(g + 1) * S, :].rearrange("(p t) d -> p t d", p=P),
                             x_res[:, g * NT // B:(g + 1) * NT // B, :]).then_inc(acc_in, 16)
            with nc.sync.Fori(2, E, 1) as e:
                for j in range(2):
                    load_matrix(e, j)
            sp.wait_ge(cst, CONSTS)
            sp.dma_start(acc[T:T + P, :], pad[:, 0:D]).then_inc(acc_in, 16)
            sp.dma_start(xs[E * CAP:E * CAP + P, :], pad[:, :]).then_inc(padded, 16)
            sp.wait_ge(cnt_r, 1)
            for e in range(E):
                n = nc.sync.value_load(cnt[0:1, e:e + 1], min_val=0, max_val=T)
                sp.dma_start(xs[bass.ds(n + e * CAP, P), :], pad[:, :]).then_inc(padded, 16)
            sp.wait_ge(padded, 16 * (E + 1))
            sp.wait_ge(acc_in, 16 * 5)

        @block.gpsimd
        def _(pool):
            g = nc.gpsimd
            pool.wait_ge(bm_r, 1)
            g.partition_all_reduce(bmr[:, :, :], bm[:, :, :], P, RMAX).then_inc(bmr_r, 1)
            g.iota(eid[:, :], pattern=[[1, E]], base=0, channel_multiplier=0,
                   allow_small_or_imprecise_dtypes=True).then_inc(cst, 1)
            g.iota(base[:, :], pattern=[[CAP, E]], base=0, channel_multiplier=0,
                   allow_small_or_imprecise_dtypes=True).then_inc(cst, 1)
            g.iota(tid[:, :], pattern=[[1, NTL]], base=0, channel_multiplier=0,
                   allow_small_or_imprecise_dtypes=True).then_inc(cst, 1)
            g.iota(tok[:, :].bitcast(I32), pattern=[[S, B], [1, NT // B]], base=0, channel_multiplier=NT // B).then_inc(cst, 1)
            g.memset(ones[:, :], 1.0).then_inc(cst, 1)
            g.memset(pad[:, 0:ROW - 1], 0.0).then_inc(cst, 1)
            g.iota(pad[:, ROW - 1:ROW].bitcast(I32), pattern=[[0, 1]], base=T, channel_multiplier=1).then_inc(cst, 1)
            g.memset(tri[:, :], 1.0).then_inc(cst, 1)
            pool.wait_ge(cst, 8)
            g.affine_select(out=tri[:, :], in_=tri[:, :], compare_op=ALU.is_gt, fill=0.0, base=0,
                            pattern=[[1, P]], channel_multiplier=-1).then_inc(cst, 1)
            g.memset(run[:, :], 0.0).then_inc(cst, 1)

            last_row = g.to_reg(E * CAP - 1)

            def send(t, j):
                pool.wait_ge(meta_r, t + 1)
                pool.wait_ge(pay0, t + 1)
                pool.wait_ge(pay1, t + 1)
                pool.sem_inc(begun, 1)
                for k in range(2):
                    g.indirect_dma_start(out=xs[:, :], out_offset=bass.IndirectOffsetOnAxis(ap=row_i[j][:, k:k + 1], axis=0),
                                         in_=pay[j][:, k, :], in_offset=None, bounds_check=last_row,
                                         oob_is_err=True).then_inc(sent[j], 16)

            with g.Fori(0, NT // NB, 1) as i:
                for j in range(NB):
                    send(NB * i + j, j)
            for j in range(NB):
                pool.wait_ge(sent[j], 32 * NT // NB)

        @block.tensor
        def _(pe):
            pe.wait_ge(r_in, 48)
            nc.tensor.transpose(ps_r[0][:, 0:E * HT], b1r[:, :], ident[0:E * HT, 0:E * HT]).then_inc(b1_t, 1)
            pe.wait_ge(b1_c, 1)

            def turn(t, j):
                pe.wait_ge(xn_r, t + 1)
                need(pe, xt_r, t - 1)
                for d in range(DT):
                    last = nc.tensor.transpose(ps_t[j][:, d * P:(d + 1) * P], xn[:, j, d * P:(d + 1) * P], ident[:, :])
                last.then_inc(t_r, 1)

            def score(t, j):
                pe.wait_ge(xt_r, t + 1)
                need(pe, sc_r, t - 1)
                for d in range(DT):
                    last = nc.tensor.matmul(ps_r[j][:, 0:E], xt[j][:, d, :], wr[:, d, :], start=(d == 0), stop=(d == DT - 1))
                last.then_inc(sc_mm, 1)

            def tile_step(i, r, t, half):
                if t is not None:
                    turn(t, i % 2)
                    if i >= 1:
                        score(t - 1, 1 - i % 2)

            def chunk_step(c):
                score(TK * c + TK - 1, 1)
                pe.wait_ge(ind_r, c + 1)
                pe.wait_ge(cst, CONSTS)
                nc.tensor.matmul(ps_c[0][:, 0:TK * E], tri[:, :], ind[:, :, :], start=True, stop=True).then_inc(rank_mm, 1)
                nc.tensor.matmul(ps_c[1][:, 0:TK * E], ones[:, :], ind[:, :, :], start=True, stop=True).then_inc(rank_mm, 1)

            walk(nc.tensor, tile_step, chunk_step)

        @block.scalar
        def _(act):
            def copy(t, j):
                act.wait_ge(t_r, t + 1)
                need(act, sc_mm, t - 1)
                nc.scalar.copy(xt[j][:, :, :], ps_t[j][:, 0:D].rearrange("p (d n) -> p d n", d=DT)).then_inc(xt_r, 1)

            def hi(e, m, h):
                act.wait_ge(half_in[2 * m + h], 16 * (e + 1))
                act.sem_inc(arrived, 1)
                nc.scalar.activation(split_half(0, e, m, h), stage[2 * m + h][:, :], ACT.Copy,
                                     scale=wsc[:, m, bass.ds(e, 1)]).then_inc(whi_r, 1)

            def copy_rows(t, j):
                act.wait_ge(pay0, t + 1)
                nc.scalar.copy(pay[j][:, 1, 0:D], pay[j][:, 0, 0:D]).then_inc(pay1, 1)

            def tile_step(i, r, t, half):
                if half:
                    hi(*half)
                if r is not None:
                    copy_rows(r, i % NB)
                if t is not None:
                    copy(t, i % 2)

            def chunk_step(c):
                act.wait_ge(d_r, c + 1)
                nc.scalar.activation(wt[:, 1, :], wt[:, 0, :], ACT.Exp).then_inc(e_r, 1)

            act.wait_ge(wsc_r, 1)
            walk(nc.scalar, tile_step, chunk_step)

        @block.vector
        def _(dve):
            v = nc.vector
            dve.wait_ge(r_in, 48)

            def layer_norm(dst, t):
                return v.tensor_scalar(dst, tile(x_res, t), mv[:, bass.ds(t, 1), 0:1].rearrange("p a b -> p (a b)"),
                                       rstd[:, bass.ds(t, 1)], ALU.subtract, ALU.mult)

            def norm(t, j):
                need(dve, t_r, t - 1)
                layer_norm(xn[:, j, :], t).then_inc(xn_r, 1)

            def score(t, i):
                dve.wait_ge(sc_mm, t + 1)
                v.tensor_tensor(scores[:, i, :], ps_r[i % 2][:, 0:E], brb[:, :], ALU.add).then_inc(sc_r, 1)

            dve.wait_ge(b1_t, 1)
            v.tensor_copy(b1T[:, :], ps_r[0][:, 0:E * HT]).then_inc(b1_c, 1)
            dve.wait_ge(b1_c, 1)
            halves = ssq[:, :].rearrange("p (m e h) -> p m e h", m=2, h=2)
            v.tensor_tensor(bm[:, 0:2, :], halves[:, :, :, 0], halves[:, :, :, 1], ALU.add)
            v.tensor_reduce(bm[:, 2, :], b1T[:, :].rearrange("p (e t) -> p e t", e=E), AX.X, ALU.max,
                            apply_absolute_value=True).then_inc(bm_r, 1)
            n = [0]

            def then(ins):
                n[0] += 1
                ins.then_inc(c, 1)
                dve.wait_ge(c, n[0])

            dve.wait_ge(bmr_r, 1)
            then(v.tensor_scalar(bm[:, 0:2, :], bmr[:, 0:2, :], 1e-30, None, ALU.max))
            then(v.tensor_scalar(wpow[:, :, :].bitcast(I32), bm[:, 0:2, :].bitcast(I32), 24, 23,
                                 ALU.logical_shift_right, ALU.logical_shift_left))
            then(v.reciprocal(wsc[:, :, :], wpow[:, :, :]))
            v.tensor_scalar(wsc[:, :, :], wsc[:, :, :], 2.0 ** (14 - 64), None, ALU.mult).then_inc(wsc_r, 1)
            then(v.tensor_scalar(hp[:, :], wpow[:, 0, :], 2.0 ** 65 * D, None, ALU.mult))
            then(v.tensor_tensor(hp[:, :], hp[:, :], bmr[:, 2, :], ALU.add))
            then(v.tensor_scalar(hp[:, :].bitcast(I32), hp[:, :].bitcast(I32), EXPONENT, None, ALU.bitwise_and))
            then(v.reciprocal(hs[:, :], hp[:, :]))
            then(v.tensor_scalar(hs[:, :], hs[:, :], 2.0 ** 14, None, ALU.mult))
            v.tensor_tensor(b1T[:, :].rearrange("p (e t) -> p e t", e=E), b1T[:, :].rearrange("p (e t) -> p e t", e=E),
                            hs[:, :].unsqueeze(2).to_broadcast([P, E, HT]), ALU.mult)
            then(v.tensor_scalar(unscale[:, 0, :], wpow[:, 0, :], 2.0 ** (64 - 14) / XN_SCALE, None, ALU.mult))
            v.tensor_tensor(unscale[:, 0, :], unscale[:, 0, :], hs[:, :], ALU.mult)
            then(v.tensor_scalar(unscale[:, 1, :], wpow[:, 1, :], 2.0 ** (64 - 14), None, ALU.mult))
            then(v.tensor_scalar(hp[:, :], hp[:, :], 2.0 ** -14, None, ALU.mult))
            v.tensor_tensor(unscale[:, 1, :], unscale[:, 1, :], hp[:, :], ALU.mult)

            def lo(e, m, h):
                dve.wait_ge(whi_r, 4 * e + 2 * m + h + 1)
                v.scalar_tensor_tensor(out=split_half(1, e, m, h), in0=stage[2 * m + h][:, :],
                                       scalar=wsc[:, m, bass.ds(e, 1)], in1=split_half(0, e, m, h),
                                       op0=ALU.mult, op1=ALU.subtract).then_inc(wlo_r, 1)

            def rows(t, i):
                j = i % NB
                if i >= NB:
                    dve.wait_ge(sent[j], 32 // NB * (t - j))
                layer_norm(pay[j][:, 0, 0:D], t).then_inc(pay0, 1)
                v.tensor_copy(pay[j][:, :, D:ROW], meta[:, i, :, :])
                v.tensor_copy(row_i[j][:, :], pos[:, i, :]).then_inc(meta_r, 1)

            def tile_step(i, r, t, half):
                if r is not None:
                    rows(r, i)
                if t is not None:
                    norm(t, i % 2)
                    if i >= 2:
                        score(t - 2, i - 2)
                if half:
                    lo(*half)

            LINKS = 15

            def chunk_step(c):
                for i in range(TK - 2, TK):
                    score(TK * c + i, i)
                dve.wait_ge(sc_r, TK * (c + 1))
                k = [0]

                def then(ins):
                    k[0] += 1
                    ins.then_inc(link, 1)
                    dve.wait_ge(link, LINKS * c + k[0])
                    dve.sem_inc(linked, 1)

                dve.sem_inc(linked, 1)
                for i in range(TK):
                    last = v.max(out=top[:, i, :], in_=scores[:, i, :])
                then(last)
                v.tensor_tensor(wt[:, 0, :], top[:, :, 1], top[:, :, 0], ALU.subtract).then_inc(d_r, 1)
                for i in range(TK):
                    last = v.max_index(out=idx[:, i, :], in_max=top[:, i, :], in_values=scores[:, i, :])
                then(last)
                then(v.tensor_copy(idf[:, :, :], idx[:, :, 0:2]))
                dve.wait_ge(cst, CONSTS)
                for n in range(2):
                    last = v.tensor_tensor(oh[:, n, :, :], idf[:, :, n].unsqueeze(2).to_broadcast([P, TK, E]),
                                           eid[:, :].unsqueeze(1).to_broadcast([P, TK, E]), ALU.is_equal)
                then(last)
                v.tensor_tensor(ind[:, :, :], oh[:, 0, :, :], oh[:, 1, :, :], ALU.add).then_inc(ind_r, 1)
                dve.wait_ge(e_r, c + 1)
                dve.sem_inc(linked, 1)
                then(v.tensor_scalar(wt[:, 0, :], wt[:, 1, :], 1.0, None, ALU.add))
                then(v.reciprocal(meta[:, :, 0, 0], wt[:, 0, :]))
                v.tensor_tensor(meta[:, :, 1, 0], wt[:, 1, :], meta[:, :, 0, 0], ALU.mult)
                for n in range(2):
                    v.tensor_copy(meta[:, :, n, 1].bitcast(U32), tok[:, bass.ds(TK * c, TK)])
                dve.wait_ge(rank_mm, 2 * (c + 1))
                dve.sem_inc(linked, 1)
                then(v.tensor_copy(tot[:, :, :], ps_c[1][:, 0:TK * E].rearrange("p (t e) -> p t e", e=E)))
                for e in range(E):
                    last = v.tensor_tensor_scan(incl[:, :, e], ones[:, 0:TK], tot[:, :, e], run[:, e:e + 1],
                                                ALU.mult, ALU.add)
                then(last)
                v.tensor_copy(run[:, :], incl[:, TK - 1, :])
                then(v.tensor_tensor(tot[:, :, :], incl[:, :, :], tot[:, :, :], ALU.subtract))
                then(v.tensor_tensor(tot[:, :, :], ps_c[0][:, 0:TK * E].rearrange("p (t e) -> p t e", e=E), tot[:, :, :],
                                     ALU.add))
                then(v.tensor_tensor(tot[:, :, :], tot[:, :, :], base[:, :].unsqueeze(1).to_broadcast([P, TK, E]), ALU.add))
                for n in range(2):
                    last = v.tensor_tensor(oh[:, n, :, :], oh[:, n, :, :], tot[:, :, :], ALU.mult)
                then(last)
                for n in range(2):
                    last = v.tensor_reduce(posf[:, :, n], oh[:, n, :, :], AX.X, ALU.add)
                then(last)
                then(v.tensor_copy(pos[:, :, :], posf[:, :, :]))
                assert k[0] <= LINKS
                dve.sem_inc(link, LINKS - k[0]) if k[0] < LINKS else None
                if not (isinstance(c, int) and c == 0):
                    for j in range(NB):
                        dve.wait_ge(sent[j], 32 * TK // NB * c)

            walk(v, tile_step, chunk_step, lambda: v.tensor_copy(cnt[:, :], run[:, :]).then_inc(cnt_r, 1))
            then(v.tensor_scalar(nti[:, :], run[:, :], float(P - 1), None, ALU.add))
            then(v.tensor_scalar(nti[:, :], nti[:, :], 7, None, ALU.logical_shift_right))
            then(v.tensor_copy(ntf[:, :], nti[:, :]))
            then(v.tensor_tensor_scan(cum[:, :], ones[:, 0:E], ntf[:, :], 0.0, ALU.mult, ALU.add))
            v.tensor_scalar(jump[:, :], ntf[:, :], -1.0, float(CAP // P), ALU.mult, ALU.add)
            then(v.tensor_tensor(ge[:, :, :], tid[:, :].unsqueeze(2).to_broadcast([P, NTL, E]),
                                 cum[:, :].unsqueeze(1).to_broadcast([P, NTL, E]), ALU.is_ge))
            then(v.tensor_reduce(tf[:, 1, :], ge[:, :, :], AX.X, ALU.add))
            then(v.tensor_tensor(ge[:, :, :], ge[:, :, :], jump[:, :].unsqueeze(1).to_broadcast([P, NTL, E]), ALU.mult))
            then(v.tensor_reduce(tf[:, 0, :], ge[:, :, :], AX.X, ALU.add))
            then(v.tensor_tensor(tf[:, 0, :], tf[:, 0, :], tid[:, :], ALU.add))
            v.tensor_scalar(table[:, 0, :], tf[:, 0, :], float(E * CAP // P), None, ALU.min)
            v.tensor_scalar(table[:, 1, :], tf[:, 1, :], float(E - 1), None, ALU.min)


def experts(nc, b2, b1T, w1, w2, unscale, ident, xs, acc, table):
    with Scope(nc, "ex") as s:
        row = [s.sb(f"row{j}", [P, ROW]) for j in range(2)]
        meta = [s.sb(f"meta{j}", [P, 2]) for j in range(2)]
        mt = [s.sb(f"mt{j}", [P, 2]) for j in range(2)]
        xT = s.sb("xT", [P, DT, P])
        xT_hi, xT_lo = ([s.sb(f"xT_{n}{j}", [P, DT, P], F16) for j in range(2)] for n in ("hi", "lo"))
        h = [s.sb(f"h{j}", [P, HID]) for j in range(2)]
        hT = s.sb("hT", [P, HT, P])
        hT_hi, hT_lo = ([s.sb(f"hT_{n}{j}", [P, HT, P], F16) for j in range(2)] for n in ("hi", "lo"))
        yb = [s.sb(f"yb{j}", [P, D]) for j in range(2)]
        yo = [s.sb(f"yo{j}", [P, D]) for j in range(2)]
        b2s = s.sb("b2s", [P, E, D])
        ps_t = s.ps("ps_t", [P, CH])
        ps_h = [s.ps(f"ps_h{j}", [P, HID]) for j in range(2)]
        ps_u = s.ps("ps_u", [P, HT, P])
        ps_y = s.ps("ps_y", [P, CH])
        b2_in, t_r, xf_r, xhi_r, xlo_r, h_mm, h_r, u_r, hf_r, hhi_r, hlo_r, y_mm, meta_r, mt_r, yb_r, yo_r, added = (
            s.sem(n) for n in ("b2_in", "t_r", "xf_r", "xhi_r", "xlo_r", "h_mm", "h_r", "u_r", "hf_r", "hhi_r", "hlo_r",
                               "y_mm", "meta_r", "mt_r", "yb_r", "yo_r", "added"))
        row_in = [s.sem(f"row_in{j}") for j in range(2)]
        begun, turned = s.sem("begun"), s.sem("turned")
        block = s.block()

        def look_up(eng, what, i, top):
            return eng.value_load(table[0:1, what, bass.ds(i, 1)], min_val=0, max_val=top)

        def flat(ps):
            return ps[:, 0:D].rearrange("p (d n) -> p d n", d=DT)

        @block.sync
        def _(sp):
            def load(i, j, first):
                r = look_up(nc.sync, 0, i, E * CAP // P)
                if not first:
                    sp.wait_ge(t_r, i - 1)
                    sp.wait_ge(meta_r, i - 1)
                sp.dma_start(row[j][:, :], xs[bass.ds(r * P, P), :]).then_inc(row_in[j], 16)

            load(0, 0, True)
            load(1, 1, True)
            sp.dma_start(b2s[:, :, :], b2.unsqueeze(0).to_broadcast([P, E, D])).then_inc(b2_in, 16)
            with nc.sync.Fori(1, NTL // 2, 1) as m:
                for j in range(2):
                    load(2 * m + j, j, False)

        @block.tensor
        def _(pe):
            def turn_x(i, j):
                pe.wait_ge(row_in[j], 16 * (i // 2 + 1))
                need(pe, xf_r, i)
                need(pe, xhi_r, i)
                for d in range(DT):
                    last = nc.tensor.transpose(ps_t[:, d * P:(d + 1) * P], row[j][:, d * P:(d + 1) * P], ident[:, :])
                last.then_inc(t_r, 1)

            def up(i, j):
                e = look_up(nc.tensor, 1, i, E - 1)
                need(pe, xhi_r, i + 1)
                need(pe, xlo_r, i + 1)
                need(pe, h_r, i - 1)
                whi, wlo = (x[:, :, :].rearrange("p e n -> p (e n)") for x in w1)
                parts = [(xT_hi[j], whi), (xT_hi[j], wlo), (xT_lo[j], whi)]
                for c in range(2):
                    for n, (d, (a, b)) in enumerate((d, p) for d in range(DT) for p in parts):
                        last = nc.tensor.matmul(ps_h[j][:, c * CH:(c + 1) * CH], a[:, d, :],
                                                b[:, bass.ds(e * WN + d * HID + c * CH, CH)],
                                                start=(n == 0), stop=(n == 3 * DT - 1))
                last.then_inc(h_mm, 1)

            def turn_h(i, j):
                need(pe, h_r, i + 1)
                for g in range(2):
                    need(pe, hf_r, 2 * (i - 1) + g + 1)
                    for n in range(4 * g, 4 * g + 4):
                        last = nc.tensor.transpose(ps_u[:, n, :], h[j][:, n * P:(n + 1) * P], ident[:, :])
                    last.then_inc(u_r, 1)

            def down(i, j):
                e = look_up(nc.tensor, 1, i, E - 1)
                need(pe, hhi_r, i + 1)
                need(pe, hlo_r, i + 1)
                need(pe, yb_r, i)
                whi, wlo = (x[:, :, :].rearrange("p e n -> p (e n)") for x in w2)
                for n in range(HT):
                    for m, (a, b) in enumerate(((hT_hi[j], whi), (hT_hi[j], wlo), (hT_lo[j], whi))):
                        last = nc.tensor.matmul(ps_y[:, 0:D], a[:, n, :], b[:, bass.ds(e * WN + n * D, D)],
                                                start=(n == 0 and m == 0), stop=(n == HT - 1 and m == 2))
                last.then_inc(y_mm, 1)

            def step(k, j):
                if there(k + 1, NTL):
                    up(k + 1, 1 - j)
                if there(k + 2, NTL):
                    turn_x(k + 2, j)
                if there(k, NTL):
                    turn_h(k, j)
                if there(k - 1, NTL):
                    down(k - 1, 1 - j)

            in_steps(nc.tensor, NTL, 2, 1, step)

        @block.scalar
        def _(act):
            def split_x(i, j):
                act.wait_ge(t_r, i + 1)
                need(act, xlo_r, i)
                nc.scalar.mul(xT[:, :, :], flat(ps_t), XN_SCALE).then_inc(xf_r, 1)
                need(act, h_mm, i - 1)
                nc.scalar.mul(xT_hi[j][:, :, :], flat(ps_t), XN_SCALE).then_inc(xhi_r, 1)

            def relu(i, j):
                e = look_up(nc.scalar, 1, i, E - 1)
                need(act, hlo_r, i)
                for g in range(2):
                    act.wait_ge(u_r, 2 * i + g + 1)
                    act.sem_inc(turned, 1)
                    for n in range(4 * g, 4 * g + 4):
                        last = nc.scalar.activation(hT[:, n, :], ps_u[:, n, :], ACT.Relu,
                                                    bias=b1T[:, bass.ds(e * HT + n, 1)])
                    last.then_inc(hf_r, 1)

            def step(k, j):
                if there(k + 2, NTL):
                    split_x(k + 2, j)
                if there(k, NTL):
                    relu(k, j)

            in_steps(nc.scalar, NTL, 2, 0, step)

        @block.vector
        def _(dve):
            def take_h(i, j):
                e = look_up(nc.vector, 1, i, E - 1)
                dve.wait_ge(h_mm, i + 1)
                need(dve, u_r, 2 * (i - 1))
                nc.vector.tensor_scalar(h[j][:, :], ps_h[j][:, :], unscale[:, 0, bass.ds(e, 1)], None,
                                        ALU.mult).then_inc(h_r, 1)

            def take_meta(i, j):
                dve.wait_ge(row_in[j], 16 * (i // 2 + 1))
                need(dve, mt_r, i - 1)
                nc.vector.tensor_copy(meta[j][:, :], row[j][:, D:ROW]).then_inc(meta_r, 1)

            def keep_meta(i, j):
                need(dve, added, 16 * (i - 1))
                dve.wait_ge(meta_r, i + 1)
                nc.vector.tensor_copy(mt[j][:, :], meta[j][:, :]).then_inc(mt_r, 1)

            def rest_x(i, j):
                dve.wait_ge(xf_r, i + 1)
                dve.wait_ge(xhi_r, i + 1)
                need(dve, h_mm, i - 1)
                nc.vector.tensor_tensor(xT_lo[j][:, :, :], xT[:, :, :], xT_hi[j][:, :, :], ALU.subtract).then_inc(xlo_r, 1)

            def split_h(i, j):
                dve.wait_ge(hf_r, 2 * i + 2)
                need(dve, y_mm, i - 1)
                nc.vector.tensor_copy(hT_hi[j][:, :, :], hT[:, :, :]).then_inc(hhi_r, 1)
                dve.wait_ge(hhi_r, i + 1)
                nc.vector.tensor_tensor(hT_lo[j][:, :, :], hT[:, :, :], hT_hi[j][:, :, :], ALU.subtract).then_inc(hlo_r, 1)

            def weigh(i, j):
                e = look_up(nc.vector, 1, i, E - 1)
                if isinstance(i, int) and i == 0:
                    dve.wait_ge(b2_in, 16)
                dve.wait_ge(y_mm, i + 1)
                nc.vector.scalar_tensor_tensor(out=yb[j][:, :], in0=ps_y[:, 0:D], scalar=unscale[:, 1, bass.ds(e, 1)],
                                               in1=b2s[:, bass.ds(e, 1), :].rearrange("p a d -> p (a d)"),
                                               op0=ALU.mult, op1=ALU.add).then_inc(yb_r, 1)
                dve.wait_ge(yb_r, i + 1)
                dve.wait_ge(mt_r, i + 1)
                nc.vector.tensor_scalar(yo[j][:, :], yb[j][:, :], mt[j][:, 0:1], None, ALU.mult).then_inc(yo_r, 1)

            def step(k, j):
                if there(k - 2, NTL):
                    weigh(k - 2, j)
                if there(k - 1, NTL):
                    keep_meta(k - 1, 1 - j)
                if there(k + 1, NTL):
                    take_h(k + 1, 1 - j)
                    take_meta(k + 1, 1 - j)
                if there(k + 2, NTL):
                    rest_x(k + 2, j)
                if there(k, NTL):
                    split_h(k, j)

            in_steps(nc.vector, NTL, 2, 2, step)

        @block.gpsimd
        def _(pool):
            last_row = nc.gpsimd.to_reg(T + P - 1)

            def add(i, j, first):
                pool.wait_ge(yo_r, i + 1)
                if not first:
                    pool.wait_ge(added, 16 * i)
                pool.sem_inc(begun, 1)
                nc.gpsimd.indirect_dma_start(out=acc[:, :],
                                             out_offset=bass.IndirectOffsetOnAxis(ap=mt[j][:, 1:2].bitcast(U32), axis=0),
                                             in_=yo[j][:, :], in_offset=None, bounds_check=last_row, oob_is_err=True,
                                             compute_op=ALU.add).then_inc(added, 16)

            add(0, 0, True)
            add(1, 1, False)
            with nc.gpsimd.Fori(1, NTL // 2, 1) as m:
                for j in range(2):
                    add(2 * m + j, j, False)
            pool.wait_ge(added, 16 * NTL)


def store_acc(nc, acc, out):
    with Scope(nc, "sa") as s:
        stored = s.sem("stored")
        ov = out.rearrange("b s d -> (b s) d")
        block = s.block()

        @block.sync
        def _(sp):
            for g in range(4):
                sp.dma_start(ov[g * T // 4:(g + 1) * T // 4, :], acc[g * T // 4:(g + 1) * T // 4, :]).then_inc(stored, 16)
            sp.wait_ge(stored, 16 * 4)


def program(nc, w, out):
    Scope.taken.clear()
    with Scope(nc, "main") as s:
        x_res = s.sb("x_res", [P, NT, D])
        mv, rstd = s.sb("mv", [P, NT, 2]), s.sb("rstd", [P, NT])
        stats = s.sb("stats", [P, NT, 6])
        ident = s.sb("ident", [P, P])
        ctxT = s.sb("ctxT", [P, 2, B * KV])
        ssq = s.sb("ssq", [P, 4 * E])
        x_in = [s.sem(f"x_in{g}") for g in range(8)]
        load(nc, w["ctx_768"], ident, ctxT)
        l0 = {"q": w["L0_xattn_w_q"], "k": w["L0_xattn_w_kv"][:, 0:INNER], "v": w["L0_xattn_w_kv"][:, INNER:2 * INNER],
              "o": w["L0_xattn_w_out"]}
        l1 = {k: w["L1_xattn_" + n] for k, n in (
            ("q", "Wq"), ("k", "Wk"), ("v", "Wv"), ("o", "Wo"), ("k_ipa", "Wk_ipa"), ("v_ipa", "Wv_ipa"),
            *((n, n) for n in ("q_down", "q_up", "q_alpha", "k_down", "k_up", "k_alpha",
                               "v_down", "v_up", "v_alpha", "o_down", "o_up", "o_alpha")))}

        def cross(layer, weights, groups, bias):
            with Scope(nc, f"c{layer}") as z:
                M = [z.sb(f"M{i}", [P, DT, B, INNER], F16) for i in range(2)]
                VW = [z.sb(f"VW{i}", [P, B, NP, D], F16) for i in range(2)]
                unscale = z.sb("unscale", [P, 2])
                if layer == 0:
                    prepare_attention(nc, "pa0", weights, ctxT, ident, M, VW, unscale, w["x"], x_res, stats, x_in)
                else:
                    prepare_attention(nc, "pa1", weights, ctxT, ident, M, VW, unscale)
                rstd_of(nc, f"r{layer}", stats, mv, rstd)
                attention(nc, f"at{layer}", groups, bias, x_res, mv, rstd, stats, ident, M, VW, unscale,
                          (w["L1_ffn_W1"], w["L1_ffn_W2"]) if layer else None, ssq)

        cross(0, l0, [(0, KV)], w["L0_xattn_b_out"])
        clear_semaphores(nc, Scope.taken)
        with Scope(nc, "f") as z:
            WgT, WuT = z.sb("WgT", [P, DT, FF]), z.sb("WuT", [P, DT, FF])
            WdT = z.sb("WdT", [P, FT, D])
            xqT = z.sb("xqT", [P, DT, T])
            scale_x = z.sb("scale_x", [P, 1])
            quantise_weights(nc, w["L0_ffn_w_gate"], w["L0_ffn_w_up"], w["L0_ffn_w_down"], WgT, WuT, WdT, ident)
            rstd_of(nc, "r2", stats, mv, rstd)
            quantise_input(nc, x_res, mv, rstd, scale_x, xqT, ident)
            gate = z.sb("gate", [P, NC * FT * CH])
            up_dram = nc.dram_tensor("up_scratch", (2 * NC, P, FT // 2 * CH), F32, kind="Internal").ap()
            gated_mlp(nc, x_res, stats, scale_x, xqT, WgT, WuT, WdT, up_dram, gate)
        clear_semaphores(nc, Scope.taken)
        cross(1, l1, [(0, KV - IPA), (KV - IPA, KV)], w["L1_xattn_bo"])
        with Scope(nc, "e") as z:
            w1 = [z.sb(f"w1_{n}", [P, E, WN], F16) for n in ("hi", "lo")]
            w2 = [z.sb(f"w2_{n}", [P, E, WN], F16) for n in ("hi", "lo")]
            b1T = z.sb("b1T", [P, E * HT])
            unscale = z.sb("unscale", [P, 2, E])
            table = z.sb("table", [P, 2, NTL], I32)
            xs = nc.dram_tensor("xs", (E * CAP + P, ROW), F32, kind="Internal").ap()
            acc = nc.dram_tensor("acc", (T + P, D), F32, kind="Internal").ap()
            rstd_of(nc, "r4", stats, mv, rstd)
            route(nc, w, b1T, x_res, mv, rstd, ident, w1, w2, ssq, unscale, xs, acc, table)
            experts(nc, w["L1_ffn_b2"], b1T, w1, w2, unscale, ident, xs, acc, table)
            store_acc(nc, acc, out)


def kernel(**inputs):
    import numpy as np
    import concourse.bacc as bacc
    from concourse.bass_utils import run_bass_kernel_spmd

    nc = bacc.Bacc("TRN2", target_bir_lowering=False, num_devices=1)
    arrays, aps = {}, {}
    for name, a in inputs.items():
        a = np.ascontiguousarray(a)
        arrays[f"in_{name}"] = a
        aps[name] = nc.dram_tensor(f"in_{name}", a.shape, mybir.dt.from_np(a.dtype), kind="ExternalInput").ap()
    out = nc.dram_tensor("out_0", (B, S, D), F32, kind="ExternalOutput").ap()
    program(nc, aps, out)
    r = run_bass_kernel_spmd(nc, [arrays], core_ids=[0])
    return r.results[0]["out_0"]
```
